# Optimizing a Trainium2 kernel written in Bass

```python
import numpy as np
import jax
import jax.numpy as jnp

def _softmax(x, axis=-1):
    return jax.nn.softmax(x, axis=axis)

def _gelu(x):
    return jax.nn.gelu(x, approximate=True)

def _silu(x):
    return jax.nn.silu(x)

def _sigmoid(x):
    return jax.nn.sigmoid(x)

def _layernorm(x, axis=-1, eps=1e-05):
    m = jnp.mean(x, axis=axis, keepdims=True)
    v = jnp.var(x, axis=axis, keepdims=True)
    return (x - m) / jnp.sqrt(v + eps)

def _scatter_add(tgt, idx, src, axis=0):
    return tgt.at[idx].add(src)

def _segment_sum(src, seg, n):
    return jax.ops.segment_sum(src, seg, n)
kernel_name = 'mk_gnn_resnorm_d4_gnn_r8_7f6431'

def setup_inputs(seed: int=0):
    np.random.seed(seed)
    _w = jnp.asarray

    def _rec_inputs():
        import jax
        import jax.numpy as jnp
        _gk = jax.random.key(seed)
        x = -0.000202 + 1 * jax.random.normal(jax.random.fold_in(_gk, 1), (12500, 64), jnp.float32)
        src = jax.random.randint(jax.random.fold_in(_gk, 2), (400000,), 0, 12500, jnp.int32)
        dst = jnp.minimum((12500 * jax.random.uniform(jax.random.fold_in(_gk, 3), (400000,)) ** 2.0).astype(jnp.int32), 99999)
        _o = jnp.argsort(dst, stable=True)
        src = src[_o]
        dst = dst[_o]
        edge_attr_64 = -6.74381e-05 + 0.999835 * jax.random.normal(jax.random.fold_in(_gk, 12), (400000, 64), jnp.float32)
        edge_type_8 = jax.random.randint(jax.random.fold_in(_gk, 14), (400000,), 0, 8, jnp.int32)
        edge_weight = jax.random.uniform(jax.random.fold_in(_gk, 15), (400000,), jnp.float32, 0.0, 1)
        return (x, src, dst, edge_attr_64, edge_type_8, edge_weight)
    x, src, dst, edge_attr_64, edge_type_8, edge_weight = _rec_inputs()

    def _L0_gnn_setup():
        import jax, jax.numpy as jnp
        import numpy as np
        N_NODES = 12500
        N_EDGES = 156250
        D = 64
        H = 128
        key = jax.random.key(seed)
        ks = jax.random.split(key, 8)
        s = 1.0 / np.sqrt(D)
        return {'nodes': jax.random.normal(ks[0], (N_NODES, D), jnp.float32), 'edges': jax.random.normal(ks[1], (N_EDGES, D), jnp.float32), 'senders': jax.random.randint(ks[2], (N_EDGES,), 0, N_NODES, jnp.int32), 'receivers': jax.random.randint(ks[3], (N_EDGES,), 0, N_NODES, jnp.int32), 'We_w': jax.random.normal(ks[4], (D, D), jnp.float32) * s, 'We_b': jnp.zeros((D,), jnp.float32), 'eps': jnp.zeros((1, 1), jnp.float32), 'W1': jax.random.normal(ks[5], (D, H), jnp.float32) * s, 'b1': jnp.zeros((H,), jnp.float32), 'W2': jax.random.normal(ks[6], (H, D), jnp.float32) * (1.0 / np.sqrt(H)), 'b2': jnp.zeros((D,), jnp.float32)}
    _L0_gnn_all = _L0_gnn_setup()
    _L0_gnn_in = {k: v for k, v in _L0_gnn_all.items() if k in ('We_w', 'We_b', 'eps', 'W1', 'b1', 'W2', 'b2')}
    del _L0_gnn_all

    def _L1_gnn_setup():
        import jax, jax.numpy as jnp
        import numpy as np
        N_NODES = 6250
        N_EDGES = 100000
        F_DIM = 64
        AVG_D_LOG = 2.833
        EPS_STD = 1e-05
        EPS_BN = 1e-05
        key = jax.random.key(seed)
        k = jax.random.split(key, 5)
        h = jax.random.normal(k[0], (N_NODES, F_DIM), dtype=jnp.float32)
        src = jax.random.randint(k[1], (N_EDGES,), 0, N_NODES)
        dst = jax.random.randint(k[2], (N_EDGES,), 0, N_NODES)
        W = jax.random.normal(k[3], (12 * F_DIM, F_DIM), dtype=jnp.float32) * 0.02
        b = jnp.zeros((F_DIM,), dtype=jnp.float32)
        gamma = jnp.ones((F_DIM,), dtype=jnp.float32)
        beta = jnp.zeros((F_DIM,), dtype=jnp.float32)
        return {'h': h, 'src': src, 'dst': dst, 'W': W, 'b': b, 'gamma': gamma, 'beta': beta}
    _L1_gnn_all = _L1_gnn_setup()
    _L1_gnn_in = {k: v for k, v in _L1_gnn_all.items() if k in ('W', 'b', 'gamma', 'beta')}
    del _L1_gnn_all

    def _L2_gnn_setup():
        import jax, jax.numpy as jnp
        import numpy as np
        N_NODES = 12500
        N_EDGES = 150000
        DIM_IN = 64
        DIM_OUT = 64
        key = jax.random.key(seed)
        k_x, k_e, k_wl, k_wr = jax.random.split(key, 4)
        x = jax.random.normal(k_x, (N_NODES, DIM_IN), dtype=jnp.float32)
        edge_index = jax.random.randint(k_e, (2, N_EDGES), 0, N_NODES, dtype=jnp.int64)
        scale = 1.0 / np.sqrt(DIM_IN)
        w_l = jax.random.uniform(k_wl, (DIM_OUT, DIM_IN), dtype=jnp.float32, minval=-scale, maxval=scale)
        w_r = jax.random.uniform(k_wr, (DIM_OUT, DIM_IN), dtype=jnp.float32, minval=-scale, maxval=scale)
        b = jnp.zeros((DIM_OUT,), dtype=jnp.float32)
        return {'x': x, 'edge_index': edge_index, 'w_l': w_l, 'w_r': w_r, 'b': b}
    _L2_gnn_all = _L2_gnn_setup()
    _L2_gnn_in = {k: v for k, v in _L2_gnn_all.items() if k in ('w_l', 'w_r', 'b')}
    del _L2_gnn_all

    def _L3_gnn_setup():
        import jax, jax.numpy as jnp
        import numpy as np
        N_NODES = 12500
        N_EDGES = 400000
        N_RELS = 8
        F_IN = 64
        F_OUT = 64
        key = jax.random.key(seed)
        k1, k2, k3, k4, k5, k6 = jax.random.split(key, 6)
        X = jax.random.normal(k1, (N_NODES, F_IN), dtype=jnp.float32)
        W = jax.random.normal(k2, (N_RELS, F_IN, F_OUT), dtype=jnp.float32) * 0.1
        A = jax.random.uniform(k3, (N_EDGES,), dtype=jnp.float32)
        src = jax.random.randint(k4, (N_EDGES,), 0, N_NODES, dtype=jnp.int32)
        dst = jax.random.randint(k5, (N_EDGES,), 0, N_NODES, dtype=jnp.int32)
        etype = jax.random.randint(k6, (N_EDGES,), 0, N_RELS, dtype=jnp.int32)
        return {'X': X, 'W': W, 'A': A, 'src': src, 'dst': dst, 'etype': etype}
    _L3_gnn_all = _L3_gnn_setup()
    _L3_gnn_in = {k: v for k, v in _L3_gnn_all.items() if k in ('W',)}
    del _L3_gnn_all
    return {'x': x, 'src': src, 'dst': dst, 'edge_attr_64': edge_attr_64, 'edge_type_8': edge_type_8, 'edge_weight': edge_weight, 'L0_gnn_We_w': _L0_gnn_in['We_w'], 'L0_gnn_We_b': _L0_gnn_in['We_b'], 'L0_gnn_eps': _L0_gnn_in['eps'], 'L0_gnn_W1': _L0_gnn_in['W1'], 'L0_gnn_b1': _L0_gnn_in['b1'], 'L0_gnn_W2': _L0_gnn_in['W2'], 'L0_gnn_b2': _L0_gnn_in['b2'], 'L1_gnn_W': _L1_gnn_in['W'], 'L1_gnn_b': _L1_gnn_in['b'], 'L1_gnn_gamma': _L1_gnn_in['gamma'], 'L1_gnn_beta': _L1_gnn_in['beta'], 'L2_gnn_w_l': _L2_gnn_in['w_l'], 'L2_gnn_w_r': _L2_gnn_in['w_r'], 'L2_gnn_b': _L2_gnn_in['b'], 'L3_gnn_W': _L3_gnn_in['W']}

def reference(x, src, dst, edge_attr_64, edge_type_8, edge_weight, L0_gnn_We_w, L0_gnn_We_b, L0_gnn_eps, L0_gnn_W1, L0_gnn_b1, L0_gnn_W2, L0_gnn_b2, L1_gnn_W, L1_gnn_b, L1_gnn_gamma, L1_gnn_beta, L2_gnn_w_l, L2_gnn_w_r, L2_gnn_b, L3_gnn_W):
    import jax
    import jax.numpy as jnp

    def _L0_gnn_ref(nodes, edges, senders, receivers, We_w, We_b, eps, W1, b1, W2, b2):
        import jax, jax.numpy as jnp
        import numpy as np
        N_NODES = 12500
        N_EDGES = 156250
        D = 64
        H = 128
        msg = nodes[senders] + (edges @ We_w + We_b)
        agg = jax.ops.segment_sum(msg, receivers, num_segments=N_NODES)
        h = (1.0 + eps) * nodes + agg
        h = jax.nn.relu(h @ W1 + b1)
        out = h @ W2 + b2
        return out

    def _L1_gnn_ref(h, src, dst, W, b, gamma, beta):
        import jax, jax.numpy as jnp
        import numpy as np
        N_NODES = 6250
        N_EDGES = 100000
        F_DIM = 64
        AVG_D_LOG = 2.833
        EPS_STD = 1e-05
        EPS_BN = 1e-05
        N = h.shape[0]
        m = h[src]
        ones = jnp.ones((src.shape[0],), dtype=h.dtype)
        deg = jax.ops.segment_sum(ones, dst, num_segments=N)
        s = jax.ops.segment_sum(m, dst, num_segments=N)
        s2 = jax.ops.segment_sum(m * m, dst, num_segments=N)
        mx = jax.ops.segment_max(m, dst, num_segments=N)
        mn = jax.ops.segment_min(m, dst, num_segments=N)
        degc = jnp.maximum(deg, 1.0)[:, None]
        mean = s / degc
        var = jax.nn.relu(s2 / degc - mean * mean)
        std = jnp.sqrt(var + EPS_STD)
        agg = jnp.concatenate([mean, mx, mn, std], axis=1)
        has = (deg > 0)[:, None]
        agg = jnp.where(has, agg, 0.0)
        logD = jnp.log(deg + 1.0)[:, None]
        amp = agg * (logD / AVG_D_LOG)
        att = agg * jnp.where(has, AVG_D_LOG / jnp.maximum(logD, 1e-12), 0.0)
        x = jnp.concatenate([agg, amp, att], axis=1)
        x = x @ W + b
        mu = jnp.mean(x, axis=0)
        v = jnp.var(x, axis=0)
        x = gamma * (x - mu) / jnp.sqrt(v + EPS_BN) + beta
        x = jax.nn.relu(x)
        x = h + x
        return x

    def _L2_gnn_ref(x, edge_index, w_l, w_r, b):
        import jax, jax.numpy as jnp
        import numpy as np
        N_NODES = 12500
        N_EDGES = 150000
        DIM_IN = 64
        DIM_OUT = 64
        src = edge_index[0]
        dst = edge_index[1]
        n = x.shape[0]
        msgs = x[src]
        summed = jax.ops.segment_sum(msgs, dst, num_segments=n)
        deg = jax.ops.segment_sum(jnp.ones((msgs.shape[0],), dtype=x.dtype), dst, num_segments=n)
        mean_aggr = summed / jnp.maximum(deg, 1.0)[:, None]
        out = mean_aggr @ w_l.T + x @ w_r.T + b
        return out

    def _L3_gnn_ref(X, W, A, src, dst, etype):
        import jax, jax.numpy as jnp
        import numpy as np
        N_NODES = 12500
        N_EDGES = 400000
        N_RELS = 8
        F_IN = 64
        F_OUT = 64
        XW = jnp.einsum('nf,rfo->rno', X, W)
        msg = XW[etype, src] * A[:, None]
        Y = jax.ops.segment_sum(msg, dst, num_segments=X.shape[0])
        return Y
    edge_index = jnp.stack([src, dst])
    x = _layernorm(x + _L0_gnn_ref(x, edge_attr_64, src, dst, L0_gnn_We_w, L0_gnn_We_b, L0_gnn_eps, L0_gnn_W1, L0_gnn_b1, L0_gnn_W2, L0_gnn_b2), axis=-1)
    x = _layernorm(x + _L1_gnn_ref(x, src, dst, L1_gnn_W, L1_gnn_b, L1_gnn_gamma, L1_gnn_beta), axis=-1)
    x = _layernorm(x + _L2_gnn_ref(x, edge_index, L2_gnn_w_l, L2_gnn_w_r, L2_gnn_b), axis=-1)
    x = _layernorm(x + _L3_gnn_ref(x, L3_gnn_W, edge_weight, src, dst, edge_type_8), axis=-1)
    return x

_drawn_inputs = setup_inputs


def setup_inputs(seed=0):
    import zlib

    import numpy as np

    out = dict(_drawn_inputs(seed))
    spreads = {'L0_gnn_We_b': (0.0, 0.1),
     'L0_gnn_b1': (0.0, 0.514),
     'L0_gnn_b2': (0.0, 0.308),
     'L1_gnn_b': (0.0, 0.8),
     'L1_gnn_gamma': (1.0, 0.2),
     'L1_gnn_beta': (0.0, 0.1),
     'L2_gnn_b': (0.0, 0.1)}
    factors = {}
    for name, (base, spread) in spreads.items():
        noise = np.random.default_rng([zlib.crc32(name.encode()), seed]).standard_normal(out[name].shape)
        drawn = base * np.exp(spread * noise) if base else spread * noise
        out[name] = jnp.asarray(drawn.astype(out[name].dtype))
    for name, factor in factors.items():
        out[name] = (out[name] * factor).astype(out[name].dtype)
    return out
```

```python
import concourse.bass as bass
from concourse import mybir
from contextlib import ExitStack

F32 = mybir.dt.float32
I32 = mybir.dt.int32
BF16 = mybir.dt.bfloat16
ALU = mybir.AluOpType
ACT = mybir.ActivationFunctionType
AX = mybir.AxisListType

P = 128
E = 400000
N = 12500
D = 64
H = 128
RELS = 8
BLOCKS = E // P
SUB = 5
SLOTS = 5
SUBS = BLOCKS // SUB
TURNS = SUBS // SLOTS
EP = 125
EW = E // EP
EB = EW // P
NT = N // EP
NW = NT * D
GRP = 4
GROUPS = NT // GRP
GTURNS = GROUPS // SLOTS
RT = GROUPS * GRP
RANKS = RT * P
assert BLOCKS * P == E and TURNS * SLOTS * SUB == BLOCKS and EP * EW == E and EB * P == EW
assert GROUPS * GRP == NT and GTURNS * SLOTS == GROUPS and RANKS >= N + P

AVG_D_LOG = 2.833
EPS = 1e-5
RESTART = -1e30

F_SRC, F_REL, F_END, F_DST, F_XW, F_WGT, F_WIN = 0, 5, 10, 15, 20, 25, 32
FIELDS = 40

XS_COLS = 192
L0_ROWS = 66
DEG, DST = 64, 65


def pipeline(eng, turns, stages, parts=1):
    for q in range(SLOTS):
        for part in range(parts):
            for lag, fn in stages:
                if q >= lag:
                    fn(0, q - lag, part)
    with eng.Fori(1, turns) as turn:
        for q in range(SLOTS):
            for part in range(parts):
                for lag, fn in stages:
                    if q >= lag:
                        fn(turn, q - lag, part)
                    else:
                        fn(turn - 1, q - lag + SLOTS, part)
    for q in range(max(lag for lag, _ in stages)):
        for part in range(parts):
            for lag, fn in stages:
                if q < lag:
                    fn(turns - 1, q - lag + SLOTS, part)


def first(turn):
    return isinstance(turn, int) and turn == 0


def gnn_kernel(nc, x_in, src_e, etype_e, weight_e, dst_n, edge_attr, eps_in, we, we_b, w1, b1, w2, b2,
               l1_w, l1_b, l1_gamma, l1_beta, wl_t, wr_t, l2_b, l3_w, out):
    with ExitStack() as ctx:
        def sb(name, shape, dt=F32):
            return ctx.enter_context(nc.sbuf_tensor(name, shape, dt))

        def psum(name, cols):
            return ctx.enter_context(nc.psum_tensor(name, [P, cols], F32))

        def sem(name):
            return ctx.enter_context(nc.semaphore(name))

        tables = [x_in] + [nc.dram_tensor(f"x{n}_table", [N, D], F32).ap() for n in (1, 2)]
        xw_table = nc.dram_tensor("xw_table", [N * RELS, D], F32).ap()
        agg = [nc.dram_tensor(f"agg{n}", [N, D], F32).ap() for n in range(4)]
        meta_d = nc.dram_tensor("meta_d", [P, SUBS * FIELDS], I32).ap()
        window_d = nc.dram_tensor("window_d", [BLOCKS], I32).ap()
        restart_d = nc.dram_tensor("restart_d", [E], BF16).ap()

        acc = sb("acc", [P, 2, RANKS])
        meta_all = acc[:, :, :].rearrange("p a r -> p (a r)")[:, 0:SUBS * FIELDS].bitcast(I32) \
            .rearrange("p (s f) -> p s f", f=FIELDS)
        xres = sb("xres", [EP, NT, D])
        WORK = 14400
        work = sb("work", [P, WORK])
        meta = sb("meta", [P, SLOTS, FIELDS], I32)
        restart = sb("restart", [P, SLOTS, SUB * P], BF16)

        def carve(at, *dims, parts=P):
            size = 1
            for d in dims:
                size *= d
            assert at + size <= WORK
            v = work[0:parts, at:at + size]
            if len(dims) > 1:
                names = " ".join(f"d{i}" for i in range(len(dims)))
                v = v.rearrange(f"p ({names}) -> p {names}", **{f"d{i}": d for i, d in enumerate(dims)})
            return v, at + size

        xs, at = carve(0, SLOTS, SUB, XS_COLS)
        onehot, at = carve(at, SLOTS, SUB, P)
        scanned, at = carve(at, SLOTS, SUB * P)
        turned, at = carve(at, SLOTS, SUB, P)
        rstage, at = carve(0, SLOTS, 2, GRP * P)
        moments, at = carve(at, SLOTS, GRP, P)
        meansq, at = carve(at, SLOTS, GRP, D)
        momt, at = carve(at, SLOTS, GRP * P)
        zbase, at = carve(at, SLOTS, GRP, D)
        rows, at = carve(at, SLOTS, GRP, L0_ROWS)
        ztmp, at = carve(at, GRP, D)
        n1, n2_at = carve(0, NT, D, parts=EP)
        n2, _ = carve(n2_at, NT, D, parts=EP)
        hstage, at = carve(n2_at, SLOTS, GRP, D, parts=EP)
        ht, at = carve(at, SLOTS, GRP * EP, parts=D)
        h1, at = carve(at, SLOTS, GRP * EP, parts=H)
        assert at <= n2_at + NW
        xw_stage, at = carve(0, SLOTS, GRP, RELS * D, parts=EP)
        xw_hstage, at = carve(at, SLOTS, GRP, D, parts=EP)
        xw_ht, at = carve(at, SLOTS, GRP * EP, parts=D)
        dst_i = work[0:EP, 0:EW].bitcast(I32)
        starts = work[0:EP, EW:2 * EW]
        inside = work[0:EP, 2 * EW:3 * EW]
        restart_row = work[0:EP, 2 * EW:2 * EW + EW // 2].bitcast(BF16)
        rel = work[0:EP, 3 * EW:4 * EW]
        xres_flat = xres[:, :, :].rearrange("p t f -> p (t f)")
        ends = xres_flat[:, 0:EW]
        dst_first = xres_flat[:, EW:2 * EW]
        src_all = work[:, 0:BLOCKS].bitcast(I32)
        etype_all = work[:, EW:EW + BLOCKS].bitcast(I32)
        weight_all = work[:, 2 * EW:2 * EW + BLOCKS]

        ident = sb("ident", [P, P])
        iota_i = sb("iota_i", [P, P], I32)
        iota = sb("iota", [P, P])
        ones = sb("ones", [P, P])
        before = sb("before", [P, P])
        zeros = sb("zeros", [EP, 640])
        dst_left = sb("dst_left", [EP, 1], I32)
        dst_right = sb("dst_right", [EP, 1], I32)
        blk_total = sb("blk_total", [EP, EB])
        blk_cum = sb("blk_cum", [EP, EB])
        blk_first = sb("blk_first", [EP, EB])
        blk_window = sb("blk_window", [EP, EB], I32)
        map_x = sb("map_x", [L0_ROWS, L0_ROWS])
        map_ea = sb("map_ea", [L0_ROWS, L0_ROWS])
        w1_sb = sb("w1_sb", [D, H])
        b1_sb = sb("b1_sb", [H, 1])
        w2_sb = sb("w2_sb", [H, D])
        w_moments = sb("w_moments", [P, 3, D])
        w_extremes = sb("w_extremes", [P, 3, D])
        wl_sb = sb("wl_sb", [D, D])
        wr_sb = sb("wr_sb", [D, D])
        w3_sb = sb("w3_sb", [D, RELS, D])
        bias = {n: sb(f"{n}_sb", [EP, D]) for n in ("b2", "l1_b", "l1_gamma", "l1_beta", "l2_b")}
        eps1 = sb("eps1", [EP, 1])
        eps_sb = sb("eps_sb", [P, 1])
        deg = sb("deg", [P, RT])
        inv_deg = sb("inv_deg", [P, RT])
        amp = sb("amp", [P, RT])
        att = sb("att", [P, RT])
        node_all = sb("node_all", [P, RT], I32)
        node_of = sb("node_of", [P, SLOTS, GRP], I32)
        no_rank = sb("no_rank", [P, GRP])
        ln_mean = sb("ln_mean", [EP, NT])
        ln_var = sb("ln_var", [EP, NT])
        bn_mean = sb("bn_mean", [EP, D])
        bn_scale = sb("bn_scale", [EP, D])

        BANK = 512
        ps_a = psum("ps_a", 2 * BANK)
        ps_b = psum("ps_b", 2 * BANK)
        ps_o = psum("ps_o", 4 * BANK)
        ps_c = ps_o[:, 3 * BANK:4 * BANK]
        O_BANKS = SUB - 1
        sums = [ps_o[:, (k % O_BANKS) * BANK + (k // O_BANKS) * 2 * P:][:, 0:2 * P].rearrange("p (a c) -> p a c", a=2)
                for k in range(SUB)]

        edge_init = sem("edge_init")
        ld_edges = sem("ld_edges")
        ld_dst = sem("ld_dst")
        ld_const = sem("ld_const")
        consts = sem("consts")
        maps_init = sem("maps_init")
        edges_copied = sem("edges_copied")
        fields_ready = sem("fields_ready")
        fields_turned = sem("fields_turned")
        fields_placed = sem("fields_placed")
        cum_ready = sem("cum_ready")
        base_ready = sem("base_ready")
        window_ready = sem("window_ready")
        window_stored = sem("window_stored")
        window_placed = sem("window_placed")
        restart_ready = sem("restart_ready")
        restart_stored = sem("restart_stored")
        meta_stored = sem("meta_stored")
        agg_zeroed = sem("agg_zeroed")
        maps_ready = sem("maps_ready")
        dve_step = sem("dve_step")
        x_loaded = sem("x_loaded")

        meta_loaded = [sem(f"meta_loaded{q}") for q in range(SLOTS)]
        aux_loaded = [sem(f"aux_loaded{q}") for q in range(SLOTS)]
        gathered = [sem(f"gathered{q}") for q in range(SLOTS)]
        scattered = [sem(f"scattered{q}") for q in range(SLOTS)]
        xw_stored = [sem(f"xw_stored{q}") for q in range(SLOTS)]

        pool_past = sem("pool_past")
        pe_past = sem("pe_past")
        acc_zero = sem("acc_zero")
        table_ready = sem("table_ready")
        agg_loaded = sem("agg_loaded")
        centered = sem("centered")
        squared = sem("squared")
        var = sem("var")
        std = sem("std")
        x_ready = sem("x_ready")

        class Layer:
            pass

        layers = []
        for n in range(4):
            L = Layer()
            L.n = n

            def ls(name, n=n):
                return sem(f"l{n}_{name}")

            L.prep = ls("prep")
            L.onehot = ls("onehot")
            L.summed = ls("summed")
            L.added = ls("added")
            L.staged = ls("staged")
            L.rows_mm = ls("rows_mm")
            L.rows_out = ls("rows_out")
            L.rows_set = ls("rows_set")
            L.hs = ls("hs")
            L.htp = ls("htp")
            L.hts = ls("hts")
            L.dense = ls("dense")
            L.dense_out = ls("dense_out")
            if n == 0:
                L.number = ls("number")
                L.u = ls("u")
                L.relu = ls("relu")
            if n == 1:
                L.tx = ls("tx")
                L.scan = ls("scan")
                L.tb = ls("tb")
                L.ts = ls("ts")
                L.t1 = ls("t1")
                L.scaled = ls("scaled")
                L.row_step = ls("row_step")
                L.logs = ls("logs")
                L.sq = ls("sq")
                L.var_r = ls("var_r")
                L.std_r = ls("std_r")
                L.t2 = ls("t2")
                L.momt = ls("momt")
                L.bn_in = ls("bn_in")
                L.bn_sum = ls("bn_sum")
                L.bn_cent = ls("bn_cent")
                L.bn_sq = ls("bn_sq")
                L.bn_var = ls("bn_var")
                L.bn_std = ls("bn_std")
                L.bn_affine = ls("bn_affine")
                L.bn_relu = ls("bn_relu")
            if n == 2:
                L.xw_hs = ls("xw_hs")
                L.xw_htp = ls("xw_htp")
                L.xw_hts = ls("xw_hts")
                L.xw_mm = ls("xw_mm")
                L.xw_out = ls("xw_out")
            layers.append(L)
        out_stored = sem("out_stored")
        CREDIT = SLOTS * SUB

        def block_no(turn, q, k):
            return turn * (SLOTS * SUB) + (q * SUB + k)

        def step_no(turn, q):
            return turn * SLOTS + q

        def loaded(L, turn, each=1):
            return turn * (each * 16) + (L.n * TURNS + 1) * each * 16

        def rows_landed(L, turns):
            return turns * (GRP * 16) + L.n * GTURNS * GRP * 16

        def wide(ap, width):
            return ap.unsqueeze(2).to_broadcast([ap.shape[0], ap.shape[1], width])

        def along(ap, tiles):
            return ap.unsqueeze(1).to_broadcast([ap.shape[0], tiles, ap.shape[1]])

        def tiles_of(array, turn, q):
            return array[:, bass.ds(step_no(turn, q) * GRP, GRP), :]

        def ranks_of(array, turn, q):
            return array[:, bass.ds(step_no(turn, q) * GRP, GRP)]

        block = ctx.enter_context(nc.Block())

        @block.sync
        def _(sp):
            sp.dma_start(src_all, src_e).then_inc(ld_edges, 16)
            sp.dma_start(etype_all, etype_e).then_inc(ld_edges, 16)
            sp.dma_start(weight_all, weight_e).then_inc(ld_edges, 16)
            sp.wait_ge(edges_copied, 1)
            sp.dma_start(dst_i, dst_n).then_inc(ld_dst, 16)
            sp.wait_ge(edge_init, 1)
            sp.dma_start(dst_left[1:EP, :], dst_n[0:EP - 1, EW - 1:EW], allow_slow_non_contiguous=True).then_inc(ld_dst, 16)
            sp.dma_start(dst_right[0:EP - 1, :], dst_n[1:EP, 0:1], allow_slow_non_contiguous=True).then_inc(ld_dst, 16)
            sp.wait_ge(maps_init, 1)
            for dst, source in (
                (map_x[DEG:DEG + 1, 0:D], we_b), (map_ea[0:D, 0:D], we), (w1_sb[:, :], w1),
                (b1_sb[:, :], b1), (w2_sb[:, :], w2), (wl_sb[:, :], wl_t), (wr_sb[:, :], wr_t),
                (w3_sb[:, :, :], l3_w.rearrange("r f o -> f r o")),
                (eps1[:, :], eps_in.to_broadcast([EP, 1])),
            ):
                sp.dma_start(dst, source, allow_slow_non_contiguous=True).then_inc(ld_const, 16)
            w_parts = l1_w.rearrange("(g s f) o -> s f g o", g=3, s=4)
            for dst, part in ((w_moments[0:D], 0), (w_extremes[D:P], 1), (w_extremes[0:D], 2), (w_moments[D:P], 3)):
                sp.dma_start(dst, w_parts[part]).then_inc(ld_const, 16)
            for name, source in (("b2", b2), ("l1_b", l1_b), ("l1_gamma", l1_gamma), ("l1_beta", l1_beta), ("l2_b", l2_b)):
                sp.dma_start(bias[name][:, :], source.to_broadcast([EP, D])).then_inc(ld_const, 16)

            sp.wait_ge(window_ready, 1)
            sp.dma_start(window_d.rearrange("(p b) -> p b", p=EP), blk_window[:, :]).then_inc(window_stored, 16)
            sp.wait_ge(restart_ready, 1)
            sp.dma_start(restart_d.rearrange("(p e) -> p e", p=EP), restart_row).then_inc(restart_stored, 16)
            sp.wait_ge(window_stored, 16)
            sp.dma_start(meta_all[0:1, :, F_WIN:F_WIN + SUB], window_d.rearrange("(a s k) -> a s k", a=1, k=SUB)) \
                .then_inc(window_placed, 16)
            sp.wait_ge(fields_placed, 3 * SUB)
            sp.wait_ge(window_placed, 16)
            sp.dma_start(meta_d, meta_all.rearrange("p s f -> p (s f)")).then_inc(meta_stored, 16)
            sp.dma_start(xres_flat, x_in.rearrange("(p t) f -> p (t f)", p=EP)).then_inc(x_loaded, 16)
            sp.wait_ge(consts, 6)
            for a in agg:
                sp.dma_start(a.rearrange("(p a t) f -> p a (t f)", p=EP, a=NW // 640),
                             zeros[:, :].unsqueeze(1).to_broadcast([EP, NW // 640, 640])).then_inc(agg_zeroed, 16)
            sp.wait_ge(meta_stored, 16)
            sp.wait_ge(restart_stored, 16)

            meta_v = meta_d.rearrange("p (s f) -> p s f", f=FIELDS)
            ea_v = edge_attr.rearrange("p (b f) -> p b f", f=D)

            for L in layers:
                def load_slot(turn, q, _, L=L):
                    sp.wait_ge(L.added, block_no(turn, q, SUB))
                    s = step_no(turn, q)
                    sp.dma_start(meta[:, q, :], meta_v[:, bass.ds(s, 1), :].rearrange("p s f -> p (s f)")) \
                        .then_inc(meta_loaded[q], 16)
                    if L.n == 0:
                        sp.dma_start(xs[:, q, :, L0_ROWS:L0_ROWS + D], ea_v[:, bass.ds(s * SUB, SUB), :]) \
                            .then_inc(aux_loaded[q], 16)
                    if L.n == 1:
                        sp.dma_start(restart[:, q, :], restart_d.unsqueeze(0)[:, bass.ds(s * (SUB * P), SUB * P)]
                                     .to_broadcast([P, SUB * P])).then_inc(aux_loaded[q], 16)

                if L.n == 0:
                    sp.wait_ge(L.prep, 1)
                pipeline(sp, TURNS, [(0, load_slot)])

                for q in range(SLOTS):
                    sp.wait_ge(scattered[q], rows_landed(L, GTURNS))
                sp.dma_start(n1, agg[L.n].rearrange("(p t) f -> p t f", p=EP)).then_inc(agg_loaded, 16)

                if L.n < 2:
                    sp.wait_ge(x_ready, L.n + 1)
                    sp.dma_start(tables[L.n + 1].rearrange("(p t) f -> p t f", p=EP), xres[:, :, :]) \
                        .then_inc(table_ready, 16)
                elif L.n == 2:
                    xw_v = xw_table.rearrange("(p t r) f -> p t (r f)", p=EP, r=RELS)

                    def store_xw(turn, q, _, L=L):
                        sp.wait_ge(L.xw_out, 1 + step_no(turn, q) + 1)
                        sp.dma_start(tiles_of(xw_v, turn, q), xw_stage[:, q, :, :]).then_inc(xw_stored[q], 16)

                    pipeline(sp, GTURNS, [(0, store_xw)])
                else:
                    sp.wait_ge(x_ready, L.n + 1)
                    sp.dma_start(out.rearrange("(p t) f -> p t f", p=EP), xres[:, :, :]).then_inc(out_stored, 16)
            sp.wait_ge(out_stored, 16)

        @block.gpsimd
        def _(pool):
            pool.memset(ones[:, :], 1.0).then_inc(consts, 1)
            pool.memset(zeros[:, :], 0.0).then_inc(consts, 1)
            pool.memset(ident[:, :], 0.0).then_inc(consts, 1)
            pool.iota(iota_i[:, :], pattern=[[1, P]], base=0, channel_multiplier=0).then_inc(consts, 1)
            pool.wait_ge(consts, 4)
            pool.affine_select(out=ident[:, :], in_=ident[:, :], compare_op=ALU.not_equal, fill=1.0, base=0,
                               pattern=[[-1, P]], channel_multiplier=1).then_inc(consts, 1)
            pool.affine_select(out=before[:, :], in_=ones[:, :], compare_op=ALU.is_gt, fill=0.0, base=0,
                               pattern=[[1, P]], channel_multiplier=-1).then_inc(consts, 1)

            for L in layers:
                if L.n == 0:
                    pool.wait_ge(meta_stored, 16)
                else:
                    pool.wait_ge(layers[L.n - 1].staged, GROUPS)
                    if L.n == 2:
                        pool.wait_ge(layers[1].rows_mm, SLOTS + GROUPS)
                for a in range(2):
                    z = pool.memset(acc[:, a, :], 0.0)
                z.then_inc(acc_zero, 1)

                if L.n == 3:
                    for xw_q in xw_stored:
                        pool.wait_ge(xw_q, GTURNS * 16)
                elif L.n > 0:
                    pool.wait_ge(table_ready, 16 * L.n)
                table = xw_table if L.n == 3 else tables[L.n]
                field = F_XW if L.n == 3 else F_SRC
                col = D if L.n == 1 else 0

                def gather(turn, q, k, L=L, table=table, field=field, col=col):
                    if k == 0:
                        pool.wait_ge(meta_loaded[q], loaded(L, turn))
                        pool.sem_inc(pool_past, 1)
                    pool.indirect_dma_start(
                        out=xs[:, q, k, col:col + D], out_offset=None, in_=table,
                        in_offset=bass.IndirectOffsetOnAxis(ap=meta[:, q, field + k:field + k + 1], axis=0),
                    ).then_inc(gathered[q], 16)

                pipeline(pool, TURNS, [(0, gather)], parts=SUB)

                def scatter(turn, q, t, L=L):
                    if t == 0:
                        pool.wait_ge(L.rows_set if L.n < 2 else L.rows_out, step_no(turn, q) + (1 if L.n < 2 else 2))
                        pool.sem_inc(pool_past, 1)
                    pool.indirect_dma_start(
                        out=agg[L.n], out_offset=bass.IndirectOffsetOnAxis(ap=node_of[:, q, t:t + 1], axis=0),
                        in_=rows[:, q, t, 0:D], in_offset=None, bounds_check=N - 1, oob_is_err=False,
                    ).then_inc(scattered[q], 16)

                if L.n == 0:
                    pool.wait_ge(agg_zeroed, 16 * len(agg))
                pipeline(pool, GTURNS, [(0, scatter)], parts=GRP)

        @block.scalar
        def _(act):
            act.wait_ge(maps_ready, 1)
            for n, field in enumerate((F_REL, F_END, F_DST)):
                for gd in range(EB // SUB):
                    turned_no = n * SUB + gd
                    act.wait_ge(fields_turned, turned_no + 1)
                    ps = (ps_a, ps_b, ps_o)[turned_no % 3][:, 0:SUB * P].rearrange("p (k c) -> p c k", k=SUB)
                    dst = meta_all.rearrange("p (c g) f -> p c g f", g=EB // SUB)[:, :, gd, field:field + SUB]
                    act.activation(dst.bitcast(F32), ps[:, 0:EP, :], ACT.Copy).then_inc(fields_placed, 1)

            for L in layers:
                if L.n == 0:
                    def prep(turn, q, _, L=L):
                        act.wait_ge(meta_loaded[q], loaded(L, turn))
                        act.wait_ge(L.summed, block_no(turn, q, SUB))
                        act.activation(xs[:, q, :, DST], meta[:, q, F_DST:F_DST + SUB].bitcast(F32), ACT.Copy) \
                            .then_inc(L.prep, 1)

                    act.wait_ge(L.prep, 1)
                    pipeline(act, TURNS, [(0, prep)])
                if L.n == 1:
                    def prep1(turn, q, k, L=L):
                        if k == 0:
                            act.wait_ge(gathered[q], loaded(L, turn, SUB))
                            act.activation(xs[:, q, :, 0:D], xs[:, q, :, D:2 * D], ACT.Copy, scale=-1.0)
                            act.activation(xs[:, q, :, 2 * D:3 * D], xs[:, q, :, D:2 * D], ACT.Square).then_inc(L.prep, 1)

                    def last_edges(turn, q, k, L=L):
                        if k == 0:
                            act.wait_ge(L.tb, SLOTS + step_no(turn, q) + 1)
                            act.wait_ge(L.summed, block_no(turn, q, SUB))
                        ins = act.activation(turned[:, q, k, :], ps_b[:, k * P:(k + 1) * P], ACT.Copy,
                                             scale=meta[:, q, F_END + k:F_END + k + 1].bitcast(F32))
                        if k == SUB - 1:
                            ins.then_inc(L.ts, 1)

                    act.sem_inc(L.ts, 1)
                    pipeline(act, TURNS, [(0, prep1), (1, last_edges)], parts=SUB)

                act.sem_inc(L.rows_out, 1)
                if L.n != 1:
                    def rows_out(turn, q, _, L=L):
                        act.wait_ge(L.rows_mm, SLOTS + step_no(turn, q) + 1)
                        if L.n == 0 and not first(turn):
                            act.wait_ge(scattered[q], rows_landed(L, turn))
                        if L.n == 2:
                            for t in range(GRP):
                                ins = act.activation(
                                    rows[:, q, t, 0:D], ps_a[:, t * P:t * P + D], ACT.Copy,
                                    scale=inv_deg[:, bass.ds(step_no(turn, q) * GRP + t, 1)])
                        else:
                            w = L0_ROWS if L.n == 0 else D
                            ins = act.activation(rows[:, q, :, 0:w], ps_a[:, 0:GRP * P].rearrange(
                                "p (t c) -> p t c", t=GRP)[:, :, 0:w], ACT.Copy)
                        ins.then_inc(L.rows_out, 1)

                    pipeline(act, GTURNS, [(0, rows_out)])
                else:
                    act.wait_ge(maps_ready, 2)
                    act.activation(amp[:, :], deg[:, :], ACT.Ln, bias=1.0).then_inc(L.logs, 1)
                    act.sem_inc(L.momt, 1)

                    def moments_act(turn, q, _, L=L):
                        step = step_no(turn, q)
                        act.wait_ge(L.scaled, 1 + step + 1)
                        act.activation(meansq[:, q, :, :], moments[:, q, :, 0:D], ACT.Square).then_inc(L.sq, 1)
                        act.wait_ge(L.var_r, step + 1)
                        act.activation(moments[:, q, :, D:P], moments[:, q, :, D:P], ACT.Sqrt, bias=eps_sb[:, 0:1]) \
                            .then_inc(L.std_r, 1)
                        act.wait_ge(L.t2, step + 1)
                        act.activation(momt[:, q, :], ps_a[:, 512:512 + GRP * P], ACT.Copy).then_inc(L.momt, 1)
                        act.wait_ge(L.rows_mm, SLOTS + step + 1)
                        act.activation(zbase[:, q, :, :], ps_b[:, :].rearrange("p (t c) -> p t c", t=GRP)[:, :, 0:D],
                                       ACT.Copy).then_inc(L.rows_out, 1)

                    pipeline(act, GTURNS, [(1, moments_act)])

                if L.n == 0 or L.n == 2:
                    act.sem_inc(L.hts, 1)

                    def hts(turn, q, _, L=L):
                        step = step_no(turn, q)
                        act.wait_ge(L.htp, SLOTS + step + 1)
                        act.wait_ge(L.u if L.n == 0 else L.dense, step + 1)
                        act.activation(ht[:, q, :], ps_a[0:D, 0:GRP * EP], ACT.Copy).then_inc(L.hts, 1)

                    def hidden(turn, q, _, L=L):
                        step = step_no(turn, q)
                        act.wait_ge(L.u, SLOTS + step + 1)
                        act.wait_ge(L.dense, step + 1)
                        act.activation(h1[:, q, :], ps_a[:, 512:512 + GRP * EP], ACT.Relu, bias=b1_sb[:, 0:1]) \
                            .then_inc(L.relu, 1)

                    if L.n == 0:
                        act.sem_inc(L.relu, 1)
                        act.wait_ge(ld_const, 18 * 16)
                        pipeline(act, GTURNS, [(1, hidden), (0, hts)])
                    else:
                        pipeline(act, GTURNS, [(0, hts)])
                if L.n == 1:
                    act.wait_ge(L.bn_cent, 1)
                    act.activation(n2, n1, ACT.Square).then_inc(L.bn_sq, 1)
                    act.wait_ge(L.bn_var, 1)
                    act.activation(bn_scale[:, :], bn_scale[:, :], ACT.Sqrt, bias=eps_sb[0:EP, 0:1]).then_inc(L.bn_std, 1)
                    act.wait_ge(L.bn_affine, 1)
                    act.activation(n1, n1, ACT.Relu).then_inc(L.bn_relu, 1)
                act.wait_ge(centered, L.n + 1)
                act.activation(n2, n1, ACT.Square).then_inc(squared, 1)
                act.wait_ge(var, L.n + 1)
                act.activation(ln_var[:, :], ln_var[:, :], ACT.Sqrt, bias=eps_sb[0:EP, 0:1], scale=1.0 / D) \
                    .then_inc(std, 1)
                if L.n == 2:
                    act.sem_inc(L.xw_hts, 1)
                    act.sem_inc(L.xw_out, 1)

                    def xw_hts(turn, q, _, L=L):
                        step = step_no(turn, q)
                        act.wait_ge(L.xw_htp, SLOTS + step + 1)
                        act.wait_ge(L.xw_mm, step + 1)
                        act.activation(xw_ht[:, q, :], ps_a[0:D, 0:GRP * EP], ACT.Copy).then_inc(L.xw_hts, 1)

                    def xw_out(turn, q, t, L=L):
                        step = step_no(turn, q)
                        if t == 0:
                            if not first(turn):
                                act.wait_ge(xw_stored[q], turn * 16)
                        act.wait_ge(L.xw_mm, SLOTS + step + 1)
                        for t in range(GRP):
                            ps = (ps_b[:, 0:512], ps_b[:, 512:1024], ps_o[:, 0:512], ps_o[:, 512:1024])[t]
                            ins = act.activation(xw_stage[:, q, t, :], ps[0:EP, :], ACT.Copy)
                        ins.then_inc(L.xw_out, 1)

                    pipeline(act, GTURNS, [(0, xw_hts), (0, xw_out)])

        @block.tensor
        def _(pe):
            pe.wait_ge(consts, 6)
            pe.wait_ge(fields_ready, 1)
            for n, field in enumerate((rel, ends, dst_first)):
                for gd in range(EB // SUB):
                    turned_no = n * SUB + gd
                    if turned_no >= 3:
                        pe.wait_ge(fields_placed, turned_no - 2)
                    ps = (ps_a, ps_b, ps_o)[turned_no % 3]
                    for k in range(SUB):
                        g = gd * SUB + k
                        ins = pe.transpose(ps[:, k * P:k * P + EP], field[:, g * P:(g + 1) * P], ident[0:EP, 0:EP])
                    ins.then_inc(fields_turned, 1)
            pe.wait_ge(cum_ready, 1)
            pe.matmul(ps_c[0:EP, 0:1], before[0:EP, 0:EP], blk_cum[:, EB - 1:EB], start=True, stop=True) \
                .then_inc(base_ready, 1)

            for L in layers:
                pe.sem_inc(L.summed, CREDIT)
                if L.n == 1:
                    pe.sem_inc(L.tb, SLOTS)

                def sum_block(turn, q, k, L=L):
                    if k == 0:
                        pe.wait_ge(gathered[q], loaded(L, turn, SUB))
                        pe.wait_ge(L.onehot, step_no(turn, q) + 1)
                        if L.n == 0:
                            pe.wait_ge(aux_loaded[q], loaded(L, turn))
                            pe.wait_ge(L.prep, 1 + step_no(turn, q) + 1)
                        if L.n == 1:
                            pe.wait_ge(L.ts, 1 + step_no(turn, q) + 1)
                    behind = {0: 1, SUB - 1: O_BANKS}.get(k, SUB)
                    pe.wait_ge(L.added, CREDIT + block_no(turn, q, k) + 1 - behind)
                    s = onehot[:, q, k, :]
                    if L.n == 0:
                        pe.matmul(sums[k][0:L0_ROWS, 0, :], xs[:, q, k, 0:L0_ROWS], s, start=True, stop=True)
                        ins = pe.matmul(sums[k][0:L0_ROWS, 1, :], xs[:, q, k, L0_ROWS:2 * L0_ROWS], s, start=True, stop=True)
                    elif L.n == 1:
                        pe.matmul(sums[k][:, 0, :], xs[:, q, k, D:3 * D], s, start=True, stop=True)
                        ins = pe.matmul(sums[k][:, 1, :], turned[:, q, k, :], s, start=True, stop=True)
                    else:
                        ins = pe.matmul(sums[k][0:D, 0, :], xs[:, q, k, 0:D], s, start=True, stop=True)
                    ins.then_inc(L.summed, 1)

                if L.n != 1:
                    pipeline(pe, TURNS, [(0, sum_block)], parts=SUB)
                else:
                    def turn_rows(turn, q, k, L=L):
                        if k == 0:
                            pe.wait_ge(L.prep, step_no(turn, q) + 1)
                            pe.wait_ge(L.scan, step_no(turn, q) + 1)
                        ins = pe.transpose(ps_a[:, k * P:(k + 1) * P], xs[:, q, k, 0:P], ident[:, :])
                        if k == SUB - 1:
                            ins.then_inc(L.tx, 1)

                    def turn_back(turn, q, k, L=L):
                        if k == 0:
                            pe.wait_ge(L.scan, 1 + step_no(turn, q) + 1)
                            pe.wait_ge(L.ts, step_no(turn, q) + 1)
                        ins = pe.transpose(ps_b[:, k * P:(k + 1) * P], scanned[:, q, k * P:(k + 1) * P], ident[:, :])
                        if k == SUB - 1:
                            ins.then_inc(L.tb, 1)

                    pipeline(pe, TURNS, [(2, sum_block), (1, turn_back), (0, turn_rows)], parts=SUB)

                pe.sem_inc(L.rows_mm, SLOTS)
                if L.n != 1:
                    def rank_rows(turn, q, _, L=L):
                        step = step_no(turn, q)
                        if L.n == 0 and first(turn) and q == 0:
                            pe.wait_ge(ld_const, 18 * 16)
                        pe.wait_ge(L.staged, step + 1)
                        pe.wait_ge(L.rows_out, step + 1)
                        for t in range(GRP):
                            c = slice(t * P, (t + 1) * P)
                            if L.n == 0:
                                pe.matmul(ps_a[:, t * P:t * P + L0_ROWS], rstage[0:L0_ROWS, q, 0, c], map_x[:, :],
                                          start=True, stop=False)
                                ins = pe.matmul(ps_a[:, t * P:t * P + L0_ROWS], rstage[0:L0_ROWS, q, 1, c], map_ea[:, :],
                                                start=False, stop=True)
                            else:
                                ins = pe.matmul(ps_a[:, t * P:t * P + D], rstage[0:D, q, 0, c],
                                                wl_sb[:, :] if L.n == 2 else ident[0:D, 0:D], start=True, stop=True)
                        ins.then_inc(L.rows_mm, 1)

                    pipeline(pe, GTURNS, [(0, rank_rows)])
                else:
                    def turn_moments(turn, q, _, L=L):
                        step = step_no(turn, q)
                        pe.wait_ge(L.staged, step + 1)
                        pe.wait_ge(L.scaled, step + 1)
                        for t in range(GRP):
                            c = slice(t * P, (t + 1) * P)
                            ins = pe.transpose(ps_a[:, c], rstage[:, q, 0, c], ident[:, :])
                        ins.then_inc(L.t1, 1)

                    def rank_rows1(turn, q, _, L=L):
                        step = step_no(turn, q)
                        pe.wait_ge(L.std_r, step + 1)
                        pe.wait_ge(L.momt, step + 1)
                        for t in range(GRP):
                            ins = pe.transpose(ps_a[:, 512 + t * P:512 + (t + 1) * P], moments[:, q, t, :], ident[:, :])
                        ins.then_inc(L.t2, 1)
                        pe.wait_ge(L.momt, 1 + step + 1)
                        if first(turn) and q == 0:
                            pe.wait_ge(maps_ready, 2)
                        else:
                            pe.wait_ge(L.rows_set, step)
                        for t in range(GRP):
                            c = slice(t * P, (t + 1) * P)
                            z = ps_b[:, t * 256:t * 256 + 3 * D]
                            pe.matmul(z, momt[:, q, c], w_moments[:, :, :], start=True, stop=False)
                            ins = pe.matmul(z, rstage[:, q, 1, c], w_extremes[:, :, :], start=False, stop=True)
                        ins.then_inc(L.rows_mm, 1)

                    pipeline(pe, GTURNS, [(0, turn_moments), (1, rank_rows1)])

                if L.n == 0 or L.n == 2:
                    pe.sem_inc(L.htp, SLOTS)
                    pe.sem_inc(L.dense, SLOTS)

                    def turn_nodes(turn, q, _, L=L):
                        step = step_no(turn, q)
                        pe.wait_ge(L.hs, step + 1)
                        pe.wait_ge(L.hts, step + 1)
                        pe.sem_inc(pe_past, 1)
                        for t in range(GRP):
                            ins = pe.transpose(ps_a[0:D, t * EP:(t + 1) * EP], hstage[:, q, t, :], ident[0:EP, 0:EP])
                        ins.then_inc(L.htp, 1)

                    def up(turn, q, _, L=L):
                        step = step_no(turn, q)
                        pe.wait_ge(L.hts, 1 + step + 1)
                        pe.wait_ge(L.relu, step + 1)
                        pe.matmul(ps_a[:, 512:512 + GRP * EP], w1_sb[:, :], ht[:, q, :], start=True, stop=True) \
                            .then_inc(L.u, 1)

                    def down(turn, q, _, L=L):
                        step = step_no(turn, q)
                        pe.wait_ge(L.relu if L.n == 0 else L.hts, 1 + step + 1)
                        pe.wait_ge(L.dense_out, step + 1)
                        h, w = (h1, w2_sb) if L.n == 0 else (ht, wr_sb)
                        for t in range(GRP):
                            ins = pe.matmul(ps_b[0:EP, t * D:(t + 1) * D], h[:, q, t * EP:(t + 1) * EP], w[:, :],
                                            start=True, stop=True)
                        ins.then_inc(L.dense, 1)

                    if L.n == 0:
                        pe.sem_inc(L.u, SLOTS)
                        pipeline(pe, GTURNS, [(0, turn_nodes), (1, up), (2, down)])
                    else:
                        pipeline(pe, GTURNS, [(0, turn_nodes), (1, down)])
                if L.n == 1:
                    for array, ready in ((n1, L.bn_in), (n2, L.bn_sq)):
                        pe.wait_ge(ready, 1)
                        flat = array.rearrange("p t f -> p (t f)")
                        cols = SUB * D
                        for c in range(NW // cols):
                            ins = pe.matmul(ps_c[0:EP, 0:cols], ones[0:EP, 0:EP], flat[:, c * cols:(c + 1) * cols],
                                            start=(c == 0), stop=(c == NW // cols - 1))
                        ins.then_inc(L.bn_sum, 1)
                if L.n == 2:
                    pe.sem_inc(L.xw_htp, SLOTS)
                    pe.sem_inc(L.xw_mm, SLOTS)

                    def xw_turn(turn, q, _, L=L):
                        step = step_no(turn, q)
                        pe.wait_ge(L.xw_hs, step + 1)
                        pe.wait_ge(L.xw_hts, step + 1)
                        pe.sem_inc(pe_past, 1)
                        for t in range(GRP):
                            ins = pe.transpose(ps_a[0:D, t * EP:(t + 1) * EP], xw_hstage[:, q, t, :], ident[0:EP, 0:EP])
                        ins.then_inc(L.xw_htp, 1)

                    def xw_mm(turn, q, _, L=L):
                        step = step_no(turn, q)
                        pe.wait_ge(L.xw_hts, 1 + step + 1)
                        pe.wait_ge(L.xw_out, step + 1)
                        for t in range(GRP):
                            ps = (ps_b[:, 0:512], ps_b[:, 512:1024], ps_o[:, 0:512], ps_o[:, 512:1024])[t]
                            ins = pe.matmul(ps[0:EP, :], xw_ht[:, q, t * EP:(t + 1) * EP], w3_sb[:, :, :],
                                            start=True, stop=True)
                        ins.then_inc(L.xw_mm, 1)

                    pipeline(pe, GTURNS, [(0, xw_turn), (0, xw_mm)])

        @block.vector
        def _(dve):
            steps = [0]

            def link(ins):
                steps[0] += 1
                ins.then_inc(dve_step, 1)
                dve.wait_ge(dve_step, steps[0])

            dve.memset(dst_left[:, :], -1)
            dve.memset(dst_right[:, :], -1).then_inc(edge_init, 1)
            dve.memset(eps_sb[:, :], EPS).then_inc(maps_ready, 1)
            dve.wait_ge(consts, 5)
            link(dve.tensor_copy(iota[:, :], iota_i[:, :]))
            dve.memset(map_ea[:, :], 0.0)
            dve.tensor_copy(map_x[:, :], ident[0:L0_ROWS, 0:L0_ROWS]).then_inc(maps_init, 1)
            dve.memset(meta_all[:, :, F_WGT + SUB:FIELDS], 0)
            dve.wait_ge(ld_edges, 48)

            def subs(array):
                return array.rearrange("p (s k) -> p s k", k=SUB)

            dve.tensor_copy(meta_all[:, :, F_SRC:F_SRC + SUB], subs(src_all))
            dve.scalar_tensor_tensor(out=meta_all[:, :, F_XW:F_XW + SUB], in0=subs(src_all), scalar=float(RELS),
                                     in1=subs(etype_all), op0=ALU.mult, op1=ALU.add)
            link(dve.tensor_copy(meta_all[:, :, F_WGT:F_WGT + SUB].bitcast(F32), subs(weight_all)))
            dve.sem_inc(edges_copied, 1)
            inside_b = inside.rearrange("p (b e) -> p b e", e=P)
            starts_b = starts.rearrange("p (b e) -> p b e", e=P)
            rel_b = rel.rearrange("p (b e) -> p b e", e=P)
            link(dve.memset(inside, 1.0))
            dve.memset(inside_b[:, :, 0:1], 0.0)
            dve.wait_ge(ld_dst, 48)
            dve.tensor_tensor(starts[:, 1:EW], dst_i[:, 1:EW], dst_i[:, 0:EW - 1], ALU.not_equal)
            dve.tensor_tensor(starts[:, 0:1], dst_i[:, 0:1], dst_left[:, :], ALU.not_equal)
            link(dve.tensor_tensor(ends[:, EW - 1:EW], dst_i[:, EW - 1:EW], dst_right[:, :], ALU.not_equal))
            dve.tensor_copy(ends[:, 0:EW - 1], starts[:, 1:EW])
            dve.tensor_tensor(dst_first, dst_i, starts, ALU.mult)
            dve.tensor_copy(blk_first[:, :], starts_b[:, :, 0])
            link(dve.tensor_tensor_scan(rel, inside, starts, 0.0, ALU.mult, ALU.add))
            dve.tensor_copy(blk_total[:, :], rel_b[:, :, P - 1])
            link(dve.tensor_scalar(restart_row, starts, RESTART, None, ALU.mult))
            dve.sem_inc(restart_ready, 1)
            link(dve.tensor_tensor(rel_b, rel_b, wide(blk_first[:, :], P), ALU.subtract))
            dve.sem_inc(fields_ready, 1)
            dve.tensor_tensor_scan(blk_cum[:, :], ones[0:EP, 0:EB], blk_total[:, :], 0.0, ALU.mult, ALU.add) \
                .then_inc(cum_ready, 1)
            dve.wait_ge(cum_ready, 1)
            link(dve.tensor_tensor(blk_total[:, :], blk_cum[:, :], blk_total[:, :], ALU.subtract))
            link(dve.tensor_tensor(blk_total[:, :], blk_total[:, :], blk_first[:, :], ALU.add))
            dve.wait_ge(base_ready, 1)
            dve.tensor_scalar(blk_window[:, :], blk_total[:, :], ps_c[0:EP, 0:1], -1.0, ALU.add, ALU.add) \
                .then_inc(window_ready, 1)
            dve.wait_ge(ld_const, 18 * 16)
            dve.tensor_scalar(eps1[:, :], eps1[:, :], 1.0, None, ALU.add)
            link(dve.tensor_scalar(w_extremes[0:D], w_extremes[0:D], -1.0, None, ALU.mult))

            for L in layers:
                if L.n == 0:
                    dve.wait_ge(fields_turned, 3 * SUB)
                    dve.wait_ge(restart_stored, 16)
                    link(dve.memset(xs[:, :, :, L0_ROWS + D:2 * L0_ROWS], 0.0))
                    dve.memset(xs[:, :, :, DEG:DEG + 1], 1.0).then_inc(L.prep, 1)
                if L.n == 1:
                    link(dve.memset(scanned[:, SLOTS - 1, SUB * P - 1:SUB * P], 0.0))
                    dve.sem_inc(L.scan, 1)
                dve.sem_inc(L.added, CREDIT)
                dve.wait_ge(acc_zero, L.n + 1)
                n_rows = (L0_ROWS, P, D, D)[L.n]
                halves = 2 if L.n < 2 else 1
                window = {}

                def hot(turn, q, k, L=L):
                    if k == 0:
                        dve.wait_ge(meta_loaded[q], loaded(L, turn))
                        dve.wait_ge(L.summed, block_no(turn, q, SUB))
                    rel_k = meta[:, q, F_REL + k:F_REL + k + 1].bitcast(F32)
                    if L.n == 3:
                        ins = dve.tensor_scalar(onehot[:, q, k, :], iota[:, :], rel_k,
                                                meta[:, q, F_WGT + k:F_WGT + k + 1].bitcast(F32),
                                                ALU.is_equal, ALU.mult)
                    else:
                        ins = dve.tensor_scalar(onehot[:, q, k, :], iota[:, :], rel_k, None, ALU.is_equal)
                    if k == SUB - 1:
                        ins.then_inc(L.onehot, 1)

                def scan(turn, q, k, L=L):
                    if k == SUB - 1:
                        dve.wait_ge(L.tx, step_no(turn, q) + 1)
                        dve.wait_ge(aux_loaded[q], loaded(L, turn))
                        dve.wait_ge(L.tb, step_no(turn, q) + 1)
                        dve.wait_ge(L.scan, 1 + step_no(turn, q))
                        before_q = (q - 1) % SLOTS
                        dve.tensor_tensor_scan(scanned[:, q, :], restart[:, q, :], ps_a[:, 0:SUB * P],
                                               scanned[:, before_q, SUB * P - 1:SUB * P], ALU.add, ALU.max) \
                            .then_inc(L.scan, 1)

                def add(turn, q, k, L=L, n_rows=n_rows, halves=halves, window=window):
                    if k == 0:
                        _, window["of"] = nc.values_load_multi_w_load_instructions(
                            meta[0:1, q, F_WIN:F_WIN + SUB], engines=[mybir.EngineType.DVE], min_val=0, max_val=N - 1,
                            skip_runtime_bounds_check_because="a rank is less than the number of nodes")
                    n = block_no(turn, q, k)
                    dve.wait_ge(L.summed, CREDIT + n + 1)
                    dve.wait_ge(L.added, CREDIT + n)
                    a = acc[0:n_rows, 0:halves, bass.ds(window["of"][k], P)]
                    dve.tensor_tensor(a, a, sums[k][0:n_rows, 0:halves, :], ALU.add).then_inc(L.added, 1)

                if L.n == 1:
                    pipeline(dve, TURNS, [(2, add), (0, hot), (0, scan)], parts=SUB)
                else:
                    pipeline(dve, TURNS, [(1, add), (0, hot)], parts=SUB)

                dve.wait_ge(L.added, CREDIT + BLOCKS)

                def stage(turn, q, _, L=L, n_rows=n_rows, halves=halves):
                    step = step_no(turn, q)
                    dve.wait_ge(L.rows_mm, step + 1)
                    if L.n > 0:
                        if not first(turn):
                            dve.wait_ge(scattered[q], rows_landed(L, turn))
                        dve.tensor_copy(node_of[:, q, :], ranks_of(node_all, turn, q))
                    dve.tensor_copy(rstage[0:n_rows, q, 0:halves, :],
                                    acc[0:n_rows, 0:halves, bass.ds(step * (GRP * P), GRP * P)]).then_inc(L.staged, 1)

                def number(turn, q, _, L=L):
                    step = step_no(turn, q)
                    dve.wait_ge(L.rows_out, 1 + step + 1)
                    if not first(turn):
                        dve.wait_ge(scattered[q], rows_landed(L, turn))
                    dve.tensor_copy(ranks_of(deg, turn, q), rows[:, q, :, DEG])
                    dve.tensor_scalar(no_rank[:, :], rows[:, q, :, DEG], 0.5, float(2 * N), ALU.is_lt, ALU.mult) \
                        .then_inc(L.number, 1)
                    dve.wait_ge(L.number, 2 * step + 1)
                    dve.tensor_tensor(node_of[:, q, :], rows[:, q, :, DST], no_rank[:, :], ALU.add).then_inc(L.number, 1)
                    dve.wait_ge(L.number, 2 * step + 2)
                    dve.tensor_copy(ranks_of(node_all, turn, q), node_of[:, q, :]).then_inc(L.rows_set, 1)

                if L.n == 0:
                    pipeline(dve, GTURNS, [(0, stage), (0, number)])
                    dve.wait_ge(L.rows_set, GROUPS)
                    link(dve.tensor_scalar(inv_deg[:, :], deg[:, :], 1.0, None, ALU.max))
                    link(dve.reciprocal(inv_deg[:, :], inv_deg[:, :]))
                    dve.sem_inc(maps_ready, 1)
                elif L.n == 1:
                    dve.wait_ge(L.logs, 1)
                    link(dve.tensor_scalar(att[:, :], amp[:, :], 1e-12, None, ALU.max))
                    link(dve.reciprocal(att[:, :], att[:, :]))
                    dve.tensor_scalar(att[:, :], att[:, :], AVG_D_LOG, None, ALU.mult)
                    link(dve.tensor_scalar(amp[:, :], amp[:, :], 1.0 / AVG_D_LOG, None, ALU.mult))
                    dve.sem_inc(L.scaled, 1)

                    def moments_dve(turn, q, _, L=L):
                        step = step_no(turn, q)
                        dve.wait_ge(L.t1, step + 1)
                        dve.tensor_tensor(moments[:, q, :, :], ps_a[:, 0:GRP * P].rearrange("p (t c) -> p t c", t=GRP),
                                          wide(ranks_of(inv_deg, turn, q), P), ALU.mult).then_inc(L.scaled, 1)
                        dve.wait_ge(L.sq, step + 1)
                        dve.tensor_tensor(moments[:, q, :, D:P], moments[:, q, :, D:P], meansq[:, q, :, :], ALU.subtract) \
                            .then_inc(L.row_step, 1)
                        dve.wait_ge(L.row_step, 4 * step + 1)
                        dve.tensor_scalar(moments[:, q, :, D:P], moments[:, q, :, D:P], 0.0, None, ALU.max) \
                            .then_inc(L.var_r, 1)
                        z = ps_b[:, :].rearrange("p (t c) -> p t c", t=GRP)
                        dve.wait_ge(L.rows_out, 1 + step + 1)
                        for n, scaler in ((1, amp), (2, att)):
                            dve.tensor_tensor(ztmp, z[:, :, n * D:(n + 1) * D], wide(ranks_of(scaler, turn, q), D),
                                              ALU.mult).then_inc(L.row_step, 1)
                            dve.wait_ge(L.row_step, 4 * step + 2 * n)
                            to = zbase[:, q, :, :] if n == 1 else rows[:, q, :, 0:D]
                            ins = dve.tensor_tensor(to, zbase[:, q, :, :], ztmp, ALU.add)
                            if n == 1:
                                ins.then_inc(L.row_step, 1)
                                dve.wait_ge(L.row_step, 4 * step + 3)
                        ins.then_inc(L.rows_set, 1)

                    pipeline(dve, GTURNS, [(0, stage), (1, moments_dve)])
                else:
                    pipeline(dve, GTURNS, [(0, stage)])

                dve.wait_ge(agg_loaded, 16 * (L.n + 1))
                if L.n == 0:
                    dve.wait_ge(x_loaded, 16)
                if L.n == 0 or L.n == 2:
                    dve.sem_inc(L.dense_out, 1)

                    def nodes_in(turn, q, _, L=L):
                        step = step_no(turn, q)
                        dve.wait_ge(L.htp, step + 1)
                        if L.n == 0:
                            dve.scalar_tensor_tensor(out=hstage[:, q, :, :], in0=tiles_of(xres, turn, q), scalar=eps1[:, 0:1],
                                                     in1=tiles_of(n1, turn, q), op0=ALU.mult, op1=ALU.add).then_inc(L.hs, 1)
                        else:
                            dve.tensor_copy(hstage[:, q, :, :], tiles_of(xres, turn, q)).then_inc(L.hs, 1)

                    def nodes_out(turn, q, _, L=L):
                        step = step_no(turn, q)
                        dve.wait_ge(L.dense, SLOTS + step + 1)
                        dve.tensor_tensor(tiles_of(n1, turn, q), tiles_of(xres if L.n == 0 else n1, turn, q),
                                          ps_b[0:EP, 0:GRP * D].rearrange("p (t f) -> p t f", t=GRP), ALU.add) \
                            .then_inc(L.dense_out, 1)

                    pipeline(dve, GTURNS, [(0, nodes_in), (2, nodes_out)])
                    dve.wait_ge(L.dense_out, 1 + GROUPS)
                    link(dve.tensor_tensor(n1, n1, along(bias["b2" if L.n == 0 else "l2_b"][:, :], NT), ALU.add))
                    if L.n == 2:
                        link(dve.tensor_tensor(n1, n1, xres[:, :, :], ALU.add))
                if L.n == 1:
                    ps_sum = ps_c[0:EP, 0:SUB * D].rearrange("p (t f) -> p f t", t=SUB)
                    dve.tensor_tensor(n1, n1, along(bias["l1_b"][:, :], NT), ALU.add).then_inc(L.bn_in, 1)
                    dve.wait_ge(L.bn_sum, 1)
                    link(dve.tensor_reduce(bn_mean[:, :], ps_sum, AX.X, ALU.add))
                    link(dve.tensor_scalar(bn_mean[:, :], bn_mean[:, :], 1.0 / N, None, ALU.mult))
                    dve.tensor_tensor(n1, n1, along(bn_mean[:, :], NT), ALU.subtract).then_inc(L.bn_cent, 1)
                    dve.wait_ge(L.bn_sum, 2)
                    link(dve.tensor_reduce(bn_scale[:, :], ps_sum, AX.X, ALU.add))
                    dve.tensor_scalar(bn_scale[:, :], bn_scale[:, :], 1.0 / N, None, ALU.mult).then_inc(L.bn_var, 1)
                    dve.wait_ge(L.bn_std, 1)
                    link(dve.reciprocal(bn_scale[:, :], bn_scale[:, :]))
                    link(dve.tensor_tensor(bn_scale[:, :], bn_scale[:, :], bias["l1_gamma"][:, :], ALU.mult))
                    link(dve.tensor_tensor(n1, n1, along(bn_scale[:, :], NT), ALU.mult))
                    dve.tensor_tensor(n1, n1, along(bias["l1_beta"][:, :], NT), ALU.add).then_inc(L.bn_affine, 1)
                    dve.wait_ge(L.bn_relu, 1)
                    link(dve.scalar_tensor_tensor(out=n1, in0=xres[:, :, :], scalar=2.0, in1=n1, op0=ALU.mult, op1=ALU.add))
                if L.n == 3:
                    link(dve.tensor_tensor(n1, n1, xres[:, :, :], ALU.add))

                link(dve.tensor_reduce(ln_mean[:, :], n1, AX.X, ALU.add))
                link(dve.tensor_scalar(ln_mean[:, :], ln_mean[:, :], 1.0 / D, None, ALU.mult))
                dve.tensor_tensor(n1, n1, wide(ln_mean[:, :], D), ALU.subtract).then_inc(centered, 1)
                dve.wait_ge(squared, L.n + 1)
                dve.tensor_reduce(ln_var[:, :], n2, AX.X, ALU.add).then_inc(var, 1)
                dve.wait_ge(std, L.n + 1)
                link(dve.reciprocal(ln_var[:, :], ln_var[:, :]))
                if 0 < L.n < 3:
                    dve.wait_ge(table_ready, 16 * L.n)
                dve.tensor_tensor(xres[:, :, :], n1, wide(ln_var[:, :], D), ALU.mult).then_inc(x_ready, 1)

                if L.n == 2:
                    dve.wait_ge(x_ready, L.n + 1)

                    def xw_in(turn, q, _, L=L):
                        dve.wait_ge(L.xw_htp, step_no(turn, q) + 1)
                        dve.tensor_copy(xw_hstage[:, q, :, :], tiles_of(xres, turn, q)).then_inc(L.xw_hs, 1)

                    pipeline(dve, GTURNS, [(0, xw_in)])


def kernel(**inputs):
    import numpy as np
    import concourse.bacc as bacc
    from concourse.bass_utils import run_bass_kernel_spmd

    def turned(a):
        a = np.asarray(a)
        a = a.reshape(BLOCKS, P, -1).transpose(1, 0, 2)
        return np.ascontiguousarray(a).reshape(P, -1)

    def arr(name, *shape):
        a = np.asarray(inputs[name])
        return np.ascontiguousarray(a.reshape(shape) if shape else a)

    arrays = {
        "x_in": arr("x"),
        "src_e": turned(inputs["src"]),
        "etype_e": turned(inputs["edge_type_8"]),
        "weight_e": turned(inputs["edge_weight"]),
        "dst_n": arr("dst", EP, EW),
        "edge_attr": turned(inputs["edge_attr_64"]),
        "eps_in": arr("L0_gnn_eps", 1, 1),
        "we": arr("L0_gnn_We_w"),
        "we_b": arr("L0_gnn_We_b", 1, D),
        "w1": arr("L0_gnn_W1"),
        "b1": arr("L0_gnn_b1", H, 1),
        "w2": arr("L0_gnn_W2"),
        "b2": arr("L0_gnn_b2", 1, D),
        "l1_w": arr("L1_gnn_W"),
        "l1_b": arr("L1_gnn_b", 1, D),
        "l1_gamma": arr("L1_gnn_gamma", 1, D),
        "l1_beta": arr("L1_gnn_beta", 1, D),
        "wl_t": np.ascontiguousarray(np.asarray(inputs["L2_gnn_w_l"]).T),
        "wr_t": np.ascontiguousarray(np.asarray(inputs["L2_gnn_w_r"]).T),
        "l2_b": arr("L2_gnn_b", 1, D),
        "l3_w": arr("L3_gnn_W"),
    }
    nc = bacc.Bacc("TRN2", target_bir_lowering=False, num_devices=1)
    args = [nc.dram_tensor(n, a.shape, mybir.dt.from_np(a.dtype), kind="ExternalInput").ap() for n, a in arrays.items()]
    out = nc.dram_tensor("out", (N, D), F32, kind="ExternalOutput").ap()
    gnn_kernel(nc, *args, out)
    return run_bass_kernel_spmd(nc, [arrays], core_ids=[0]).results[0]["out"]
```

```python
import concourse.bass as bass
from concourse import mybir
from contextlib import ExitStack

F32 = mybir.dt.float32
I32 = mybir.dt.int32
BF16 = mybir.dt.bfloat16
ALU = mybir.AluOpType
ACT = mybir.ActivationFunctionType
AX = mybir.AxisListType

P = 128
E = 400000
N = 12500
D = 64
H = 128
RELS = 8
BLOCKS = E // P
SUB = 5
SLOTS = 5
SUBS = BLOCKS // SUB
TURNS = SUBS // SLOTS
EP = 125
EW = E // EP
EB = EW // P
NT = N // EP
NW = NT * D
GRP = 4
GROUPS = NT // GRP
GTURNS = GROUPS // SLOTS
RT = GROUPS * GRP
RANKS = RT * P
assert BLOCKS * P == E and TURNS * SLOTS * SUB == BLOCKS and EP * EW == E and EB * P == EW
assert GROUPS * GRP == NT and GTURNS * SLOTS == GROUPS and RANKS >= N + P

AVG_D_LOG = 2.833
EPS = 1e-5
RESTART = -1e30

F_SRC, F_REL, F_END, F_DST, F_XW, F_WGT, F_WIN = 0, 5, 10, 15, 20, 25, 32
FIELDS = 40

XS_COLS = 192
L0_ROWS = 66
DEG, DST = 64, 65


def pipeline(eng, turns, stages, parts=1):
    for q in range(SLOTS):
        for part in range(parts):
            for lag, fn in stages:
                if q >= lag:
                    fn(0, q - lag, part)
    with eng.Fori(1, turns) as turn:
        for q in range(SLOTS):
            for part in range(parts):
                for lag, fn in stages:
                    if q >= lag:
                        fn(turn, q - lag, part)
                    else:
                        fn(turn - 1, q - lag + SLOTS, part)
    for q in range(max(lag for lag, _ in stages)):
        for part in range(parts):
            for lag, fn in stages:
                if q < lag:
                    fn(turns - 1, q - lag + SLOTS, part)


def first(turn):
    return isinstance(turn, int) and turn == 0


def gnn_kernel(nc, x_in, src_e, etype_e, weight_e, dst_n, edge_attr, eps_in, we, we_b, w1, b1, w2, b2,
               l1_w, l1_b, l1_gamma, l1_beta, wl_t, wr_t, l2_b, l3_w, out):
    with ExitStack() as ctx:
        def sb(name, shape, dt=F32):
            return ctx.enter_context(nc.sbuf_tensor(name, shape, dt))

        def psum(name, cols):
            return ctx.enter_context(nc.psum_tensor(name, [P, cols], F32))

        def sem(name):
            return ctx.enter_context(nc.semaphore(name))

        tables = [x_in] + [nc.dram_tensor(f"x{n}_table", [N, D], F32).ap() for n in (1, 2)]
        xw_table = nc.dram_tensor("xw_table", [N * RELS, D], F32).ap()
        agg = [nc.dram_tensor(f"agg{n}", [N, D], F32).ap() for n in range(4)]
        meta_d = nc.dram_tensor("meta_d", [P, SUBS * FIELDS], I32).ap()
        window_d = nc.dram_tensor("window_d", [BLOCKS], I32).ap()
        restart_d = nc.dram_tensor("restart_d", [E], BF16).ap()

        acc = sb("acc", [P, 2, RANKS])
        meta_all = acc[:, :, :].rearrange("p a r -> p (a r)")[:, 0:SUBS * FIELDS].bitcast(I32) \
            .rearrange("p (s f) -> p s f", f=FIELDS)
        xres = sb("xres", [EP, NT, D])
        WORK = 14400
        work = sb("work", [P, WORK])
        meta = sb("meta", [P, SLOTS, FIELDS], I32)
        restart = sb("restart", [P, SLOTS, SUB * P], BF16)

        def carve(at, *dims, parts=P):
            size = 1
            for d in dims:
                size *= d
            assert at + size <= WORK
            v = work[0:parts, at:at + size]
            if len(dims) > 1:
                names = " ".join(f"d{i}" for i in range(len(dims)))
                v = v.rearrange(f"p ({names}) -> p {names}", **{f"d{i}": d for i, d in enumerate(dims)})
            return v, at + size

        xs, at = carve(0, SLOTS, SUB, XS_COLS)
        onehot, at = carve(at, SLOTS, SUB, P)
        scanned, at = carve(at, SLOTS, SUB * P)
        turned, at = carve(at, SLOTS, SUB, P)
        rstage1, at = carve(0, SLOTS, 2, GRP * P)
        moments, at = carve(at, SLOTS, GRP, P)
        meansq, at = carve(at, SLOTS, GRP, D)
        momt, at = carve(at, SLOTS, GRP * P)
        zbase, at = carve(at, SLOTS, GRP, D)
        rows1, at = carve(at, SLOTS, GRP, L0_ROWS)
        ztmp, at = carve(at, GRP, D)
        n1, n2_at = carve(0, NT, D, parts=EP)
        n2, _ = carve(n2_at, NT, D, parts=EP)
        dst_i = work[0:EP, 0:EW].bitcast(I32)
        starts = work[0:EP, EW:2 * EW]
        inside = work[0:EP, 2 * EW:3 * EW]
        restart_row = work[0:EP, 2 * EW:2 * EW + EW // 2].bitcast(BF16)
        rel = work[0:EP, 3 * EW:4 * EW]
        xres_flat = xres[:, :, :].rearrange("p t f -> p (t f)")
        xres_groups = xres_flat.rearrange("p (g f) -> p g f", g=GROUPS)
        ends = xres_flat[:, 0:EW]
        dst_first = xres_flat[:, EW:2 * EW]
        src_all = work[:, 0:BLOCKS].bitcast(I32)
        etype_all = work[:, EW:EW + BLOCKS].bitcast(I32)
        weight_all = work[:, 2 * EW:2 * EW + BLOCKS]

        ident = sb("ident", [P, P])
        iota_i = sb("iota_i", [P, P], I32)
        iota = sb("iota", [P, P])
        ones = sb("ones", [P, P])
        before = sb("before", [P, P])
        zeros = sb("zeros", [EP, 640])
        dst_left = sb("dst_left", [EP, 1], I32)
        dst_right = sb("dst_right", [EP, 1], I32)
        blk_total = sb("blk_total", [EP, EB])
        blk_cum = sb("blk_cum", [EP, EB])
        blk_first = sb("blk_first", [EP, EB])
        blk_window = sb("blk_window", [EP, EB], I32)
        map_x = sb("map_x", [L0_ROWS, L0_ROWS])
        map_ea = sb("map_ea", [L0_ROWS, L0_ROWS])
        w1_sb = sb("w1_sb", [D, H])
        b1_sb = sb("b1_sb", [H, 1])
        w2_sb = sb("w2_sb", [H, D])
        w_moments = sb("w_moments", [P, 3, D])
        w_extremes = sb("w_extremes", [P, 3, D])
        wl_sb = sb("wl_sb", [D, D])
        wr_sb = sb("wr_sb", [D, D])
        w3_sb = sb("w3_sb", [D, RELS, D])
        bias = {n: sb(f"{n}_sb", [EP, D]) for n in ("b2", "l1_b", "l1_gamma", "l1_beta", "l2_b")}
        eps1 = sb("eps1", [EP, 1])
        eps_sb = sb("eps_sb", [P, 1])
        deg = sb("deg", [P, RT])
        inv_deg = sb("inv_deg", [P, RT])
        amp = sb("amp", [P, RT])
        att = sb("att", [P, RT])
        node_all = sb("node_all", [P, RT], I32)
        node_of = sb("node_of", [P, SLOTS, GRP], I32)
        no_rank = sb("no_rank", [P, GRP])
        ln_mean = sb("ln_mean", [EP, NT])
        ln_var = sb("ln_var", [EP, NT])
        bn_mean = sb("bn_mean", [EP, D])
        bn_scale = sb("bn_scale", [EP, D])

        BANK = 512
        ps_a = psum("ps_a", 2 * BANK)
        ps_b = psum("ps_b", 2 * BANK)
        ps_o = psum("ps_o", 4 * BANK)
        ps_rank, ps_turn = ps_a[:, 0:BANK], ps_a[:, BANK:2 * BANK]
        ps_mid, ps_dense = ps_b[:, 0:BANK], ps_b[:, BANK:2 * BANK]
        ps_c = ps_o[:, 3 * BANK:4 * BANK]
        O_BANKS = SUB - 1
        sums = [ps_o[:, (k % O_BANKS) * BANK + (k // O_BANKS) * 2 * P:][:, 0:2 * P].rearrange("p (a c) -> p a c", a=2)
                for k in range(SUB)]

        edge_init = sem("edge_init")
        ld_edges = sem("ld_edges")
        ld_dst = sem("ld_dst")
        ld_const = sem("ld_const")
        consts = sem("consts")
        maps_init = sem("maps_init")
        edges_copied = sem("edges_copied")
        fields_ready = sem("fields_ready")
        fields_turned = sem("fields_turned")
        fields_placed = sem("fields_placed")
        cum_ready = sem("cum_ready")
        base_ready = sem("base_ready")
        window_ready = sem("window_ready")
        window_stored = sem("window_stored")
        window_placed = sem("window_placed")
        restart_ready = sem("restart_ready")
        restart_stored = sem("restart_stored")
        meta_stored = sem("meta_stored")
        agg_zeroed = sem("agg_zeroed")
        maps_ready = sem("maps_ready")
        dve_step = sem("dve_step")
        x_loaded = sem("x_loaded")

        meta_loaded = [sem(f"meta_loaded{q}") for q in range(SLOTS)]
        aux_loaded = [sem(f"aux_loaded{q}") for q in range(SLOTS)]
        gathered = [sem(f"gathered{q}") for q in range(SLOTS)]
        scattered = [sem(f"scattered{q}") for q in range(SLOTS)]
        agg_loaded = [sem(f"agg_loaded{q}") for q in range(SLOTS)]
        xw_stored = [sem(f"xw_stored{q}") for q in range(SLOTS)]

        pool_past = sem("pool_past")
        pe_past = sem("pe_past")
        act_past = sem("act_past")
        sp_past = sem("sp_past")
        acc_zero = sem("acc_zero")
        table_ready = sem("table_ready")
        centered = sem("centered")
        squared = sem("squared")
        var = sem("var")
        std = sem("std")
        x_ready = sem("x_ready")

        class Layer:
            pass

        layers = []
        for n in range(4):
            L = Layer()
            L.n = n

            def ls(name, n=n):
                return sem(f"l{n}_{name}")

            L.prep = ls("prep")
            L.onehot = ls("onehot")
            L.summed = ls("summed")
            L.added = ls("added")
            L.staged = ls("staged")
            L.rows_mm = ls("rows_mm")
            L.rows_out = ls("rows_out")
            if n < 2:
                L.rows_set = ls("rows_set")
            if n != 1:
                L.ln_in = ls("ln_in")
                L.ln_scale = ls("ln_scale")
            if n == 0 or n == 2:
                L.hs = ls("hs")
                L.htp = ls("htp")
                L.hts = ls("hts")
                L.dense = ls("dense")
                L.dense_out = ls("dense_out")
            if n == 0:
                L.number = ls("number")
                L.u = ls("u")
                L.relu = ls("relu")
            if n == 1:
                L.tx = ls("tx")
                L.scan = ls("scan")
                L.tb = ls("tb")
                L.ts = ls("ts")
                L.t1 = ls("t1")
                L.scaled = ls("scaled")
                L.row_step = ls("row_step")
                L.logs = ls("logs")
                L.sq = ls("sq")
                L.var_r = ls("var_r")
                L.std_r = ls("std_r")
                L.t2 = ls("t2")
                L.momt = ls("momt")
                L.bn_in = ls("bn_in")
                L.bn_sum = ls("bn_sum")
                L.bn_cent = ls("bn_cent")
                L.bn_sq = ls("bn_sq")
                L.bn_var = ls("bn_var")
                L.bn_std = ls("bn_std")
                L.bn_affine = ls("bn_affine")
                L.bn_relu = ls("bn_relu")
            if n == 2:
                L.xw_htp = ls("xw_htp")
                L.xw_hts = ls("xw_hts")
                L.xw_mm = ls("xw_mm")
                L.xw_act = ls("xw_act")
                L.xw_dve = ls("xw_dve")
            if n != 1:
                L.rstage, at = carve(0, SLOTS, 2 if n == 0 else 1, GRP * P)
                L.rows, at = carve(at, SLOTS, GRP, L0_ROWS if n == 0 else D)
                L.nodes, at = carve(at, SLOTS, GRP, D, parts=EP)
                if n != 3:
                    L.h_in, at = carve(at, SLOTS, GRP, D, parts=EP)
                    L.ht, at = carve(at, SLOTS, GRP * EP, parts=D)
                if n == 0:
                    L.h1, at = carve(at, SLOTS, GRP * EP, parts=H)
                    L.square = restart[0:EP, :, :].rearrange("p s e -> p (s e)").bitcast(F32)[:, 0:SLOTS * GRP * D] \
                        .rearrange("p (s t f) -> p s t f", s=SLOTS, t=GRP)
                else:
                    L.square, at = carve(at, SLOTS, GRP, D, parts=EP)
                if n == 2:
                    L.x_out, at = carve(at, SLOTS, GRP, D, parts=EP)
                    L.xt, at = carve(at, SLOTS, GRP * EP, parts=D)
                    L.xw = acc[0:EP, 1, 0:SLOTS * GRP * RELS * D].rearrange("p (s t f) -> p s t f", s=SLOTS, t=GRP)
            else:
                L.rstage, L.rows = rstage1, rows1
            layers.append(L)
        out_stored = sem("out_stored")
        CREDIT = SLOTS * SUB
        XW_CREDIT = SLOTS * GRP

        def block_no(turn, q, k):
            return turn * (SLOTS * SUB) + (q * SUB + k)

        def step_no(turn, q):
            return turn * SLOTS + q

        def loaded(L, turn, each=1):
            return turn * (each * 16) + (L.n * TURNS + 1) * each * 16

        def rows_landed(L, turns):
            return turns * (GRP * 16) + L.n * GTURNS * GRP * 16

        def agg_there(L, turns):
            return turns * 16 + (L.n * GTURNS - (GTURNS - 1) * (L.n > 1)) * 16

        def ln_no(L, turn, q):
            return step_no(turn, q) + (L.n * GROUPS + 1)

        def node_view(table):
            return table.rearrange("(g p t) f -> p g (t f)", p=EP, t=GRP)

        def group_of(view, turn, q):
            return view[:, bass.ds(step_no(turn, q), 1), :].rearrange("p g f -> p (g f)")

        def flat(tiles):
            return tiles.rearrange("p t f -> p (t f)")

        def wide(ap, width):
            return ap.unsqueeze(2).to_broadcast([ap.shape[0], ap.shape[1], width])

        def along(ap, tiles):
            return ap.unsqueeze(1).to_broadcast([ap.shape[0], tiles, ap.shape[1]])

        def tiles_of(array, turn, q):
            return array[:, bass.ds(step_no(turn, q) * GRP, GRP), :]

        def ranks_of(array, turn, q):
            return array[:, bass.ds(step_no(turn, q) * GRP, GRP)]

        block = ctx.enter_context(nc.Block())

        @block.sync
        def _(sp):
            sp.dma_start(src_all, src_e).then_inc(ld_edges, 16)
            sp.dma_start(etype_all, etype_e).then_inc(ld_edges, 16)
            sp.dma_start(weight_all, weight_e).then_inc(ld_edges, 16)
            sp.wait_ge(edges_copied, 1)
            sp.dma_start(dst_i, dst_n).then_inc(ld_dst, 16)
            sp.wait_ge(edge_init, 1)
            sp.dma_start(dst_left[1:EP, :], dst_n[0:EP - 1, EW - 1:EW], allow_slow_non_contiguous=True).then_inc(ld_dst, 16)
            sp.dma_start(dst_right[0:EP - 1, :], dst_n[1:EP, 0:1], allow_slow_non_contiguous=True).then_inc(ld_dst, 16)
            sp.wait_ge(maps_init, 1)
            for dst, source in (
                (map_x[DEG:DEG + 1, 0:D], we_b), (map_ea[0:D, 0:D], we), (w1_sb[:, :], w1),
                (b1_sb[:, :], b1), (w2_sb[:, :], w2), (wl_sb[:, :], wl_t), (wr_sb[:, :], wr_t),
                (w3_sb[:, :, :], l3_w.rearrange("r f o -> f r o")),
                (eps1[:, :], eps_in.to_broadcast([EP, 1])),
            ):
                sp.dma_start(dst, source, allow_slow_non_contiguous=True).then_inc(ld_const, 16)
            w_parts = l1_w.rearrange("(g s f) o -> s f g o", g=3, s=4)
            for dst, part in ((w_moments[0:D], 0), (w_extremes[D:P], 1), (w_extremes[0:D], 2), (w_moments[D:P], 3)):
                sp.dma_start(dst, w_parts[part]).then_inc(ld_const, 16)
            for name, source in (("b2", b2), ("l1_b", l1_b), ("l1_gamma", l1_gamma), ("l1_beta", l1_beta), ("l2_b", l2_b)):
                sp.dma_start(bias[name][:, :], source.to_broadcast([EP, D])).then_inc(ld_const, 16)

            sp.wait_ge(window_ready, 1)
            sp.dma_start(window_d.rearrange("(p b) -> p b", p=EP), blk_window[:, :]).then_inc(window_stored, 16)
            sp.wait_ge(restart_ready, 1)
            sp.dma_start(restart_d.rearrange("(p e) -> p e", p=EP), restart_row).then_inc(restart_stored, 16)
            sp.wait_ge(window_stored, 16)
            sp.dma_start(meta_all[0:1, :, F_WIN:F_WIN + SUB], window_d.rearrange("(a s k) -> a s k", a=1, k=SUB)) \
                .then_inc(window_placed, 16)
            sp.wait_ge(fields_placed, 3 * SUB)
            sp.wait_ge(window_placed, 16)
            sp.dma_start(meta_d, meta_all.rearrange("p s f -> p (s f)")).then_inc(meta_stored, 16)
            sp.dma_start(xres_groups, node_view(x_in)).then_inc(x_loaded, 16)
            sp.wait_ge(consts, 6)
            for a in agg:
                sp.dma_start(a.rearrange("(p a t) f -> p a (t f)", p=EP, a=NW // 640),
                             zeros[:, :].unsqueeze(1).to_broadcast([EP, NW // 640, 640])).then_inc(agg_zeroed, 16)
            sp.wait_ge(meta_stored, 16)
            sp.wait_ge(restart_stored, 16)

            meta_v = meta_d.rearrange("p (s f) -> p s f", f=FIELDS)
            ea_v = edge_attr.rearrange("p (b f) -> p b f", f=D)

            for L in layers:
                def load_slot(turn, q, _, L=L):
                    sp.wait_ge(L.added, block_no(turn, q, SUB))
                    s = step_no(turn, q)
                    sp.dma_start(meta[:, q, :], meta_v[:, bass.ds(s, 1), :].rearrange("p s f -> p (s f)")) \
                        .then_inc(meta_loaded[q], 16)
                    if L.n == 0:
                        sp.dma_start(xs[:, q, :, L0_ROWS:L0_ROWS + D], ea_v[:, bass.ds(s * SUB, SUB), :]) \
                            .then_inc(aux_loaded[q], 16)
                    if L.n == 1:
                        sp.dma_start(restart[:, q, :], restart_d.unsqueeze(0)[:, bass.ds(s * (SUB * P), SUB * P)]
                                     .to_broadcast([P, SUB * P])).then_inc(aux_loaded[q], 16)

                if L.n == 0:
                    sp.wait_ge(L.prep, 1)
                pipeline(sp, TURNS, [(0, load_slot)])

                agg_v = node_view(agg[L.n])
                if L.n == 1:
                    for q in range(SLOTS):
                        sp.wait_ge(scattered[q], rows_landed(L, GTURNS))
                    n1_v = n1.rearrange("p (g t) f -> p g (t f)", t=GRP)
                    for q in range(SLOTS):
                        part = slice(q * GTURNS, (q + 1) * GTURNS)
                        sp.dma_start(n1_v[:, part, :], agg_v[:, part, :]).then_inc(agg_loaded[q], 16)
                    for q in range(SLOTS):
                        part = slice(q * GTURNS, (q + 1) * GTURNS)
                        sp.wait_ge(x_ready, GROUPS + (q + 1) * GTURNS)
                        sp.dma_start(node_view(tables[2])[:, part, :], xres_groups[:, part, :]).then_inc(table_ready, 16)
                    continue

                def load_sums(turn, q, _, L=L, agg_v=agg_v):
                    sp.wait_ge(scattered[q], rows_landed(L, turn + 1))
                    sp.sem_inc(sp_past, 1)
                    if not first(turn):
                        sp.wait_ge(x_ready, ln_no(L, turn, q) - SLOTS)
                    sp.dma_start(flat(L.nodes[:, q]), group_of(agg_v, turn, q)).then_inc(agg_loaded[q], 16)

                def store_x(turn, q, _, L=L):
                    sp.wait_ge(x_ready, ln_no(L, turn, q))
                    to = out if L.n == 3 else tables[L.n + 1]
                    sp.dma_start(group_of(node_view(to), turn, q), group_of(xres_groups, turn, q)) \
                        .then_inc(out_stored if L.n == 3 else table_ready, 16)

                xw_v = xw_table.rearrange("(g p t r) f -> p g (t r f)", p=EP, t=GRP, r=RELS)

                def store_xw(turn, q, _, L=L, xw_v=xw_v):
                    step = step_no(turn, q)
                    sp.wait_ge(L.xw_act, 2 + 2 * step + 2)
                    sp.wait_ge(L.xw_dve, 2 + 2 * step + 2)
                    sp.dma_start(group_of(xw_v, turn, q), flat(L.xw[:, q])).then_inc(xw_stored[q], 16)

                if L.n == 2:
                    pipeline(sp, GTURNS, [(0, load_sums), (5, store_xw)])
                else:
                    pipeline(sp, GTURNS, [(5 if L.n == 0 else 4, store_x), (0, load_sums)])
            sp.wait_ge(out_stored, 16 * GROUPS)

        @block.gpsimd
        def _(pool):
            pool.memset(ones[:, :], 1.0).then_inc(consts, 1)
            pool.memset(zeros[:, :], 0.0).then_inc(consts, 1)
            pool.memset(ident[:, :], 0.0).then_inc(consts, 1)
            pool.iota(iota_i[:, :], pattern=[[1, P]], base=0, channel_multiplier=0).then_inc(consts, 1)
            pool.wait_ge(consts, 4)
            pool.affine_select(out=ident[:, :], in_=ident[:, :], compare_op=ALU.not_equal, fill=1.0, base=0,
                               pattern=[[-1, P]], channel_multiplier=1).then_inc(consts, 1)
            pool.affine_select(out=before[:, :], in_=ones[:, :], compare_op=ALU.is_gt, fill=0.0, base=0,
                               pattern=[[1, P]], channel_multiplier=-1).then_inc(consts, 1)

            for L in layers:
                if L.n == 0:
                    pool.wait_ge(meta_stored, 16)
                else:
                    pool.wait_ge(layers[L.n - 1].staged, GROUPS)
                for a in range(2 if L.n < 2 else 1):
                    z = pool.memset(acc[:, a, :], 0.0)
                z.then_inc(acc_zero, 1)

                if L.n == 3:
                    for xw_q in xw_stored:
                        pool.wait_ge(xw_q, GTURNS * 16)
                elif L.n > 0:
                    pool.wait_ge(table_ready, 16 * (GROUPS if L.n == 1 else GROUPS + SLOTS))
                table = xw_table if L.n == 3 else tables[L.n]
                field = F_XW if L.n == 3 else F_SRC
                col = D if L.n == 1 else 0

                def gather(turn, q, k, L=L, table=table, field=field, col=col):
                    if k == 0:
                        pool.wait_ge(meta_loaded[q], loaded(L, turn))
                        pool.sem_inc(pool_past, 1)
                    pool.indirect_dma_start(
                        out=xs[:, q, k, col:col + D], out_offset=None, in_=table,
                        in_offset=bass.IndirectOffsetOnAxis(ap=meta[:, q, field + k:field + k + 1], axis=0),
                    ).then_inc(gathered[q], 16)

                pipeline(pool, TURNS, [(0, gather)], parts=SUB)

                def scatter(turn, q, t, L=L):
                    if t == 0:
                        pool.wait_ge(L.rows_set if L.n < 2 else L.rows_out, step_no(turn, q) + (1 if L.n < 2 else 2))
                        pool.sem_inc(pool_past, 1)
                    pool.indirect_dma_start(
                        out=agg[L.n], out_offset=bass.IndirectOffsetOnAxis(ap=node_of[:, q, t:t + 1], axis=0),
                        in_=L.rows[:, q, t, 0:D], in_offset=None, bounds_check=N - 1, oob_is_err=False,
                    ).then_inc(scattered[q], 16)

                if L.n == 0:
                    pool.wait_ge(agg_zeroed, 16 * len(agg))
                pipeline(pool, GTURNS, [(0, scatter)], parts=GRP)

        @block.scalar
        def _(act):
            act.wait_ge(maps_ready, 1)
            for n, field in enumerate((F_REL, F_END, F_DST)):
                for gd in range(EB // SUB):
                    turned_no = n * SUB + gd
                    act.wait_ge(fields_turned, turned_no + 1)
                    ps = (ps_a, ps_b, ps_o)[turned_no % 3][:, 0:SUB * P].rearrange("p (k c) -> p c k", k=SUB)
                    dst = meta_all.rearrange("p (c g) f -> p c g f", g=EB // SUB)[:, :, gd, field:field + SUB]
                    act.activation(dst.bitcast(F32), ps[:, 0:EP, :], ACT.Copy).then_inc(fields_placed, 1)

            for L in layers:
                if L.n == 0:
                    def prep(turn, q, _, L=L):
                        act.wait_ge(meta_loaded[q], loaded(L, turn))
                        act.wait_ge(L.summed, block_no(turn, q, SUB))
                        act.activation(xs[:, q, :, DST], meta[:, q, F_DST:F_DST + SUB].bitcast(F32), ACT.Copy) \
                            .then_inc(L.prep, 1)

                    act.wait_ge(L.prep, 1)
                    pipeline(act, TURNS, [(0, prep)])
                if L.n == 1:
                    def prep1(turn, q, k, L=L):
                        if k == 0:
                            act.wait_ge(gathered[q], loaded(L, turn, SUB))
                            act.activation(xs[:, q, :, 0:D], xs[:, q, :, D:2 * D], ACT.Copy, scale=-1.0)
                            act.activation(xs[:, q, :, 2 * D:3 * D], xs[:, q, :, D:2 * D], ACT.Square).then_inc(L.prep, 1)

                    def last_edges(turn, q, k, L=L):
                        if k == 0:
                            act.wait_ge(L.tb, SLOTS + step_no(turn, q) + 1)
                            act.wait_ge(L.summed, block_no(turn, q, SUB))
                        ins = act.activation(turned[:, q, k, :], ps_b[:, k * P:(k + 1) * P], ACT.Copy,
                                             scale=meta[:, q, F_END + k:F_END + k + 1].bitcast(F32))
                        if k == SUB - 1:
                            ins.then_inc(L.ts, 1)

                    act.sem_inc(L.ts, 1)
                    pipeline(act, TURNS, [(0, prep1), (1, last_edges)], parts=SUB)

                def columns(turn, q, _, L=L):
                    step = step_no(turn, q)
                    n_rows, halves = (L0_ROWS, 2) if L.n == 0 else (D, 1)
                    act.wait_ge(L.rows_mm, step + 1)
                    act.sem_inc(act_past, 1)
                    act.activation(L.rstage[0:n_rows, q], acc[0:n_rows, 0:halves, bass.ds(step * (GRP * P), GRP * P)],
                                   ACT.Copy).then_inc(L.staged, 1)

                def rows_out(turn, q, _, L=L):
                    act.wait_ge(L.rows_mm, SLOTS + step_no(turn, q) + 1)
                    if not first(turn):
                        act.wait_ge(scattered[q], rows_landed(L, turn))
                    act.activation(L.rows[:, q], ps_rank.rearrange("p (t c) -> p t c", t=GRP)[:, :, 0:L0_ROWS], ACT.Copy) \
                        .then_inc(L.rows_out, 1)

                def copy_in(turn, q, _, L=L):
                    act.wait_ge(L.htp, step_no(turn, q) + 1)
                    act.sem_inc(act_past, 1)
                    act.activation(L.h_in[:, q], tiles_of(xres, turn, q), ACT.Copy).then_inc(L.hs, 1)

                def take_turned(turn, q, _, L=L):
                    step = step_no(turn, q)
                    act.wait_ge(L.htp, SLOTS + step + 1)
                    act.wait_ge(L.u if L.n == 0 else L.dense, step + 1)
                    act.activation(L.ht[:, q, :], ps_turn[0:D, 0:GRP * EP], ACT.Copy).then_inc(L.hts, 1)

                def hidden(turn, q, _, L=L):
                    step = step_no(turn, q)
                    act.wait_ge(L.u, SLOTS + step + 1)
                    act.wait_ge(L.dense, step + 1)
                    act.activation(L.h1[:, q, :], ps_mid[:, 0:GRP * EP], ACT.Relu, bias=b1_sb[:, 0:1]).then_inc(L.relu, 1)

                def square(turn, q, _, L=L):
                    act.wait_ge(centered, ln_no(L, turn, q))
                    act.activation(L.square[:, q], L.nodes[:, q], ACT.Square).then_inc(squared, 1)

                def deviation(turn, q, _, L=L):
                    act.wait_ge(var, ln_no(L, turn, q))
                    v = ln_var[:, q * GRP:(q + 1) * GRP]
                    act.activation(v, v, ACT.Sqrt, bias=eps_sb[0:EP, 0:1], scale=1.0 / D).then_inc(std, 1)

                def copy_out(turn, q, _, L=L):
                    act.wait_ge(x_ready, ln_no(L, turn, q))
                    act.sem_inc(act_past, 1)
                    act.activation(tiles_of(xres, turn, q), L.x_out[:, q], ACT.Copy)

                def xw_turned(turn, q, _, L=L):
                    step = step_no(turn, q)
                    act.wait_ge(L.xw_htp, SLOTS + step + 1)
                    act.wait_ge(L.xw_mm, GRP * (step + 1))
                    act.activation(L.xt[:, q, :], ps_mid[0:D, 0:GRP * EP], ACT.Copy).then_inc(L.xw_hts, 1)

                def xw_out(turn, q, _, L=L):
                    step = step_no(turn, q)
                    if not first(turn):
                        act.wait_ge(xw_stored[q], turn * 16)
                    for t in (0, 1):
                        act.wait_ge(L.xw_mm, XW_CREDIT + GRP * step + (t + 1))
                        act.activation(L.xw[:, q, t, :], ps_o[0:EP, t * BANK:(t + 1) * BANK], ACT.Copy).then_inc(L.xw_act, 1)

                if L.n != 2 and L.n != 3:
                    act.sem_inc(L.rows_out, 1)
                if L.n != 1:
                    act.wait_ge(L.added, CREDIT + BLOCKS)
                if L.n == 0:
                    act.sem_inc(L.hts, 1)
                    act.sem_inc(L.relu, 1)
                    act.wait_ge(ld_const, 18 * 16)
                    pipeline(act, GTURNS, [(0, columns), (5, square), (4, hidden), (5, deviation), (3, take_turned),
                                           (0, rows_out)])
                elif L.n == 2:
                    act.sem_inc(L.hts, 1)
                    act.sem_inc(L.xw_hts, 1)
                    act.sem_inc(L.xw_act, 2)
                    pipeline(act, GTURNS, [(0, columns), (5, xw_turned), (0, copy_in), (1, take_turned), (4, deviation),
                                           (3, square), (4, copy_out), (5, xw_out)])
                elif L.n == 3:
                    pipeline(act, GTURNS, [(0, columns), (4, deviation), (3, square)])
                else:
                    act.wait_ge(maps_ready, 2)
                    act.activation(amp[:, :], deg[:, :], ACT.Ln, bias=1.0).then_inc(L.logs, 1)
                    act.sem_inc(L.momt, 1)

                    def moments_act(turn, q, _, L=L):
                        step = step_no(turn, q)
                        act.wait_ge(L.scaled, 1 + step + 1)
                        act.activation(meansq[:, q, :, :], moments[:, q, :, 0:D], ACT.Square).then_inc(L.sq, 1)
                        act.wait_ge(L.var_r, step + 1)
                        act.activation(moments[:, q, :, D:P], moments[:, q, :, D:P], ACT.Sqrt, bias=eps_sb[:, 0:1]) \
                            .then_inc(L.std_r, 1)
                        act.wait_ge(L.t2, step + 1)
                        act.activation(momt[:, q, :], ps_a[:, 512:512 + GRP * P], ACT.Copy).then_inc(L.momt, 1)
                        act.wait_ge(L.rows_mm, SLOTS + step + 1)
                        act.activation(zbase[:, q, :, :], ps_b[:, :].rearrange("p (t c) -> p t c", t=GRP)[:, :, 0:D],
                                       ACT.Copy).then_inc(L.rows_out, 1)

                    pipeline(act, GTURNS, [(1, moments_act)])

                if L.n == 1:
                    act.wait_ge(L.bn_cent, 1)
                    act.activation(n2, n1, ACT.Square).then_inc(L.bn_sq, 1)
                    act.wait_ge(L.bn_var, 1)
                    act.activation(bn_scale[:, :], bn_scale[:, :], ACT.Sqrt, bias=eps_sb[0:EP, 0:1]).then_inc(L.bn_std, 1)
                    act.wait_ge(L.bn_affine, 1)
                    act.activation(n1, n1, ACT.Relu).then_inc(L.bn_relu, 1)
                    act.wait_ge(centered, 2 * GROUPS)
                    act.activation(n2, n1, ACT.Square).then_inc(squared, GROUPS)
                    act.wait_ge(var, 2 * GROUPS)
                    act.activation(ln_var[:, :], ln_var[:, :], ACT.Sqrt, bias=eps_sb[0:EP, 0:1], scale=1.0 / D) \
                        .then_inc(std, GROUPS)

        @block.tensor
        def _(pe):
            pe.wait_ge(consts, 6)
            pe.wait_ge(fields_ready, 1)
            for n, field in enumerate((rel, ends, dst_first)):
                for gd in range(EB // SUB):
                    turned_no = n * SUB + gd
                    if turned_no >= 3:
                        pe.wait_ge(fields_placed, turned_no - 2)
                    ps = (ps_a, ps_b, ps_o)[turned_no % 3]
                    for k in range(SUB):
                        g = gd * SUB + k
                        ins = pe.transpose(ps[:, k * P:k * P + EP], field[:, g * P:(g + 1) * P], ident[0:EP, 0:EP])
                    ins.then_inc(fields_turned, 1)
            pe.wait_ge(cum_ready, 1)
            pe.matmul(ps_c[0:EP, 0:1], before[0:EP, 0:EP], blk_cum[:, EB - 1:EB], start=True, stop=True) \
                .then_inc(base_ready, 1)

            for L in layers:
                pe.sem_inc(L.summed, CREDIT)
                if L.n == 1:
                    pe.sem_inc(L.tb, SLOTS)

                def sum_block(turn, q, k, L=L):
                    if k == 0:
                        pe.wait_ge(gathered[q], loaded(L, turn, SUB))
                        pe.wait_ge(L.onehot, step_no(turn, q) + 1)
                        if L.n == 0:
                            pe.wait_ge(aux_loaded[q], loaded(L, turn))
                            pe.wait_ge(L.prep, 1 + step_no(turn, q) + 1)
                        if L.n == 1:
                            pe.wait_ge(L.ts, 1 + step_no(turn, q) + 1)
                    behind = {0: 1, SUB - 1: O_BANKS}.get(k, SUB)
                    pe.wait_ge(L.added, CREDIT + block_no(turn, q, k) + 1 - behind)
                    s = onehot[:, q, k, :]
                    if L.n == 0:
                        pe.matmul(sums[k][0:L0_ROWS, 0, :], xs[:, q, k, 0:L0_ROWS], s, start=True, stop=True)
                        ins = pe.matmul(sums[k][0:L0_ROWS, 1, :], xs[:, q, k, L0_ROWS:2 * L0_ROWS], s, start=True, stop=True)
                    elif L.n == 1:
                        pe.matmul(sums[k][:, 0, :], xs[:, q, k, D:3 * D], s, start=True, stop=True)
                        ins = pe.matmul(sums[k][:, 1, :], turned[:, q, k, :], s, start=True, stop=True)
                    else:
                        ins = pe.matmul(sums[k][0:D, 0, :], xs[:, q, k, 0:D], s, start=True, stop=True)
                    ins.then_inc(L.summed, 1)

                if L.n != 1:
                    pipeline(pe, TURNS, [(0, sum_block)], parts=SUB)
                else:
                    def turn_rows(turn, q, k, L=L):
                        if k == 0:
                            pe.wait_ge(L.prep, step_no(turn, q) + 1)
                            pe.wait_ge(L.scan, step_no(turn, q) + 1)
                        ins = pe.transpose(ps_a[:, k * P:(k + 1) * P], xs[:, q, k, 0:P], ident[:, :])
                        if k == SUB - 1:
                            ins.then_inc(L.tx, 1)

                    def turn_back(turn, q, k, L=L):
                        if k == 0:
                            pe.wait_ge(L.scan, 1 + step_no(turn, q) + 1)
                            pe.wait_ge(L.ts, step_no(turn, q) + 1)
                        ins = pe.transpose(ps_b[:, k * P:(k + 1) * P], scanned[:, q, k * P:(k + 1) * P], ident[:, :])
                        if k == SUB - 1:
                            ins.then_inc(L.tb, 1)

                    pipeline(pe, TURNS, [(2, sum_block), (1, turn_back), (0, turn_rows)], parts=SUB)

                pe.sem_inc(L.rows_mm, SLOTS)
                def rank_rows(turn, q, _, L=L):
                    step = step_no(turn, q)
                    if L.n == 0 and first(turn) and q == 0:
                        pe.wait_ge(ld_const, 18 * 16)
                    if L.n == 2 and first(turn) and q == 0:
                        pe.wait_ge(maps_ready, 2)
                    pe.wait_ge(L.staged, step + 1)
                    pe.wait_ge(L.rows_out, step + 1)
                    for t in range(GRP):
                        c = slice(t * P, (t + 1) * P)
                        if L.n == 0:
                            pe.matmul(ps_rank[:, t * P:t * P + L0_ROWS], L.rstage[0:L0_ROWS, q, 0, c], map_x[:, :],
                                      start=True, stop=False)
                            ins = pe.matmul(ps_rank[:, t * P:t * P + L0_ROWS], L.rstage[0:L0_ROWS, q, 1, c], map_ea[:, :],
                                            start=False, stop=True)
                        else:
                            ins = pe.matmul(ps_rank[:, t * P:t * P + D], L.rstage[0:D, q, 0, c],
                                            wl_sb[:, :] if L.n == 2 else ident[0:D, 0:D], start=True, stop=True)
                    ins.then_inc(L.rows_mm, 1)

                def turn_nodes(turn, q, _, L=L):
                    step = step_no(turn, q)
                    pe.wait_ge(L.hs, step + 1)
                    pe.wait_ge(L.hts, step + 1)
                    pe.sem_inc(pe_past, 1)
                    for t in range(GRP):
                        ins = pe.transpose(ps_turn[0:D, t * EP:(t + 1) * EP], L.h_in[:, q, t, :], ident[0:EP, 0:EP])
                    ins.then_inc(L.htp, 1)

                def up(turn, q, _, L=L):
                    step = step_no(turn, q)
                    pe.wait_ge(L.hts, 1 + step + 1)
                    pe.wait_ge(L.relu, step + 1)
                    pe.matmul(ps_mid[:, 0:GRP * EP], w1_sb[:, :], L.ht[:, q, :], start=True, stop=True).then_inc(L.u, 1)

                def down(turn, q, _, L=L):
                    step = step_no(turn, q)
                    pe.wait_ge(L.relu if L.n == 0 else L.hts, 1 + step + 1)
                    pe.wait_ge(L.dense_out, step + 1)
                    h, w = (L.h1, w2_sb) if L.n == 0 else (L.ht, wr_sb)
                    for t in range(GRP):
                        ins = pe.matmul(ps_dense[0:EP, t * D:(t + 1) * D], h[:, q, t * EP:(t + 1) * EP], w[:, :],
                                        start=True, stop=True)
                    ins.then_inc(L.dense, 1)

                def turn_x(turn, q, _, L=L):
                    step = step_no(turn, q)
                    pe.wait_ge(x_ready, ln_no(L, turn, q))
                    pe.wait_ge(L.xw_hts, step + 1)
                    pe.sem_inc(pe_past, 1)
                    for t in range(GRP):
                        ins = pe.transpose(ps_mid[0:D, t * EP:(t + 1) * EP], L.x_out[:, q, t, :], ident[0:EP, 0:EP])
                    ins.then_inc(L.xw_htp, 1)

                def xw_mm(turn, q, _, L=L):
                    step = step_no(turn, q)
                    pe.wait_ge(L.xw_hts, 1 + step + 1)
                    for t in range(GRP):
                        pe.wait_ge(L.xw_act if t < 2 else L.xw_dve, 2 * step + (t % 2 + 1))
                        pe.matmul(ps_o[0:EP, t * BANK:(t + 1) * BANK], L.xt[:, q, t * EP:(t + 1) * EP], w3_sb[:, :, :],
                                  start=True, stop=True).then_inc(L.xw_mm, 1)

                if L.n == 0 or L.n == 2:
                    pe.sem_inc(L.htp, SLOTS)
                    pe.sem_inc(L.dense, SLOTS)
                if L.n == 0:
                    pe.sem_inc(L.u, SLOTS)
                    pipeline(pe, GTURNS, [(4, up), (0, rank_rows), (3, turn_nodes), (4, down)])
                elif L.n == 2:
                    pe.sem_inc(L.xw_htp, SLOTS)
                    pe.sem_inc(L.xw_mm, XW_CREDIT)
                    pipeline(pe, GTURNS, [(0, rank_rows), (3, down), (1, turn_nodes), (5, xw_mm), (4, turn_x)])
                elif L.n == 3:
                    pipeline(pe, GTURNS, [(0, rank_rows)])
                else:
                    def turn_moments(turn, q, _, L=L):
                        step = step_no(turn, q)
                        pe.wait_ge(L.staged, step + 1)
                        pe.wait_ge(L.scaled, step + 1)
                        for t in range(GRP):
                            c = slice(t * P, (t + 1) * P)
                            ins = pe.transpose(ps_a[:, c], L.rstage[:, q, 0, c], ident[:, :])
                        ins.then_inc(L.t1, 1)

                    def rank_rows1(turn, q, _, L=L):
                        step = step_no(turn, q)
                        pe.wait_ge(L.std_r, step + 1)
                        pe.wait_ge(L.momt, step + 1)
                        for t in range(GRP):
                            ins = pe.transpose(ps_a[:, 512 + t * P:512 + (t + 1) * P], moments[:, q, t, :], ident[:, :])
                        ins.then_inc(L.t2, 1)
                        pe.wait_ge(L.momt, 1 + step + 1)
                        if first(turn) and q == 0:
                            pe.wait_ge(maps_ready, 2)
                        else:
                            pe.wait_ge(L.rows_set, step)
                        for t in range(GRP):
                            c = slice(t * P, (t + 1) * P)
                            z = ps_b[:, t * 256:t * 256 + 3 * D]
                            pe.matmul(z, momt[:, q, c], w_moments[:, :, :], start=True, stop=False)
                            ins = pe.matmul(z, L.rstage[:, q, 1, c], w_extremes[:, :, :], start=False, stop=True)
                        ins.then_inc(L.rows_mm, 1)

                    pipeline(pe, GTURNS, [(0, turn_moments), (1, rank_rows1)])

                if L.n == 1:
                    for array, ready in ((n1, L.bn_in), (n2, L.bn_sq)):
                        pe.wait_ge(ready, 1)
                        cells = flat(array)
                        cols = SUB * D
                        for c in range(NW // cols):
                            ins = pe.matmul(ps_c[0:EP, 0:cols], ones[0:EP, 0:EP], cells[:, c * cols:(c + 1) * cols],
                                            start=(c == 0), stop=(c == NW // cols - 1))
                        ins.then_inc(L.bn_sum, 1)

        @block.vector
        def _(dve):
            steps = [0]

            def link(ins):
                steps[0] += 1
                ins.then_inc(dve_step, 1)
                dve.wait_ge(dve_step, steps[0])

            dve.memset(dst_left[:, :], -1)
            dve.memset(dst_right[:, :], -1).then_inc(edge_init, 1)
            dve.memset(eps_sb[:, :], EPS).then_inc(maps_ready, 1)
            dve.wait_ge(consts, 5)
            link(dve.tensor_copy(iota[:, :], iota_i[:, :]))
            dve.memset(map_ea[:, :], 0.0)
            dve.tensor_copy(map_x[:, :], ident[0:L0_ROWS, 0:L0_ROWS]).then_inc(maps_init, 1)
            dve.memset(meta_all[:, :, F_WGT + SUB:FIELDS], 0)
            dve.wait_ge(ld_edges, 48)

            def subs(array):
                return array.rearrange("p (s k) -> p s k", k=SUB)

            dve.tensor_copy(meta_all[:, :, F_SRC:F_SRC + SUB], subs(src_all))
            dve.scalar_tensor_tensor(out=meta_all[:, :, F_XW:F_XW + SUB], in0=subs(src_all), scalar=float(RELS),
                                     in1=subs(etype_all), op0=ALU.mult, op1=ALU.add)
            link(dve.tensor_copy(meta_all[:, :, F_WGT:F_WGT + SUB].bitcast(F32), subs(weight_all)))
            dve.sem_inc(edges_copied, 1)
            inside_b = inside.rearrange("p (b e) -> p b e", e=P)
            starts_b = starts.rearrange("p (b e) -> p b e", e=P)
            rel_b = rel.rearrange("p (b e) -> p b e", e=P)
            link(dve.memset(inside, 1.0))
            dve.memset(inside_b[:, :, 0:1], 0.0)
            dve.wait_ge(ld_dst, 48)
            dve.tensor_tensor(starts[:, 1:EW], dst_i[:, 1:EW], dst_i[:, 0:EW - 1], ALU.not_equal)
            dve.tensor_tensor(starts[:, 0:1], dst_i[:, 0:1], dst_left[:, :], ALU.not_equal)
            link(dve.tensor_tensor(ends[:, EW - 1:EW], dst_i[:, EW - 1:EW], dst_right[:, :], ALU.not_equal))
            dve.tensor_copy(ends[:, 0:EW - 1], starts[:, 1:EW])
            dve.tensor_tensor(dst_first, dst_i, starts, ALU.mult)
            dve.tensor_copy(blk_first[:, :], starts_b[:, :, 0])
            link(dve.tensor_tensor_scan(rel, inside, starts, 0.0, ALU.mult, ALU.add))
            dve.tensor_copy(blk_total[:, :], rel_b[:, :, P - 1])
            link(dve.tensor_scalar(restart_row, starts, RESTART, None, ALU.mult))
            dve.sem_inc(restart_ready, 1)
            link(dve.tensor_tensor(rel_b, rel_b, wide(blk_first[:, :], P), ALU.subtract))
            dve.sem_inc(fields_ready, 1)
            dve.tensor_tensor_scan(blk_cum[:, :], ones[0:EP, 0:EB], blk_total[:, :], 0.0, ALU.mult, ALU.add) \
                .then_inc(cum_ready, 1)
            dve.wait_ge(cum_ready, 1)
            link(dve.tensor_tensor(blk_total[:, :], blk_cum[:, :], blk_total[:, :], ALU.subtract))
            link(dve.tensor_tensor(blk_total[:, :], blk_total[:, :], blk_first[:, :], ALU.add))
            dve.wait_ge(base_ready, 1)
            dve.tensor_scalar(blk_window[:, :], blk_total[:, :], ps_c[0:EP, 0:1], -1.0, ALU.add, ALU.add) \
                .then_inc(window_ready, 1)
            dve.wait_ge(ld_const, 18 * 16)
            dve.tensor_scalar(eps1[:, :], eps1[:, :], 1.0, None, ALU.add)
            dve.tensor_tensor(wr_sb[:, :], wr_sb[:, :], ident[0:D, 0:D], ALU.add)
            link(dve.tensor_scalar(w_extremes[0:D], w_extremes[0:D], -1.0, None, ALU.mult))

            for L in layers:
                if L.n == 0:
                    dve.wait_ge(fields_turned, 3 * SUB)
                    dve.wait_ge(restart_stored, 16)
                    link(dve.memset(xs[:, :, :, L0_ROWS + D:2 * L0_ROWS], 0.0))
                    dve.memset(xs[:, :, :, DEG:DEG + 1], 1.0).then_inc(L.prep, 1)
                if L.n == 1:
                    link(dve.memset(scanned[:, SLOTS - 1, SUB * P - 1:SUB * P], 0.0))
                    dve.sem_inc(L.scan, 1)
                dve.sem_inc(L.added, CREDIT)
                dve.wait_ge(acc_zero, L.n + 1)
                n_rows = (L0_ROWS, P, D, D)[L.n]
                halves = 2 if L.n < 2 else 1
                window = {}

                def hot(turn, q, k, L=L):
                    if k == 0:
                        dve.wait_ge(meta_loaded[q], loaded(L, turn))
                        dve.wait_ge(L.summed, block_no(turn, q, SUB))
                    rel_k = meta[:, q, F_REL + k:F_REL + k + 1].bitcast(F32)
                    if L.n == 3:
                        ins = dve.tensor_scalar(onehot[:, q, k, :], iota[:, :], rel_k,
                                                meta[:, q, F_WGT + k:F_WGT + k + 1].bitcast(F32),
                                                ALU.is_equal, ALU.mult)
                    else:
                        ins = dve.tensor_scalar(onehot[:, q, k, :], iota[:, :], rel_k, None, ALU.is_equal)
                    if k == SUB - 1:
                        ins.then_inc(L.onehot, 1)

                def scan(turn, q, k, L=L):
                    if k == SUB - 1:
                        dve.wait_ge(L.tx, step_no(turn, q) + 1)
                        dve.wait_ge(aux_loaded[q], loaded(L, turn))
                        dve.wait_ge(L.tb, step_no(turn, q) + 1)
                        dve.wait_ge(L.scan, 1 + step_no(turn, q))
                        before_q = (q - 1) % SLOTS
                        dve.tensor_tensor_scan(scanned[:, q, :], restart[:, q, :], ps_a[:, 0:SUB * P],
                                               scanned[:, before_q, SUB * P - 1:SUB * P], ALU.add, ALU.max) \
                            .then_inc(L.scan, 1)

                def add(turn, q, k, L=L, n_rows=n_rows, halves=halves, window=window):
                    if k == 0:
                        _, window["of"] = nc.values_load_multi_w_load_instructions(
                            meta[0:1, q, F_WIN:F_WIN + SUB], engines=[mybir.EngineType.DVE], min_val=0, max_val=N - 1,
                            skip_runtime_bounds_check_because="a rank is less than the number of nodes")
                    n = block_no(turn, q, k)
                    dve.wait_ge(L.summed, CREDIT + n + 1)
                    dve.wait_ge(L.added, CREDIT + n)
                    a = acc[0:n_rows, 0:halves, bass.ds(window["of"][k], P)]
                    dve.tensor_tensor(a, a, sums[k][0:n_rows, 0:halves, :], ALU.add).then_inc(L.added, 1)

                if L.n == 1:
                    pipeline(dve, TURNS, [(2, add), (0, hot), (0, scan)], parts=SUB)
                else:
                    pipeline(dve, TURNS, [(1, add), (0, hot)], parts=SUB)

                dve.wait_ge(L.added, CREDIT + BLOCKS)

                def node_numbers(turn, q, L=L):
                    if not first(turn):
                        dve.wait_ge(scattered[q], rows_landed(L, turn))
                    dve.tensor_copy(node_of[:, q, :], ranks_of(node_all, turn, q))

                def stage(turn, q, _, L=L, node_numbers=node_numbers):
                    step = step_no(turn, q)
                    dve.wait_ge(L.rows_mm, step + 1)
                    node_numbers(turn, q)
                    dve.tensor_copy(L.rstage[:, q], acc[:, :, bass.ds(step * (GRP * P), GRP * P)]).then_inc(L.staged, 1)

                def rows_out(turn, q, _, L=L, node_numbers=node_numbers):
                    step = step_no(turn, q)
                    dve.wait_ge(L.rows_mm, SLOTS + step + 1)
                    node_numbers(turn, q)
                    ps = ps_rank.rearrange("p (t c) -> p t c", t=GRP)[:, :, 0:D]
                    if L.n == 2:
                        ins = dve.tensor_tensor(L.rows[:, q], ps, wide(ranks_of(inv_deg, turn, q), D), ALU.mult)
                    else:
                        ins = dve.tensor_copy(L.rows[:, q], ps)
                    ins.then_inc(L.rows_out, 1)

                def nodes_in(turn, q, _, L=L):
                    step = step_no(turn, q)
                    dve.wait_ge(agg_loaded[q], agg_there(L, turn + 1))
                    dve.wait_ge(L.htp, step + 1)
                    dve.scalar_tensor_tensor(out=L.h_in[:, q], in0=tiles_of(xres, turn, q), scalar=eps1[:, 0:1],
                                             in1=L.nodes[:, q], op0=ALU.mult, op1=ALU.add).then_inc(L.hs, 1)

                def center(turn, q, _, L=L):
                    step = step_no(turn, q)
                    v, mean = L.nodes[:, q], ln_mean[:, q * GRP:(q + 1) * GRP]
                    if L.n == 3:
                        dve.wait_ge(agg_loaded[q], agg_there(L, turn + 1))
                        dve.tensor_tensor(v, tiles_of(xres, turn, q), v, ALU.add).then_inc(L.ln_in, 1)
                    else:
                        if L.n == 2:
                            dve.wait_ge(agg_loaded[q], agg_there(L, turn + 1))
                        dve.wait_ge(L.dense, SLOTS + step + 1)
                        dve.tensor_tensor(v, tiles_of(xres, turn, q) if L.n == 0 else v,
                                          ps_dense[0:EP, 0:GRP * D].rearrange("p (t f) -> p t f", t=GRP), ALU.add) \
                            .then_inc(L.dense_out, 1)
                        dve.wait_ge(L.dense_out, 1 + step + 1)
                        dve.tensor_tensor(v, v, along(bias["b2" if L.n == 0 else "l2_b"][:, :], GRP), ALU.add) \
                            .then_inc(L.ln_in, 1)
                    dve.wait_ge(L.ln_in, 2 * step + 1)
                    dve.tensor_reduce(mean, v, AX.X, ALU.add).then_inc(L.ln_in, 1)
                    dve.wait_ge(L.ln_in, 2 * step + 2)
                    dve.scalar_tensor_tensor(out=v, in0=wide(mean, D), scalar=-1.0 / D, in1=v, op0=ALU.mult, op1=ALU.add) \
                        .then_inc(centered, 1)

                def variance(turn, q, _, L=L):
                    dve.wait_ge(squared, ln_no(L, turn, q))
                    dve.tensor_reduce(ln_var[:, q * GRP:(q + 1) * GRP], L.square[:, q], AX.X, ALU.add).then_inc(var, 1)

                def scale(turn, q, _, L=L):
                    step = step_no(turn, q)
                    v = ln_var[:, q * GRP:(q + 1) * GRP]
                    dve.wait_ge(std, ln_no(L, turn, q))
                    dve.reciprocal(v, v).then_inc(L.ln_scale, 1)
                    if L.n == 2:
                        dve.wait_ge(L.xw_htp, step + 1)
                    dve.wait_ge(L.ln_scale, step + 1)
                    dve.tensor_tensor(L.x_out[:, q] if L.n == 2 else tiles_of(xres, turn, q), L.nodes[:, q], wide(v, D),
                                      ALU.mult).then_inc(x_ready, 1)

                def xw_out(turn, q, _, L=L):
                    step = step_no(turn, q)
                    if not first(turn):
                        dve.wait_ge(xw_stored[q], turn * 16)
                    for t in (2, 3):
                        dve.wait_ge(L.xw_mm, XW_CREDIT + GRP * step + (t + 1))
                        dve.tensor_copy(L.xw[:, q, t, :], ps_o[0:EP, t * BANK:(t + 1) * BANK]).then_inc(L.xw_dve, 1)

                def number(turn, q, _, L=L):
                    step = step_no(turn, q)
                    dve.wait_ge(L.rows_out, 1 + step + 1)
                    if not first(turn):
                        dve.wait_ge(scattered[q], rows_landed(L, turn))
                    dve.tensor_copy(ranks_of(deg, turn, q), L.rows[:, q, :, DEG])
                    dve.tensor_scalar(no_rank[:, :], L.rows[:, q, :, DEG], 0.5, float(2 * N), ALU.is_lt, ALU.mult) \
                        .then_inc(L.number, 1)
                    dve.wait_ge(L.number, 2 * step + 1)
                    dve.tensor_tensor(node_of[:, q, :], L.rows[:, q, :, DST], no_rank[:, :], ALU.add).then_inc(L.number, 1)
                    dve.wait_ge(L.number, 2 * step + 2)
                    dve.tensor_copy(ranks_of(node_all, turn, q), node_of[:, q, :]).then_inc(L.rows_set, 1)

                if L.n == 0:
                    dve.wait_ge(x_loaded, 16)
                    dve.sem_inc(L.dense_out, 1)
                    pipeline(dve, GTURNS, [(5, center), (3, nodes_in), (5, variance), (5, scale), (0, number)])
                    dve.wait_ge(L.rows_set, GROUPS)
                    link(dve.tensor_scalar(inv_deg[:, :], deg[:, :], 1.0, None, ALU.max))
                    link(dve.reciprocal(inv_deg[:, :], inv_deg[:, :]))
                    dve.sem_inc(maps_ready, 1)
                elif L.n == 1:
                    dve.wait_ge(L.logs, 1)
                    link(dve.tensor_scalar(att[:, :], amp[:, :], 1e-12, None, ALU.max))
                    link(dve.reciprocal(att[:, :], att[:, :]))
                    dve.tensor_scalar(att[:, :], att[:, :], AVG_D_LOG, None, ALU.mult)
                    link(dve.tensor_scalar(amp[:, :], amp[:, :], 1.0 / AVG_D_LOG, None, ALU.mult))
                    dve.sem_inc(L.scaled, 1)

                    def moments_dve(turn, q, _, L=L):
                        step = step_no(turn, q)
                        dve.wait_ge(L.t1, step + 1)
                        dve.tensor_tensor(moments[:, q, :, :], ps_a[:, 0:GRP * P].rearrange("p (t c) -> p t c", t=GRP),
                                          wide(ranks_of(inv_deg, turn, q), P), ALU.mult).then_inc(L.scaled, 1)
                        dve.wait_ge(L.sq, step + 1)
                        dve.tensor_tensor(moments[:, q, :, D:P], moments[:, q, :, D:P], meansq[:, q, :, :], ALU.subtract) \
                            .then_inc(L.row_step, 1)
                        dve.wait_ge(L.row_step, 4 * step + 1)
                        dve.tensor_scalar(moments[:, q, :, D:P], moments[:, q, :, D:P], 0.0, None, ALU.max) \
                            .then_inc(L.var_r, 1)
                        z = ps_b[:, :].rearrange("p (t c) -> p t c", t=GRP)
                        dve.wait_ge(L.rows_out, 1 + step + 1)
                        for n, scaler in ((1, amp), (2, att)):
                            dve.tensor_tensor(ztmp, z[:, :, n * D:(n + 1) * D], wide(ranks_of(scaler, turn, q), D),
                                              ALU.mult).then_inc(L.row_step, 1)
                            dve.wait_ge(L.row_step, 4 * step + 2 * n)
                            to = zbase[:, q, :, :] if n == 1 else L.rows[:, q, :, 0:D]
                            ins = dve.tensor_tensor(to, zbase[:, q, :, :], ztmp, ALU.add)
                            if n == 1:
                                ins.then_inc(L.row_step, 1)
                                dve.wait_ge(L.row_step, 4 * step + 3)
                        ins.then_inc(L.rows_set, 1)

                    pipeline(dve, GTURNS, [(0, stage), (1, moments_dve)])
                elif L.n == 2:
                    dve.sem_inc(L.rows_out, 1)
                    dve.sem_inc(L.dense_out, 1)
                    dve.sem_inc(L.xw_dve, 2)
                    pipeline(dve, GTURNS, [(0, rows_out), (3, center), (4, scale), (3, variance), (5, xw_out)])
                else:
                    dve.sem_inc(L.rows_out, 1)
                    pipeline(dve, GTURNS, [(0, rows_out), (3, center), (4, scale), (3, variance)])

                if L.n == 1:
                    for agg_q in agg_loaded:
                        dve.wait_ge(agg_q, agg_there(L, 1))
                    ps_sum = ps_c[0:EP, 0:SUB * D].rearrange("p (t f) -> p f t", t=SUB)
                    dve.tensor_tensor(n1, n1, along(bias["l1_b"][:, :], NT), ALU.add).then_inc(L.bn_in, 1)
                    dve.wait_ge(L.bn_sum, 1)
                    link(dve.tensor_reduce(bn_mean[:, :], ps_sum, AX.X, ALU.add))
                    link(dve.tensor_scalar(bn_mean[:, :], bn_mean[:, :], 1.0 / N, None, ALU.mult))
                    dve.tensor_tensor(n1, n1, along(bn_mean[:, :], NT), ALU.subtract).then_inc(L.bn_cent, 1)
                    dve.wait_ge(L.bn_sum, 2)
                    link(dve.tensor_reduce(bn_scale[:, :], ps_sum, AX.X, ALU.add))
                    dve.tensor_scalar(bn_scale[:, :], bn_scale[:, :], 1.0 / N, None, ALU.mult).then_inc(L.bn_var, 1)
                    dve.wait_ge(L.bn_std, 1)
                    link(dve.reciprocal(bn_scale[:, :], bn_scale[:, :]))
                    link(dve.tensor_tensor(bn_scale[:, :], bn_scale[:, :], bias["l1_gamma"][:, :], ALU.mult))
                    link(dve.tensor_tensor(n1, n1, along(bn_scale[:, :], NT), ALU.mult))
                    dve.tensor_tensor(n1, n1, along(bias["l1_beta"][:, :], NT), ALU.add).then_inc(L.bn_affine, 1)
                    dve.wait_ge(L.bn_relu, 1)
                    link(dve.scalar_tensor_tensor(out=n1, in0=xres[:, :, :], scalar=2.0, in1=n1, op0=ALU.mult, op1=ALU.add))
                    link(dve.tensor_reduce(ln_mean[:, :], n1, AX.X, ALU.add))
                    link(dve.tensor_scalar(ln_mean[:, :], ln_mean[:, :], 1.0 / D, None, ALU.mult))
                    dve.tensor_tensor(n1, n1, wide(ln_mean[:, :], D), ALU.subtract).then_inc(centered, GROUPS)
                    dve.wait_ge(squared, 2 * GROUPS)
                    dve.tensor_reduce(ln_var[:, :], n2, AX.X, ALU.add).then_inc(var, GROUPS)
                    dve.wait_ge(std, 2 * GROUPS)
                    link(dve.reciprocal(ln_var[:, :], ln_var[:, :]))
                    dve.wait_ge(table_ready, 16 * GROUPS)
                    for q in range(SLOTS):
                        part = slice(q * (NT // SLOTS), (q + 1) * (NT // SLOTS))
                        dve.tensor_tensor(xres[:, part, :], n1[:, part, :], wide(ln_var[:, part], D), ALU.mult) \
                            .then_inc(x_ready, GTURNS)


def kernel(**inputs):
    import numpy as np
    import concourse.bacc as bacc
    from concourse.bass_utils import run_bass_kernel_spmd

    def turned(a):
        a = np.asarray(a)
        a = a.reshape(BLOCKS, P, -1).transpose(1, 0, 2)
        return np.ascontiguousarray(a).reshape(P, -1)

    def arr(name, *shape):
        a = np.asarray(inputs[name])
        return np.ascontiguousarray(a.reshape(shape) if shape else a)

    arrays = {
        "x_in": arr("x"),
        "src_e": turned(inputs["src"]),
        "etype_e": turned(inputs["edge_type_8"]),
        "weight_e": turned(inputs["edge_weight"]),
        "dst_n": arr("dst", EP, EW),
        "edge_attr": turned(inputs["edge_attr_64"]),
        "eps_in": arr("L0_gnn_eps", 1, 1),
        "we": arr("L0_gnn_We_w"),
        "we_b": arr("L0_gnn_We_b", 1, D),
        "w1": arr("L0_gnn_W1"),
        "b1": arr("L0_gnn_b1", H, 1),
        "w2": arr("L0_gnn_W2"),
        "b2": arr("L0_gnn_b2", 1, D),
        "l1_w": arr("L1_gnn_W"),
        "l1_b": arr("L1_gnn_b", 1, D),
        "l1_gamma": arr("L1_gnn_gamma", 1, D),
        "l1_beta": arr("L1_gnn_beta", 1, D),
        "wl_t": np.ascontiguousarray(np.asarray(inputs["L2_gnn_w_l"]).T),
        "wr_t": np.ascontiguousarray(np.asarray(inputs["L2_gnn_w_r"]).T),
        "l2_b": arr("L2_gnn_b", 1, D),
        "l3_w": arr("L3_gnn_W"),
    }
    nc = bacc.Bacc("TRN2", target_bir_lowering=False, num_devices=1)
    args = [nc.dram_tensor(n, a.shape, mybir.dt.from_np(a.dtype), kind="ExternalInput").ap() for n, a in arrays.items()]
    out = nc.dram_tensor("out", (N, D), F32, kind="ExternalOutput").ap()
    gnn_kernel(nc, *args, out)
    return run_bass_kernel_spmd(nc, [arrays], core_ids=[0]).results[0]["out"]
```

```python
import concourse.bass as bass
from concourse import mybir
from contextlib import ExitStack

F32 = mybir.dt.float32
I32 = mybir.dt.int32
BF16 = mybir.dt.bfloat16
ALU = mybir.AluOpType
ACT = mybir.ActivationFunctionType
AX = mybir.AxisListType

P = 128
E = 400000
N = 12500
D = 64
H = 128
RELS = 8
BLOCKS = E // P
SUB = 5
SLOTS = 5
SUBS = BLOCKS // SUB
TURNS = SUBS // SLOTS
EP = 125
EW = E // EP
EB = EW // P
NT = N // EP
NW = NT * D
GRP = 4
GROUPS = NT // GRP
GTURNS = GROUPS // SLOTS
PART = NT // SLOTS
RT = GROUPS * GRP
RANKS = RT * P
assert BLOCKS * P == E and TURNS * SLOTS * SUB == BLOCKS and EP * EW == E and EB * P == EW
assert GROUPS * GRP == NT and GTURNS * SLOTS == GROUPS and RANKS >= N + P

AVG_D_LOG = 2.833
EPS = 1e-5
RESTART = -1e30

F_REL, F_END, F_DST = 0, 5, 10
FIELDS = 15

XS_COLS = 192
L0_ROWS = 66
DEG, DST = 64, 65


def pipeline(eng, turns, stages, parts=1, start=0):
    for q in range(SLOTS):
        for part in range(parts):
            for lag, fn in stages:
                if q >= lag:
                    fn(start, q - lag, part)
    with eng.Fori(start + 1, turns) as turn:
        for q in range(SLOTS):
            for part in range(parts):
                for lag, fn in stages:
                    if q >= lag:
                        fn(turn, q - lag, part)
                    else:
                        fn(turn - 1, q - lag + SLOTS, part)
    for q in range(max(lag for lag, _ in stages)):
        for part in range(parts):
            for lag, fn in stages:
                if q < lag:
                    fn(turns - 1, q - lag + SLOTS, part)


def first(turn):
    return isinstance(turn, int) and turn == 0


def is_last(turn, q):
    return isinstance(turn, int) and turn == GTURNS - 1 and q == SLOTS - 1


def gnn_kernel(nc, x_in, src_e, etype_e, weight_e, dst_n, edge_attr, eps_in, we, we_b, w1, b1, w2, b2,
               l1_w, l1_b, l1_gamma, l1_beta, wl_t, wr_t, l2_b, l3_w, out):
    with ExitStack() as ctx:
        def sb(name, shape, dt=F32):
            return ctx.enter_context(nc.sbuf_tensor(name, shape, dt))

        def psum(name, cols):
            return ctx.enter_context(nc.psum_tensor(name, [P, cols], F32))

        def sem(name):
            return ctx.enter_context(nc.semaphore(name))

        tables = [x_in] + [nc.dram_tensor(f"x{n}_table", [N, D], F32).ap() for n in (1, 2)]
        xw_table = nc.dram_tensor("xw_table", [N * RELS, D], F32).ap()
        agg = [nc.dram_tensor(f"agg{n}", [N, D], F32).ap() for n in range(4)]
        meta_d = nc.dram_tensor("meta_d", [P, SUBS * FIELDS], F32).ap()
        xw_rows_d = nc.dram_tensor("xw_rows_d", [P, BLOCKS], I32).ap()
        window_d = nc.dram_tensor("window_d", [BLOCKS], I32).ap()
        restart_d = nc.dram_tensor("restart_d", [E], BF16).ap()
        inv_d = nc.dram_tensor("inv_d", [RANKS], F32).ap()

        ZP = N // TURNS // GRP
        acc = sb("acc", [P, 2, RANKS])
        META_CHUNK = SUBS * FIELDS // SLOTS
        meta_flat = acc[:, 0, 0:SUBS * FIELDS]
        meta_all = meta_flat.rearrange("p (s f) -> p s f", f=FIELDS)
        src_all = acc[:, 1, 0:BLOCKS].bitcast(I32)
        etype_all = acc[:, 1, BLOCKS:2 * BLOCKS].bitcast(I32)
        xres = sb("xres", [EP, NT, D])
        WORK = 14400
        work = sb("work", [P, WORK])
        meta = sb("meta", [P, SLOTS, FIELDS])
        index = sb("index", [P, SLOTS, SUB], I32)
        weight = sb("weight", [P, SLOTS, SUB])
        window = sb("window", [1, SLOTS, SUB], I32)
        restart = sb("restart", [P, SLOTS, SUB * P], BF16)

        def carve(at, *dims, parts=P):
            size = 1
            for d in dims:
                size *= d
            assert at + size <= WORK
            v = work[0:parts, at:at + size]
            if len(dims) > 1:
                names = " ".join(f"d{i}" for i in range(len(dims)))
                v = v.rearrange(f"p ({names}) -> p {names}", **{f"d{i}": d for i, d in enumerate(dims)})
            return v, at + size

        xs, at = carve(0, SLOTS, SUB, XS_COLS)
        onehot, at = carve(at, SLOTS, SUB, P)
        edge_end = at
        scanned, at = carve(at, SLOTS, SUB * P)
        turned, at = carve(at, SLOTS, SUB, P)
        n1, n2_at = carve(0, NT, D, parts=EP)
        n2, _ = carve(n2_at, NT, D, parts=EP)
        n1_groups = n1.rearrange("p (g t) f -> p g (t f)", t=GRP)
        RING = 3
        inv_wide, at = carve(n2_at, SLOTS, GRP * P)
        moments, at = carve(at, RING, GRP * P)
        extremes, at = carve(at, RING, GRP * P)
        rows1, at = carve(at, SLOTS, GRP, D)
        z_part, at = carve(at, GRP, D)
        meansq = restart[:, :, :].rearrange("p s e -> p (s e)").bitcast(F32)[:, 0:RING * GRP * P] \
            .rearrange("p (s e) -> p s e", s=RING)
        dst_i = work[0:EP, 0:EW].bitcast(I32)
        starts = work[0:EP, EW:2 * EW]
        rel = work[0:EP, 2 * EW:3 * EW]
        inside = work[0:EP, 3 * EW:4 * EW]
        restart_row = work[0:EP, 3 * EW:3 * EW + EW // 2].bitcast(BF16)
        xres_flat = xres[:, :, :].rearrange("p t f -> p (t f)")
        xres_groups = xres_flat.rearrange("p (g f) -> p g f", g=GROUPS)
        ends = xres_flat[:, 0:EW]
        dst_first = xres_flat[:, EW:2 * EW]

        ident = sb("ident", [P, P])
        iota_i = sb("iota_i", [P, P], I32)
        iota = sb("iota", [P, P])
        ones = sb("ones", [P, P])
        before = sb("before", [P, P])
        zeros = sb("zeros", [ZP, GRP * D])
        dst_left = sb("dst_left", [EP, 1], I32)
        dst_right = sb("dst_right", [EP, 1], I32)
        blk_total = sb("blk_total", [EP, EB])
        blk_cum = sb("blk_cum", [EP, EB])
        blk_first = sb("blk_first", [EP, EB])
        blk_window = sb("blk_window", [EP, EB], I32)
        map_x = sb("map_x", [L0_ROWS, L0_ROWS])
        map_ea = sb("map_ea", [L0_ROWS, L0_ROWS])
        w1_sb = sb("w1_sb", [D, H])
        b1_sb = sb("b1_sb", [H, 1])
        w2_sb = sb("w2_sb", [H, D])
        w_moments = sb("w_moments", [P, 3, D])
        w_extremes = sb("w_extremes", [P, 3, D])
        wl_sb = sb("wl_sb", [D, D])
        wr_sb = sb("wr_sb", [D, D])
        w3_sb = sb("w3_sb", [D, RELS, D])
        bias = {n: sb(f"{n}_sb", [EP, D]) for n in ("b2", "l1_b", "l1_gamma", "l1_beta", "l2_b")}
        eps1 = sb("eps1", [EP, 1])
        eps_sb = sb("eps_sb", [P, 1])
        deg = sb("deg", [P, RT])
        inv_deg = sb("inv_deg", [P, RT])
        inv_row = sb("inv_row", [RT, P])
        amp = sb("amp", [P, RT])
        att = sb("att", [P, RT])
        node_all = sb("node_all", [P, RT], I32)
        node_of = sb("node_of", [P, SLOTS, GRP], I32)
        no_rank = sb("no_rank", [P, GRP])
        ln_mean = sb("ln_mean", [EP, NT])
        ln_var = sb("ln_var", [EP, NT])
        bn_mean = sb("bn_mean", [EP, D])
        bn_scale = sb("bn_scale", [EP, D])

        BANK = 512
        ps_a = psum("ps_a", 2 * BANK)
        ps_b = psum("ps_b", 2 * BANK)
        ps_o = psum("ps_o", 4 * BANK)
        ps_rank, ps_turn = ps_a[:, 0:BANK], ps_a[:, BANK:2 * BANK]
        ps_mid, ps_dense = ps_b[:, 0:BANK], ps_b[:, BANK:2 * BANK]
        ps_c = ps_o[:, 3 * BANK:4 * BANK]
        z_banks = (ps_a, ps_b, ps_o[:, 0:2 * BANK])
        O_BANKS = SUB - 1
        sums = [ps_o[:, (k % O_BANKS) * BANK + (k // O_BANKS) * 2 * P:][:, 0:2 * P].rearrange("p (a c) -> p a c", a=2)
                for k in range(SUB)]

        edge_init = sem("edge_init")
        ld_edges = sem("ld_edges")
        ld_dst = sem("ld_dst")
        ld_const = sem("ld_const")
        consts = sem("consts")
        maps_init = sem("maps_init")
        xw_numbered = sem("xw_numbered")
        xw_rows_stored = sem("xw_rows_stored")
        fields_ready = sem("fields_ready")
        fields_turned = sem("fields_turned")
        fields_placed = sem("fields_placed")
        cum_ready = sem("cum_ready")
        base_ready = sem("base_ready")
        window_ready = sem("window_ready")
        window_stored = sem("window_stored")
        restart_ready = sem("restart_ready")
        restart_stored = sem("restart_stored")
        meta_stored = [sem(f"meta_stored{c}") for c in range(SLOTS)]
        agg_zeroed = sem("agg_zeroed")
        maps_ready = sem("maps_ready")
        dve_step = sem("dve_step")
        x_loaded = sem("x_loaded")

        meta_loaded = [sem(f"meta_loaded{q}") for q in range(SLOTS)]
        aux_loaded = [sem(f"aux_loaded{q}") for q in range(SLOTS)]
        gathered = [sem(f"gathered{q}") for q in range(SLOTS)]
        scattered = [sem(f"scattered{q}") for q in range(SLOTS)]
        agg_loaded = [sem(f"agg_loaded{q}") for q in range(SLOTS)]
        xw_stored = [sem(f"xw_stored{q}") for q in range(SLOTS)]

        pool_past = sem("pool_past")
        pe_past = sem("pe_past")
        act_past = sem("act_past")
        sp_past = sem("sp_past")
        acc_zero = sem("acc_zero")
        table_ready = sem("table_ready")
        centered = sem("centered")
        squared = sem("squared")
        var = sem("var")
        std = sem("std")
        x_ready = sem("x_ready")

        class Layer:
            pass

        layers = []
        for n in range(4):
            L = Layer()
            L.n = n

            def ls(name, n=n):
                return sem(f"l{n}_{name}")

            L.prep = ls("prep")
            L.onehot = ls("onehot")
            L.summed = ls("summed")
            L.added = ls("added")
            L.staged = ls("staged")
            L.rows_mm = ls("rows_mm")
            L.rows_out = ls("rows_out")
            if n == 0:
                L.rows_set = ls("rows_set")
            if n != 1:
                L.ln_in = ls("ln_in")
                L.ln_scale = ls("ln_scale")
            if n == 0 or n == 2:
                L.hs = ls("hs")
                L.htp = ls("htp")
                L.hts = ls("hts")
                L.dense = ls("dense")
                L.dense_out = ls("dense_out")
            if n == 0:
                L.number = ls("number")
                L.u = ls("u")
                L.relu = ls("relu")
            if n == 1:
                L.tx = ls("tx")
                L.scan = ls("scan")
                L.tb = ls("tb")
                L.ts = ls("ts")
                L.inv_turned = ls("inv_turned")
                L.inv_copied = ls("inv_copied")
                L.inv_stored = ls("inv_stored")
                L.logs = ls("logs")
                L.scalers = ls("scalers")
                L.means = ls("means")
                L.sq = ls("sq")
                L.var_step = ls("var_step")
                L.var_r = ls("var_r")
                L.std_r = ls("std_r")
                L.z_part = ls("z_part")
                L.bn_in = ls("bn_in")
                L.bn_sum = ls("bn_sum")
                L.bn_cent = ls("bn_cent")
                L.bn_sq = ls("bn_sq")
                L.bn_var = ls("bn_var")
                L.bn_std = ls("bn_std")
                L.bn_scaled = ls("bn_scaled")
                L.bn_affine = ls("bn_affine")
            if n == 2:
                L.xw_htp = ls("xw_htp")
                L.xw_hts = ls("xw_hts")
                L.xw_mm = ls("xw_mm")
                L.xw_act = ls("xw_act")
                L.xw_dve = ls("xw_dve")
            if n != 1:
                L.rstage, at = carve(0, SLOTS, 2 if n == 0 else 1, GRP * P)
                L.rows, at = carve(at, SLOTS, GRP, L0_ROWS if n == 0 else D)
                L.nodes, at = carve(at, SLOTS, GRP, D, parts=EP)
                if n == 0:
                    L.h_in, at = carve(at, SLOTS, GRP, D, parts=EP)
                    L.ht, at = carve(at, SLOTS, GRP * EP, parts=D)
                    L.h1, at = carve(at, SLOTS, GRP * EP, parts=H)
                    L.square = restart[0:EP, :, :].rearrange("p s e -> p (s e)").bitcast(F32)[:, 0:SLOTS * GRP * D] \
                        .rearrange("p (s t f) -> p s t f", s=SLOTS, t=GRP)
                else:
                    L.square, at = carve(at, SLOTS, GRP, D, parts=EP)
                if n == 2:
                    L.x_out, at = carve(at, SLOTS, GRP, D, parts=EP)
                    L.xt, at = carve(at, SLOTS, GRP * EP, parts=D)
                    L.h_in, at = carve(max(at, edge_end), GRP, D, parts=EP)
                    L.ht, at = carve(at, GRP * EP, parts=D)
                    L.xw = acc[0:EP, 1, 0:SLOTS * GRP * RELS * D].rearrange("p (s t f) -> p s t f", s=SLOTS, t=GRP)
            else:
                L.rows = rows1
            layers.append(L)
        out_stored = sem("out_stored")
        CREDIT = SLOTS * SUB
        XW_CREDIT = SLOTS * GRP

        def block_no(turn, q, k):
            return turn * (SLOTS * SUB) + (q * SUB + k)

        def step_no(turn, q):
            return turn * SLOTS + q

        def loaded(L, turn, each=1):
            return turn * (each * 16) + (L.n * TURNS + 1) * each * 16

        def meta_there(L, turn):
            return loaded(L, turn, 3)

        def aux_there(L, turn):
            before = {0: 0, 1: TURNS, 3: 2 * TURNS + GTURNS}[L.n]
            return turn * 16 + (before + 1) * 16

        def rows_landed(L, turns):
            return turns * (GRP * 16) + L.n * GTURNS * GRP * 16

        def agg_there(L, turns):
            return turns * 16 + L.n * GTURNS * 16

        def inv_there(turn):
            return turn * 16 + (2 * TURNS + 1) * 16

        def ln_no(L, turn, q):
            return step_no(turn, q) + (L.n * GROUPS + 1)

        def node_view(table):
            return table.rearrange("(g p t) f -> p g (t f)", p=EP, t=GRP)

        def group_of(view, turn, q):
            return view[:, bass.ds(turn if q is None else step_no(turn, q), 1), :].rearrange("p g f -> p (g f)")

        def flat(tiles):
            return tiles.rearrange("p t f -> p (t f)")

        def wide(ap, width):
            return ap.unsqueeze(2).to_broadcast([ap.shape[0], ap.shape[1], width])

        def along(ap, tiles):
            return ap.unsqueeze(1).to_broadcast([ap.shape[0], tiles, ap.shape[1]])

        def tiles_of(array, turn, q):
            return array[:, bass.ds(step_no(turn, q) * GRP, GRP), :]

        def ranks_of(array, turn, q):
            return array[:, bass.ds(step_no(turn, q) * GRP, GRP)]

        block = ctx.enter_context(nc.Block())

        @block.sync
        def _(sp):
            sp.dma_start(dst_i, dst_n).then_inc(ld_dst, 16)
            sp.wait_ge(edge_init, 1)
            sp.dma_start(dst_left[1:EP, :], dst_n[0:EP - 1, EW - 1:EW], allow_slow_non_contiguous=True).then_inc(ld_dst, 16)
            sp.dma_start(dst_right[0:EP - 1, :], dst_n[1:EP, 0:1], allow_slow_non_contiguous=True).then_inc(ld_dst, 16)
            sp.dma_start(src_all, src_e).then_inc(ld_edges, 16)
            sp.dma_start(etype_all, etype_e).then_inc(ld_edges, 16)
            sp.wait_ge(maps_init, 1)
            for dst, source in (
                (map_x[DEG:DEG + 1, 0:D], we_b), (map_ea[0:D, 0:D], we), (w1_sb[:, :], w1),
                (b1_sb[:, :], b1), (w2_sb[:, :], w2), (wl_sb[:, :], wl_t), (wr_sb[:, :], wr_t),
                (w3_sb[:, :, :], l3_w.rearrange("r f o -> f r o")),
                (eps1[:, :], eps_in.to_broadcast([EP, 1])),
            ):
                sp.dma_start(dst, source, allow_slow_non_contiguous=True).then_inc(ld_const, 16)
            w_parts = l1_w.rearrange("(g s f) o -> s f g o", g=3, s=4)
            for dst, part in ((w_moments[0:D], 0), (w_extremes[D:P], 1), (w_extremes[0:D], 2), (w_moments[D:P], 3)):
                sp.dma_start(dst, w_parts[part]).then_inc(ld_const, 16)
            for name, source in (("b2", b2), ("l1_b", l1_b), ("l1_gamma", l1_gamma), ("l1_beta", l1_beta), ("l2_b", l2_b)):
                sp.dma_start(bias[name][:, :], source.to_broadcast([EP, D])).then_inc(ld_const, 16)

            sp.wait_ge(restart_ready, 1)
            sp.dma_start(restart_d.rearrange("(p e) -> p e", p=EP), restart_row).then_inc(restart_stored, 16)
            sp.wait_ge(window_ready, 1)
            sp.dma_start(window_d.rearrange("(p b) -> p b", p=EP), blk_window[:, :]).then_inc(window_stored, 16)
            sp.wait_ge(fields_placed, 3 * SUB)

            def store_meta(c):
                part = slice(c * META_CHUNK, (c + 1) * META_CHUNK)
                sp.dma_start(meta_d[:, part], meta_flat[:, part]).then_inc(meta_stored[c], 16)

            store_meta(0)
            sp.wait_ge(window_stored, 16)
            sp.wait_ge(meta_stored[0], 16)
            sp.wait_ge(consts, 6)

            meta_v = meta_d.rearrange("p (s f) -> p s f", f=FIELDS)
            ea_v = edge_attr.rearrange("p (b f) -> p b f", f=D)

            for L in layers:
                if L.n == 1:
                    sp.wait_ge(L.inv_copied, 1)
                    sp.dma_start(inv_d.rearrange("(t p) -> t p", p=P), inv_row[:, :]).then_inc(L.inv_stored, 16)

                def load_slot(turn, q, _, L=L):
                    sp.wait_ge(L.added, block_no(turn, q, SUB))
                    s = step_no(turn, q)
                    rows = xw_rows_d if L.n == 3 else src_e
                    sp.dma_start(index[:, q, :], rows[:, bass.ds(s * SUB, SUB)]).then_inc(meta_loaded[q], 16)
                    sp.dma_start(meta[:, q, :], meta_v[:, bass.ds(s, 1), :].rearrange("p s f -> p (s f)")) \
                        .then_inc(meta_loaded[q], 16)
                    sp.dma_start(window[:, q, :], window_d.unsqueeze(0)[:, bass.ds(s * SUB, SUB)]) \
                        .then_inc(meta_loaded[q], 16)
                    if L.n == 3:
                        sp.dma_start(weight[:, q, :], weight_e[:, bass.ds(s * SUB, SUB)]).then_inc(aux_loaded[q], 16)
                    if L.n == 0:
                        sp.dma_start(xs[:, q, :, L0_ROWS:L0_ROWS + D], ea_v[:, bass.ds(s * SUB, SUB), :]) \
                            .then_inc(aux_loaded[q], 16)
                    if L.n == 1:
                        sp.dma_start(restart[:, q, :], restart_d.unsqueeze(0)[:, bass.ds(s * (SUB * P), SUB * P)]
                                     .to_broadcast([P, SUB * P])).then_inc(aux_loaded[q], 16)

                    if L.n == 0 and first(turn) and q == SLOTS - 1:
                        for c in range(1, SLOTS):
                            store_meta(c)
                        sp.wait_ge(xw_numbered, 1)
                        sp.dma_start(xw_rows_d, src_all).then_inc(xw_rows_stored, 16)
                    if q == SLOTS - 1:
                        zeroed = agg[L.n].rearrange("(u p t) f -> p u (t f)", p=ZP, t=GRP)[:, bass.ds(turn, 1), :]
                        sp.dma_start(zeroed.rearrange("p u f -> p (u f)"), zeros[:, :]).then_inc(agg_zeroed, 16)

                def load_x(g, q, _):
                    if q == 1:
                        sp.dma_start(group_of(xres_groups, g, None), group_of(node_view(x_in), g, None)).then_inc(x_loaded, 16)

                if L.n == 0:
                    sp.wait_ge(L.prep, 1)
                    pipeline(sp, GROUPS, [(0, load_slot), (0, load_x)])
                    pipeline(sp, TURNS, [(0, load_slot)], start=GROUPS)
                else:
                    pipeline(sp, TURNS, [(0, load_slot)])

                agg_v = node_view(agg[L.n])
                def load_sums(turn, q, _, L=L, agg_v=agg_v):
                    sp.wait_ge(scattered[q], rows_landed(L, turn + 1))
                    sp.sem_inc(sp_past, 1)
                    if L.n != 1 and not first(turn):
                        sp.wait_ge(x_ready, ln_no(L, turn, q) - SLOTS)
                    to = group_of(n1_groups, turn, q) if L.n == 1 else flat(L.nodes[:, q])
                    sp.dma_start(to, group_of(agg_v, turn, q)).then_inc(agg_loaded[q], 16)

                def load_inv(turn, q, _, L=L):
                    step = step_no(turn, q)
                    sp.wait_ge(L.means, step + 1)
                    sp.dma_start(inv_wide[:, q, :], inv_d.unsqueeze(0)[:, bass.ds(step * (GRP * P), GRP * P)]
                                 .to_broadcast([P, GRP * P])).then_inc(aux_loaded[q], 16)

                def store_x(turn, q, _, L=L):
                    sp.wait_ge(x_ready, ln_no(L, turn, q))
                    to = out if L.n == 3 else tables[L.n + 1]
                    sp.dma_start(group_of(node_view(to), turn, q), group_of(xres_groups, turn, q)) \
                        .then_inc(out_stored if L.n == 3 else table_ready, 16)

                xw_v = xw_table.rearrange("(g p t r) f -> p g (t r f)", p=EP, t=GRP, r=RELS)

                def store_xw(turn, q, _, L=L, xw_v=xw_v):
                    step = step_no(turn, q)
                    sp.wait_ge(L.xw_act, 2 + 2 * step + 2)
                    sp.wait_ge(L.xw_dve, 2 + 2 * step + 2)
                    sp.dma_start(group_of(xw_v, turn, q), flat(L.xw[:, q])).then_inc(xw_stored[q], 16)

                if L.n == 1:
                    sp.wait_ge(L.inv_stored, 16)
                    sp.wait_ge(L.added, CREDIT + BLOCKS)
                    pipeline(sp, GTURNS, [(0, load_inv), (5, load_sums)])
                    for q in range(SLOTS):
                        part = slice(q * GTURNS, (q + 1) * GTURNS)
                        sp.wait_ge(x_ready, GROUPS + (q + 1) * GTURNS)
                        sp.dma_start(node_view(tables[2])[:, part, :], xres_groups[:, part, :]).then_inc(table_ready, 16)
                elif L.n == 2:
                    pipeline(sp, GTURNS, [(0, load_sums), (5, store_xw)])
                else:
                    pipeline(sp, GTURNS, [(5 if L.n == 0 else 4, store_x), (0, load_sums)])
            sp.wait_ge(out_stored, 16 * GROUPS)

        @block.gpsimd
        def _(pool):
            pool.memset(ones[:, :], 1.0).then_inc(consts, 1)
            pool.memset(zeros[:, :], 0.0).then_inc(consts, 1)
            pool.memset(ident[:, :], 0.0).then_inc(consts, 1)
            pool.iota(iota_i[:, :], pattern=[[1, P]], base=0, channel_multiplier=0).then_inc(consts, 1)
            pool.wait_ge(consts, 4)
            pool.affine_select(out=ident[:, :], in_=ident[:, :], compare_op=ALU.not_equal, fill=1.0, base=0,
                               pattern=[[-1, P]], channel_multiplier=1).then_inc(consts, 1)
            pool.affine_select(out=before[:, :], in_=ones[:, :], compare_op=ALU.is_gt, fill=0.0, base=0,
                               pattern=[[1, P]], channel_multiplier=-1).then_inc(consts, 1)

            pool.memset(acc[:, 0, SUBS * FIELDS:], 0.0)
            pool.memset(acc[:, 1, 2 * BLOCKS:], 0.0).then_inc(acc_zero, 1)

            for L in layers:
                if L.n > 0:
                    pool.wait_ge(layers[L.n - 1].staged, GROUPS)
                    if L.n == 2:
                        pool.wait_ge(layers[1].means, SLOTS + GROUPS)
                    for a in range(2 if L.n < 2 else 1):
                        z = pool.memset(acc[:, a, :], 0.0)
                    z.then_inc(acc_zero, 1)

                if L.n == 3:
                    for xw_q in xw_stored:
                        pool.wait_ge(xw_q, GTURNS * 16)
                elif L.n > 0:
                    pool.wait_ge(table_ready, 16 * (GROUPS if L.n == 1 else GROUPS + SLOTS))
                table = xw_table if L.n == 3 else tables[L.n]
                col = D if L.n == 1 else 0

                def gather(turn, q, k, L=L, table=table, col=col):
                    if k == 0:
                        pool.wait_ge(meta_loaded[q], meta_there(L, turn))
                        pool.sem_inc(pool_past, 1)
                    pool.indirect_dma_start(
                        out=xs[:, q, k, col:col + D], out_offset=None, in_=table,
                        in_offset=bass.IndirectOffsetOnAxis(ap=index[:, q, k:k + 1], axis=0),
                    ).then_inc(gathered[q], 16)

                pipeline(pool, TURNS, [(0, gather)], parts=SUB)

                def scatter(turn, q, t, L=L):
                    if t == 0:
                        pool.wait_ge(L.rows_out if L.n else L.rows_set, step_no(turn, q) + (1, 3, 2, 2)[L.n])
                        pool.sem_inc(pool_past, 1)
                    pool.indirect_dma_start(
                        out=agg[L.n], out_offset=bass.IndirectOffsetOnAxis(ap=node_of[:, q, t:t + 1], axis=0),
                        in_=L.rows[:, q, t, 0:D], in_offset=None, bounds_check=N - 1, oob_is_err=False,
                    ).then_inc(scattered[q], 16)

                pool.wait_ge(agg_zeroed, 16 * TURNS * (L.n + 1))
                pipeline(pool, GTURNS, [(0, scatter)], parts=GRP)

                if L.n == 1:
                    for c in range(SLOTS):
                        pool.wait_ge(L.bn_scaled, c + 1)
                        v = n1[:, c * PART:(c + 1) * PART, :]
                        pool.tensor_tensor(v, v, along(bias["l1_beta"][:, :], PART), ALU.add).then_inc(L.bn_affine, 1)

        @block.scalar
        def _(act):
            act.wait_ge(maps_ready, 1)
            for n, field in enumerate((F_END, F_DST, F_REL)):
                for gd in range(EB // SUB):
                    turned_no = n * SUB + gd
                    act.wait_ge(fields_turned, turned_no + 1)
                    ps = (ps_a, ps_b, ps_o)[turned_no % 3][:, 0:SUB * P].rearrange("p (k c) -> p c k", k=SUB)
                    dst = meta_all.rearrange("p (c g) f -> p c g f", g=EB // SUB)[:, :, gd, field:field + SUB]
                    act.activation(dst, ps[:, 0:EP, :], ACT.Copy).then_inc(fields_placed, 1)

            for L in layers:
                if L.n == 0:
                    def prep(turn, q, _, L=L):
                        act.wait_ge(meta_loaded[q], meta_there(L, turn))
                        act.wait_ge(L.summed, block_no(turn, q, SUB))
                        act.activation(xs[:, q, :, DST], meta[:, q, F_DST:F_DST + SUB], ACT.Copy) \
                            .then_inc(L.prep, 1)

                    act.wait_ge(L.prep, 1)
                    pipeline(act, TURNS, [(0, prep)])
                if L.n == 1:
                    act.wait_ge(L.inv_turned, 1)
                    act.activation(inv_row[:, :], ps_c[0:RT, 0:P], ACT.Copy).then_inc(L.inv_copied, 1)
                    act.wait_ge(maps_ready, 2)
                    act.activation(amp[:, :], deg[:, :], ACT.Ln, bias=1.0).then_inc(L.logs, 1)

                    def prep1(turn, q, k, L=L):
                        if k == 0:
                            act.wait_ge(gathered[q], loaded(L, turn, SUB))
                            act.activation(xs[:, q, :, 0:D], xs[:, q, :, D:2 * D], ACT.Copy, scale=-1.0)
                            act.activation(xs[:, q, :, 2 * D:3 * D], xs[:, q, :, D:2 * D], ACT.Square).then_inc(L.prep, 1)

                    def last_edges(turn, q, k, L=L):
                        if k == 0:
                            act.wait_ge(L.tb, SLOTS + step_no(turn, q) + 1)
                            act.wait_ge(L.summed, block_no(turn, q, SUB))
                        ins = act.activation(turned[:, q, k, :], ps_b[:, k * P:(k + 1) * P], ACT.Copy,
                                             scale=meta[:, q, F_END + k:F_END + k + 1])
                        if k == SUB - 1:
                            ins.then_inc(L.ts, 1)

                    act.sem_inc(L.ts, 1)
                    pipeline(act, TURNS, [(0, prep1), (1, last_edges)], parts=SUB)

                if L.n == 2:
                    act.sem_inc(L.hts, 1)
                    act.wait_ge(x_ready, 2 * GROUPS)

                    def own_features(turn, q, _, L=L):
                        g = step_no(turn, q)
                        act.wait_ge(L.htp, g + 1)
                        act.sem_inc(act_past, 1)
                        act.activation(L.h_in, tiles_of(xres, turn, q), ACT.Copy).then_inc(L.hs, 1)
                        act.wait_ge(L.htp, 1 + g + 1)
                        act.wait_ge(L.dense, g + 1)
                        act.activation(L.ht, ps_turn[0:D, 0:GRP * EP], ACT.Copy).then_inc(L.hts, 1)

                    pipeline(act, GTURNS, [(0, own_features)])

                def columns(turn, q, _, L=L):
                    step = step_no(turn, q)
                    n_rows, halves = (L0_ROWS, 2) if L.n == 0 else (D, 1)
                    act.wait_ge(L.rows_mm, step + 1)
                    act.sem_inc(act_past, 1)
                    act.activation(L.rstage[0:n_rows, q], acc[0:n_rows, 0:halves, bass.ds(step * (GRP * P), GRP * P)],
                                   ACT.Copy).then_inc(L.staged, 1)

                def rows_out(turn, q, _, L=L):
                    act.wait_ge(L.rows_mm, SLOTS + step_no(turn, q) + 1)
                    if not first(turn):
                        act.wait_ge(scattered[q], rows_landed(L, turn))
                    act.activation(L.rows[:, q], ps_rank.rearrange("p (t c) -> p t c", t=GRP)[:, :, 0:L0_ROWS], ACT.Copy) \
                        .then_inc(L.rows_out, 1)

                def take_turned(turn, q, _, L=L):
                    step = step_no(turn, q)
                    act.wait_ge(L.htp, SLOTS + step + 1)
                    act.wait_ge(L.u, step + 1)
                    act.activation(L.ht[:, q, :], ps_turn[0:D, 0:GRP * EP], ACT.Copy).then_inc(L.hts, 1)

                def hidden(turn, q, _, L=L):
                    step = step_no(turn, q)
                    act.wait_ge(L.u, SLOTS + step + 1)
                    act.wait_ge(L.dense, step + 1)
                    act.activation(L.h1[:, q, :], ps_mid[:, 0:GRP * EP], ACT.Relu, bias=b1_sb[:, 0:1]).then_inc(L.relu, 1)

                def square(turn, q, _, L=L):
                    act.wait_ge(centered, ln_no(L, turn, q))
                    act.activation(L.square[:, q], L.nodes[:, q], ACT.Square).then_inc(squared, 1)

                def deviation(turn, q, _, L=L):
                    act.wait_ge(var, ln_no(L, turn, q))
                    v = ln_var[:, q * GRP:(q + 1) * GRP]
                    act.activation(v, v, ACT.Sqrt, bias=eps_sb[0:EP, 0:1], scale=1.0 / D).then_inc(std, 1)

                def copy_out(turn, q, _, L=L):
                    act.wait_ge(x_ready, ln_no(L, turn, q))
                    act.sem_inc(act_past, 1)
                    act.activation(tiles_of(xres, turn, q), L.x_out[:, q], ACT.Copy)

                def xw_turned(turn, q, _, L=L):
                    step = step_no(turn, q)
                    act.wait_ge(L.xw_htp, SLOTS + step + 1)
                    act.wait_ge(L.xw_mm, GRP * (step + 1))
                    act.activation(L.xt[:, q, :], ps_mid[0:D, 0:GRP * EP], ACT.Copy).then_inc(L.xw_hts, 1)

                def xw_out(turn, q, _, L=L):
                    step = step_no(turn, q)
                    if not first(turn):
                        act.wait_ge(xw_stored[q], turn * 16)
                    for t in (0, 1):
                        act.wait_ge(L.xw_mm, XW_CREDIT + GRP * step + (t + 1))
                        act.activation(L.xw[:, q, t, :], ps_o[0:EP, t * BANK:(t + 1) * BANK], ACT.Copy).then_inc(L.xw_act, 1)

                act.wait_ge(L.added, CREDIT + BLOCKS)
                if L.n == 0:
                    act.sem_inc(L.rows_out, 1)
                    act.sem_inc(L.hts, 1)
                    act.sem_inc(L.relu, 1)
                    act.wait_ge(ld_const, 18 * 16)
                    pipeline(act, GTURNS, [(0, columns), (4, hidden), (5, square), (5, deviation), (0, rows_out),
                                           (3, take_turned)])
                elif L.n == 2:
                    act.sem_inc(L.xw_hts, 1)
                    act.sem_inc(L.xw_act, 2)
                    pipeline(act, GTURNS, [(0, columns), (5, xw_turned), (4, deviation),
                                           (3, square), (4, copy_out), (5, xw_out)])
                elif L.n == 3:
                    pipeline(act, GTURNS, [(0, columns), (4, deviation), (3, square)])
                else:
                    def extremes_in(turn, q, _, L=L):
                        step = step_no(turn, q)
                        act.wait_ge(L.rows_mm, step + SLOTS - 1)
                        act.sem_inc(act_past, 1)
                        act.activation(extremes[:, q % RING, :], acc[:, 1, bass.ds(step * (GRP * P), GRP * P)], ACT.Copy) \
                            .then_inc(L.staged, 1)

                    def double(turn, q, _, L=L):
                        x = tiles_of(xres, turn, q)
                        act.activation(x, x, ACT.Copy, scale=2.0)

                    def square_means(turn, q, _, L=L):
                        act.wait_ge(L.means, SLOTS + step_no(turn, q) + 1)
                        act.activation(meansq[D:P, q % RING, :], moments[0:D, q % RING, :], ACT.Square).then_inc(L.sq, 1)

                    def deviations(turn, q, _, L=L):
                        act.wait_ge(L.var_r, step_no(turn, q) + 1)
                        v = moments[D:P, q % RING, :]
                        act.activation(v, v, ACT.Sqrt, bias=eps_sb[D:P, 0:1]).then_inc(L.std_r, 1)

                    pipeline(act, GTURNS, [(1, deviations), (0, extremes_in), (0, double), (0, square_means)])

                    for c in range(SLOTS):
                        part = slice(c * PART, (c + 1) * PART)
                        act.wait_ge(L.bn_cent, c + 1)
                        act.activation(n2[:, part, :], n1[:, part, :], ACT.Square).then_inc(L.bn_sq, 1)
                    act.wait_ge(L.bn_var, 1)
                    act.activation(bn_scale[:, :], bn_scale[:, :], ACT.Sqrt, bias=eps_sb[0:EP, 0:1]).then_inc(L.bn_std, 1)
                    for c in range(SLOTS + 1):
                        if c < SLOTS:
                            part = slice(c * PART, (c + 1) * PART)
                            act.wait_ge(centered, GROUPS + (c + 1) * GTURNS)
                            act.activation(n2[:, part, :], n1[:, part, :], ACT.Square).then_inc(squared, GTURNS)
                        if c > 0:
                            v = ln_var[:, (c - 1) * PART:c * PART]
                            act.wait_ge(var, GROUPS + c * GTURNS)
                            act.activation(v, v, ACT.Sqrt, bias=eps_sb[0:EP, 0:1], scale=1.0 / D).then_inc(std, GTURNS)

        @block.tensor
        def _(pe):
            pe.wait_ge(consts, 6)
            for n, field in enumerate((ends, dst_first, rel)):
                pe.wait_ge(fields_ready, n + 1)
                for gd in range(EB // SUB):
                    turned_no = n * SUB + gd
                    if turned_no >= 3:
                        pe.wait_ge(fields_placed, turned_no - 2)
                    ps = (ps_a, ps_b, ps_o)[turned_no % 3]
                    for k in range(SUB):
                        g = gd * SUB + k
                        ins = pe.transpose(ps[:, k * P:k * P + EP], field[:, g * P:(g + 1) * P], ident[0:EP, 0:EP])
                    ins.then_inc(fields_turned, 1)
            pe.wait_ge(cum_ready, 1)
            pe.matmul(ps_c[0:EP, 0:1], before[0:EP, 0:EP], blk_cum[:, EB - 1:EB], start=True, stop=True) \
                .then_inc(base_ready, 1)

            for L in layers:
                if L.n == 1:
                    pe.wait_ge(maps_ready, 2)
                    pe.transpose(ps_c[0:RT, 0:P], inv_deg[:, :], ident[:, :]).then_inc(L.inv_turned, 1)
                    pe.wait_ge(L.inv_copied, 1)
                pe.sem_inc(L.summed, CREDIT)
                if L.n == 1:
                    pe.sem_inc(L.tb, SLOTS)

                def sum_block(turn, q, k, L=L):
                    if k == 0:
                        pe.wait_ge(gathered[q], loaded(L, turn, SUB))
                        pe.wait_ge(L.onehot, step_no(turn, q) + 1)
                        if L.n == 0:
                            pe.wait_ge(aux_loaded[q], aux_there(L, turn))
                            pe.wait_ge(L.prep, 1 + step_no(turn, q) + 1)
                        if L.n == 1:
                            pe.wait_ge(L.ts, 1 + step_no(turn, q) + 1)
                    behind = {0: 1, SUB - 1: O_BANKS}.get(k, SUB)
                    pe.wait_ge(L.added, CREDIT + block_no(turn, q, k) + 1 - behind)
                    s = onehot[:, q, k, :]
                    if L.n == 0:
                        pe.matmul(sums[k][0:L0_ROWS, 0, :], xs[:, q, k, 0:L0_ROWS], s, start=True, stop=True)
                        ins = pe.matmul(sums[k][0:L0_ROWS, 1, :], xs[:, q, k, L0_ROWS:2 * L0_ROWS], s, start=True, stop=True)
                    elif L.n == 1:
                        pe.matmul(sums[k][:, 0, :], xs[:, q, k, D:3 * D], s, start=True, stop=True)
                        ins = pe.matmul(sums[k][:, 1, :], turned[:, q, k, :], s, start=True, stop=True)
                    else:
                        ins = pe.matmul(sums[k][0:D, 0, :], xs[:, q, k, 0:D], s, start=True, stop=True)
                    ins.then_inc(L.summed, 1)

                if L.n == 2:
                    pe.sem_inc(L.htp, 1)
                    pe.sem_inc(L.dense, 1)
                    pe.wait_ge(maps_ready, 2)

                    def own_features(g, q, k, L=L):
                        if (q, k) == (1, 0):
                            pe.wait_ge(L.hs, g + 1)
                            pe.wait_ge(L.hts, g + 1)
                            pe.sem_inc(pe_past, 1)
                            for t in range(GRP):
                                ins = pe.transpose(ps_turn[0:D, t * EP:(t + 1) * EP], L.h_in[:, t, :], ident[0:EP, 0:EP])
                            ins.then_inc(L.htp, 1)
                        if (q, k) == (3, 0):
                            pe.wait_ge(L.hts, 1 + g + 1)
                            pe.wait_ge(L.dense_out, g + 1)
                            for t in range(GRP):
                                ins = pe.matmul(ps_dense[0:EP, t * D:(t + 1) * D], L.ht[:, t * EP:(t + 1) * EP], wr_sb[:, :],
                                                start=True, stop=True)
                            ins.then_inc(L.dense, 1)

                    pipeline(pe, GROUPS, [(0, sum_block), (0, own_features)], parts=SUB)
                    pipeline(pe, TURNS, [(0, sum_block)], parts=SUB, start=GROUPS)
                elif L.n != 1:
                    pipeline(pe, TURNS, [(0, sum_block)], parts=SUB)
                else:
                    def turn_rows(turn, q, k, L=L):
                        if k == 0:
                            pe.wait_ge(L.prep, step_no(turn, q) + 1)
                            pe.wait_ge(L.scan, step_no(turn, q) + 1)
                        ins = pe.transpose(ps_a[:, k * P:(k + 1) * P], xs[:, q, k, 0:P], ident[:, :])
                        if k == SUB - 1:
                            ins.then_inc(L.tx, 1)

                    def turn_back(turn, q, k, L=L):
                        if k == 0:
                            pe.wait_ge(L.scan, 1 + step_no(turn, q) + 1)
                            pe.wait_ge(L.ts, step_no(turn, q) + 1)
                        ins = pe.transpose(ps_b[:, k * P:(k + 1) * P], scanned[:, q, k * P:(k + 1) * P], ident[:, :])
                        if k == SUB - 1:
                            ins.then_inc(L.tb, 1)

                    pipeline(pe, TURNS, [(2, sum_block), (1, turn_back), (0, turn_rows)], parts=SUB)

                pe.sem_inc(L.rows_mm, SLOTS)
                def rank_rows(turn, q, _, L=L):
                    step = step_no(turn, q)
                    if L.n == 0 and first(turn) and q == 0:
                        pe.wait_ge(ld_const, 18 * 16)
                    pe.wait_ge(L.staged, step + 1)
                    pe.wait_ge(L.rows_out, step + 1)
                    for t in range(GRP):
                        c = slice(t * P, (t + 1) * P)
                        if L.n == 0:
                            pe.matmul(ps_rank[:, t * P:t * P + L0_ROWS], L.rstage[0:L0_ROWS, q, 0, c], map_x[:, :],
                                      start=True, stop=False)
                            ins = pe.matmul(ps_rank[:, t * P:t * P + L0_ROWS], L.rstage[0:L0_ROWS, q, 1, c], map_ea[:, :],
                                            start=False, stop=True)
                        else:
                            ins = pe.matmul(ps_rank[:, t * P:t * P + D], L.rstage[0:D, q, 0, c],
                                            wl_sb[:, :] if L.n == 2 else ident[0:D, 0:D], start=True, stop=True)
                    ins.then_inc(L.rows_mm, 1)

                def turn_nodes(turn, q, _, L=L):
                    step = step_no(turn, q)
                    pe.wait_ge(L.hs, step + 1)
                    pe.wait_ge(L.hts, step + 1)
                    pe.sem_inc(pe_past, 1)
                    for t in range(GRP):
                        ins = pe.transpose(ps_turn[0:D, t * EP:(t + 1) * EP], L.h_in[:, q, t, :], ident[0:EP, 0:EP])
                    ins.then_inc(L.htp, 1)

                def up(turn, q, _, L=L):
                    step = step_no(turn, q)
                    pe.wait_ge(L.hts, 1 + step + 1)
                    pe.wait_ge(L.relu, step + 1)
                    pe.matmul(ps_mid[:, 0:GRP * EP], w1_sb[:, :], L.ht[:, q, :], start=True, stop=True).then_inc(L.u, 1)

                def down(turn, q, _, L=L):
                    step = step_no(turn, q)
                    pe.wait_ge(L.relu, 1 + step + 1)
                    pe.wait_ge(L.dense_out, step + 1)
                    for t in range(GRP):
                        ins = pe.matmul(ps_dense[0:EP, t * D:(t + 1) * D], L.h1[:, q, t * EP:(t + 1) * EP], w2_sb[:, :],
                                        start=True, stop=True)
                    ins.then_inc(L.dense, 1)

                def turn_x(turn, q, _, L=L):
                    step = step_no(turn, q)
                    pe.wait_ge(x_ready, ln_no(L, turn, q))
                    pe.wait_ge(L.xw_hts, step + 1)
                    pe.sem_inc(pe_past, 1)
                    for t in range(GRP):
                        ins = pe.transpose(ps_mid[0:D, t * EP:(t + 1) * EP], L.x_out[:, q, t, :], ident[0:EP, 0:EP])
                    ins.then_inc(L.xw_htp, 1)

                def xw_mm(turn, q, _, L=L):
                    step = step_no(turn, q)
                    pe.wait_ge(L.xw_hts, 1 + step + 1)
                    for t in range(GRP):
                        pe.wait_ge(L.xw_act if t < 2 else L.xw_dve, 2 * step + (t % 2 + 1))
                        pe.matmul(ps_o[0:EP, t * BANK:(t + 1) * BANK], L.xt[:, q, t * EP:(t + 1) * EP], w3_sb[:, :, :],
                                  start=True, stop=True).then_inc(L.xw_mm, 1)

                if L.n == 0:
                    pe.sem_inc(L.htp, SLOTS)
                    pe.sem_inc(L.dense, SLOTS)
                    pe.sem_inc(L.u, SLOTS)
                    pipeline(pe, GTURNS, [(5, down), (4, up), (0, rank_rows), (3, turn_nodes)])
                elif L.n == 2:
                    pe.sem_inc(L.xw_htp, SLOTS)
                    pe.sem_inc(L.xw_mm, XW_CREDIT)
                    pipeline(pe, GTURNS, [(0, rank_rows), (5, xw_mm), (4, turn_x)])
                elif L.n == 3:
                    pipeline(pe, GTURNS, [(0, rank_rows)])
                else:
                    def rank_rows1(turn, q, _, L=L):
                        step = step_no(turn, q)
                        pe.wait_ge(L.std_r, step + 1)
                        pe.wait_ge(L.staged, step + 1)
                        pe.wait_ge(L.rows_out, step + 1)
                        for t in range(GRP):
                            c = slice(t * P, (t + 1) * P)
                            z = z_banks[q % RING][:, t * 256:t * 256 + 3 * D]
                            pe.matmul(z, moments[:, q % RING, c], w_moments[:, :, :], start=True, stop=False)
                            ins = pe.matmul(z, extremes[:, q % RING, c], w_extremes[:, :, :], start=False, stop=True)
                        ins.then_inc(L.rows_mm, 1)

                    def node_sums(turn, q, _, L=L):
                        step = step_no(turn, q)
                        pe.wait_ge(L.bn_in, step + 1)
                        ins = pe.matmul(ps_c[0:EP, 0:GRP * D], ones[0:EP, 0:EP], group_of(n1_groups, turn, q),
                                        start=first(turn) and q == 0, stop=is_last(turn, q))
                        if is_last(turn, q):
                            ins.then_inc(L.bn_sum, 1)

                    pipeline(pe, GTURNS, [(1, rank_rows1), (4, node_sums)])

                    cells = flat(n2)
                    cols = PART * D // 4
                    for c in range(4 * SLOTS):
                        if c % 4 == 0:
                            pe.wait_ge(L.bn_sq, c // 4 + 1)
                        ins = pe.matmul(ps_c[0:EP, 0:cols], ones[0:EP, 0:EP], cells[:, c * cols:(c + 1) * cols],
                                        start=c == 0, stop=c == 4 * SLOTS - 1)
                    ins.then_inc(L.bn_sum, 1)

        @block.vector
        def _(dve):
            steps = [0]

            def link(ins):
                steps[0] += 1
                ins.then_inc(dve_step, 1)
                dve.wait_ge(dve_step, steps[0])

            dve.memset(dst_left[:, :], -1)
            dve.memset(dst_right[:, :], -1).then_inc(edge_init, 1)
            dve.memset(eps_sb[:, :], EPS).then_inc(maps_ready, 1)
            dve.wait_ge(consts, 5)
            link(dve.tensor_copy(iota[:, :], iota_i[:, :]))
            dve.memset(map_ea[:, :], 0.0)
            dve.tensor_copy(map_x[:, :], ident[0:L0_ROWS, 0:L0_ROWS]).then_inc(maps_init, 1)
            link(dve.memset(inside, 1.0))
            dve.memset(inside.rearrange("p (b e) -> p b e", e=P)[:, :, 0:1], 0.0)
            starts_b = starts.rearrange("p (b e) -> p b e", e=P)
            rel_b = rel.rearrange("p (b e) -> p b e", e=P)
            dve.wait_ge(ld_dst, 48)
            dve.tensor_tensor(starts[:, 1:EW], dst_i[:, 1:EW], dst_i[:, 0:EW - 1], ALU.not_equal)
            dve.tensor_tensor(starts[:, 0:1], dst_i[:, 0:1], dst_left[:, :], ALU.not_equal)
            link(dve.tensor_tensor(ends[:, EW - 1:EW], dst_i[:, EW - 1:EW], dst_right[:, :], ALU.not_equal))
            dve.tensor_copy(ends[:, 0:EW - 1], starts[:, 1:EW]).then_inc(fields_ready, 1)
            dve.tensor_tensor(dst_first, dst_i, starts, ALU.mult).then_inc(fields_ready, 1)
            dve.tensor_copy(blk_first[:, :], starts_b[:, :, 0])
            link(dve.tensor_tensor_scan(rel, inside, starts, 0.0, ALU.mult, ALU.add))
            link(dve.tensor_copy(blk_total[:, :], rel_b[:, :, P - 1]))
            link(dve.tensor_tensor(rel_b, rel_b, wide(blk_first[:, :], P), ALU.subtract))
            dve.sem_inc(fields_ready, 1)
            dve.tensor_scalar(restart_row, starts, RESTART, None, ALU.mult).then_inc(restart_ready, 1)
            dve.tensor_tensor_scan(blk_cum[:, :], ones[0:EP, 0:EB], blk_total[:, :], 0.0, ALU.mult, ALU.add) \
                .then_inc(cum_ready, 1)
            dve.wait_ge(cum_ready, 1)
            link(dve.tensor_tensor(blk_total[:, :], blk_cum[:, :], blk_total[:, :], ALU.subtract))
            link(dve.tensor_tensor(blk_total[:, :], blk_total[:, :], blk_first[:, :], ALU.add))
            dve.wait_ge(base_ready, 1)
            dve.tensor_scalar(blk_window[:, :], blk_total[:, :], ps_c[0:EP, 0:1], -1.0, ALU.add, ALU.add) \
                .then_inc(window_ready, 1)
            dve.wait_ge(ld_edges, 32)
            dve.scalar_tensor_tensor(out=src_all, in0=src_all, scalar=float(RELS), in1=etype_all, op0=ALU.mult, op1=ALU.add) \
                .then_inc(xw_numbered, 1)
            dve.wait_ge(ld_const, 18 * 16)
            dve.tensor_scalar(eps1[:, :], eps1[:, :], 1.0, None, ALU.add)
            dve.tensor_tensor(wr_sb[:, :], wr_sb[:, :], ident[0:D, 0:D], ALU.add)
            link(dve.tensor_scalar(w_extremes[0:D], w_extremes[0:D], -1.0, None, ALU.mult))

            for L in layers:
                dve.sem_inc(L.added, CREDIT)
                if L.n == 0:
                    dve.wait_ge(fields_turned, 3 * SUB)
                    dve.wait_ge(restart_stored, 16)
                    link(dve.memset(xs[:, :, :, L0_ROWS + D:2 * L0_ROWS], 0.0))
                    dve.memset(xs[:, :, :, DEG:DEG + 1], 1.0).then_inc(L.prep, 1)
                    for c in range(SLOTS):
                        dve.wait_ge(meta_stored[c], 16)
                        dve.memset(acc[:, 0, c * META_CHUNK:(c + 1) * META_CHUNK], 0.0)
                    dve.wait_ge(xw_rows_stored, 16)
                    dve.memset(acc[:, 1, 0:2 * BLOCKS], 0.0).then_inc(acc_zero, 1)
                if L.n == 1:
                    link(dve.memset(scanned[:, SLOTS - 1, SUB * P - 1:SUB * P], 0.0))
                    dve.sem_inc(L.scan, 1)
                    dve.wait_ge(L.logs, 1)
                    link(dve.tensor_scalar(att[:, :], amp[:, :], 1e-12, None, ALU.max))
                    link(dve.reciprocal(att[:, :], att[:, :]))
                    link(dve.tensor_scalar(att[:, :], att[:, :], AVG_D_LOG, None, ALU.mult))
                    dve.tensor_scalar(amp[:, :], amp[:, :], 1.0 / AVG_D_LOG, None, ALU.mult).then_inc(L.scalers, 1)
                dve.wait_ge(acc_zero, L.n + 2)
                n_rows = (L0_ROWS, P, D, D)[L.n]
                halves = 2 if L.n < 2 else 1
                first_rank = {}

                def hot(turn, q, k, L=L):
                    if k == 0:
                        dve.wait_ge(meta_loaded[q], meta_there(L, turn))
                        dve.wait_ge(L.summed, block_no(turn, q, SUB))
                    rel_k = meta[:, q, F_REL + k:F_REL + k + 1]
                    if L.n == 3:
                        if k == 0:
                            dve.wait_ge(aux_loaded[q], aux_there(L, turn))
                        ins = dve.tensor_scalar(onehot[:, q, k, :], iota[:, :], rel_k,
                                                weight[:, q, k:k + 1],
                                                ALU.is_equal, ALU.mult)
                    else:
                        ins = dve.tensor_scalar(onehot[:, q, k, :], iota[:, :], rel_k, None, ALU.is_equal)
                    if k == SUB - 1:
                        ins.then_inc(L.onehot, 1)

                def scan(turn, q, k, L=L):
                    if k == SUB - 1:
                        dve.wait_ge(L.tx, step_no(turn, q) + 1)
                        dve.wait_ge(aux_loaded[q], aux_there(L, turn))
                        dve.wait_ge(L.tb, step_no(turn, q) + 1)
                        dve.wait_ge(L.scan, 1 + step_no(turn, q))
                        before_q = (q - 1) % SLOTS
                        dve.tensor_tensor_scan(scanned[:, q, :], restart[:, q, :], ps_a[:, 0:SUB * P],
                                               scanned[:, before_q, SUB * P - 1:SUB * P], ALU.add, ALU.max) \
                            .then_inc(L.scan, 1)

                def add(turn, q, k, L=L, n_rows=n_rows, halves=halves, first_rank=first_rank):
                    if k == 0:
                        _, first_rank["of"] = nc.values_load_multi_w_load_instructions(
                            window[0:1, q, :], engines=[mybir.EngineType.DVE], min_val=0, max_val=N - 1,
                            skip_runtime_bounds_check_because="a rank is less than the number of nodes")
                    n = block_no(turn, q, k)
                    dve.wait_ge(L.summed, CREDIT + n + 1)
                    dve.wait_ge(L.added, CREDIT + n)
                    a = acc[0:n_rows, 0:halves, bass.ds(first_rank["of"][k], P)]
                    dve.tensor_tensor(a, a, sums[k][0:n_rows, 0:halves, :], ALU.add).then_inc(L.added, 1)

                if L.n == 1:
                    pipeline(dve, TURNS, [(2, add), (0, hot), (0, scan)], parts=SUB)
                elif L.n == 2:
                    dve.sem_inc(L.dense_out, 1)
                    dve.wait_ge(table_ready, 16 * (GROUPS + SLOTS))

                    def own_features(g, q, k, L=L):
                        if (q, k) == (SLOTS - 1, SUB - 1):
                            dve.wait_ge(L.dense, 1 + g + 1)
                            dve.tensor_tensor(xres[:, bass.ds(g * GRP, GRP), :],
                                              ps_dense[0:EP, 0:GRP * D].rearrange("p (t f) -> p t f", t=GRP),
                                              along(bias["l2_b"][:, :], GRP), ALU.add).then_inc(L.dense_out, 1)

                    pipeline(dve, GROUPS, [(1, add), (0, hot), (0, own_features)], parts=SUB)
                    pipeline(dve, TURNS, [(1, add), (0, hot)], parts=SUB, start=GROUPS)
                else:
                    pipeline(dve, TURNS, [(1, add), (0, hot)], parts=SUB)

                dve.wait_ge(L.added, CREDIT + BLOCKS)

                def node_numbers(turn, q, L=L):
                    if not first(turn):
                        dve.wait_ge(scattered[q], rows_landed(L, turn))
                    dve.tensor_copy(node_of[:, q, :], ranks_of(node_all, turn, q))

                def rows_out(turn, q, _, L=L, node_numbers=node_numbers):
                    step = step_no(turn, q)
                    dve.wait_ge(L.rows_mm, SLOTS + step + 1)
                    node_numbers(turn, q)
                    ps = ps_rank.rearrange("p (t c) -> p t c", t=GRP)[:, :, 0:D]
                    if L.n == 2:
                        ins = dve.tensor_tensor(L.rows[:, q], ps, wide(ranks_of(inv_deg, turn, q), D), ALU.mult)
                    else:
                        ins = dve.tensor_copy(L.rows[:, q], ps)
                    ins.then_inc(L.rows_out, 1)

                def nodes_in(turn, q, _, L=L):
                    step = step_no(turn, q)
                    dve.wait_ge(agg_loaded[q], agg_there(L, turn + 1))
                    dve.wait_ge(L.htp, step + 1)
                    dve.scalar_tensor_tensor(out=L.h_in[:, q], in0=tiles_of(xres, turn, q), scalar=eps1[:, 0:1],
                                             in1=L.nodes[:, q], op0=ALU.mult, op1=ALU.add).then_inc(L.hs, 1)

                def center(turn, q, _, L=L):
                    step = step_no(turn, q)
                    v, mean = L.nodes[:, q], ln_mean[:, q * GRP:(q + 1) * GRP]
                    if L.n == 0:
                        dve.wait_ge(L.dense, SLOTS + step + 1)
                        dve.tensor_tensor(v, tiles_of(xres, turn, q),
                                          ps_dense[0:EP, 0:GRP * D].rearrange("p (t f) -> p t f", t=GRP), ALU.add) \
                            .then_inc(L.dense_out, 1)
                        dve.wait_ge(L.dense_out, 1 + step + 1)
                        dve.tensor_tensor(v, v, along(bias["b2"][:, :], GRP), ALU.add).then_inc(L.ln_in, 1)
                    else:
                        dve.wait_ge(agg_loaded[q], agg_there(L, turn + 1))
                        dve.tensor_tensor(v, tiles_of(xres, turn, q), v, ALU.add).then_inc(L.ln_in, 1)
                    dve.wait_ge(L.ln_in, 2 * step + 1)
                    dve.tensor_reduce(mean, v, AX.X, ALU.add).then_inc(L.ln_in, 1)
                    dve.wait_ge(L.ln_in, 2 * step + 2)
                    dve.scalar_tensor_tensor(out=v, in0=wide(mean, D), scalar=-1.0 / D, in1=v, op0=ALU.mult, op1=ALU.add) \
                        .then_inc(centered, 1)

                def variance(turn, q, _, L=L):
                    dve.wait_ge(squared, ln_no(L, turn, q))
                    dve.tensor_reduce(ln_var[:, q * GRP:(q + 1) * GRP], L.square[:, q], AX.X, ALU.add).then_inc(var, 1)

                def scale(turn, q, _, L=L):
                    step = step_no(turn, q)
                    v = ln_var[:, q * GRP:(q + 1) * GRP]
                    dve.wait_ge(std, ln_no(L, turn, q))
                    dve.reciprocal(v, v).then_inc(L.ln_scale, 1)
                    if L.n == 2:
                        dve.wait_ge(L.xw_htp, step + 1)
                    dve.wait_ge(L.ln_scale, step + 1)
                    dve.tensor_tensor(L.x_out[:, q] if L.n == 2 else tiles_of(xres, turn, q), L.nodes[:, q], wide(v, D),
                                      ALU.mult).then_inc(x_ready, 1)

                def xw_out(turn, q, _, L=L):
                    step = step_no(turn, q)
                    if not first(turn):
                        dve.wait_ge(xw_stored[q], turn * 16)
                    for t in (2, 3):
                        dve.wait_ge(L.xw_mm, XW_CREDIT + GRP * step + (t + 1))
                        dve.tensor_copy(L.xw[:, q, t, :], ps_o[0:EP, t * BANK:(t + 1) * BANK]).then_inc(L.xw_dve, 1)

                def number(turn, q, _, L=L):
                    step = step_no(turn, q)
                    dve.wait_ge(L.rows_out, 1 + step + 1)
                    if not first(turn):
                        dve.wait_ge(scattered[q], rows_landed(L, turn))
                    dve.tensor_copy(ranks_of(deg, turn, q), L.rows[:, q, :, DEG])
                    dve.tensor_scalar(no_rank[:, :], L.rows[:, q, :, DEG], 0.5, float(2 * N), ALU.is_lt, ALU.mult) \
                        .then_inc(L.number, 1)
                    dve.wait_ge(L.number, 2 * step + 1)
                    dve.tensor_tensor(node_of[:, q, :], L.rows[:, q, :, DST], no_rank[:, :], ALU.add).then_inc(L.number, 1)
                    dve.wait_ge(L.number, 2 * step + 2)
                    dve.tensor_copy(ranks_of(node_all, turn, q), node_of[:, q, :]).then_inc(L.rows_set, 1)

                if L.n == 0:
                    dve.wait_ge(x_loaded, 16 * GROUPS)
                    dve.sem_inc(L.dense_out, 1)
                    pipeline(dve, GTURNS, [(3, nodes_in), (5, center), (5, variance), (5, scale), (0, number)])
                    dve.wait_ge(L.rows_set, GROUPS)
                    link(dve.tensor_scalar(inv_deg[:, :], deg[:, :], 1.0, None, ALU.max))
                    link(dve.reciprocal(inv_deg[:, :], inv_deg[:, :]))
                    dve.sem_inc(maps_ready, 1)
                elif L.n == 1:
                    dve.wait_ge(L.scalers, 1)
                    dve.sem_inc(L.means, SLOTS)
                    dve.sem_inc(L.rows_out, 2)

                    def means(turn, q, _, L=L):
                        step = step_no(turn, q)
                        dve.wait_ge(aux_loaded[q], inv_there(turn))
                        dve.wait_ge(L.rows_mm, step + SLOTS - 1)
                        dve.tensor_tensor(moments[:, q % RING, :], acc[:, 0, bass.ds(step * (GRP * P), GRP * P)],
                                          inv_wide[:, q, :], ALU.mult).then_inc(L.means, 1)

                    def variances(turn, q, _, L=L):
                        step = step_no(turn, q)
                        v = moments[D:P, q % RING, :]
                        dve.wait_ge(L.sq, step + 1)
                        dve.tensor_tensor(v, v, meansq[D:P, q % RING, :], ALU.subtract).then_inc(L.var_step, 1)
                        dve.wait_ge(L.var_step, step + 1)
                        dve.tensor_scalar(v, v, 0.0, None, ALU.max).then_inc(L.var_r, 1)

                    def rows_out1(turn, q, _, L=L, node_numbers=node_numbers):
                        step = step_no(turn, q)
                        dve.wait_ge(L.rows_mm, SLOTS + step + 1)
                        node_numbers(turn, q)
                        z = z_banks[q % RING].rearrange("p (t n f) -> p t n f", t=GRP, f=D)
                        rows = L.rows[:, q]
                        dve.wait_ge(L.rows_out, 2 + step)
                        dve.tensor_tensor(z_part, z[:, :, 1, :], wide(ranks_of(amp, turn, q), D), ALU.mult).then_inc(L.z_part, 1)
                        dve.tensor_tensor(rows, z[:, :, 2, :], wide(ranks_of(att, turn, q), D), ALU.mult).then_inc(L.z_part, 1)
                        dve.wait_ge(L.z_part, 3 * step + 1)
                        dve.tensor_tensor(z_part, z_part, z[:, :, 0, :], ALU.add).then_inc(L.z_part, 1)
                        dve.wait_ge(L.z_part, 3 * step + 3)
                        dve.tensor_tensor(rows, rows, z_part, ALU.add).then_inc(L.rows_out, 1)

                    def add_bias(turn, q, _, L=L):
                        dve.wait_ge(agg_loaded[q], agg_there(L, turn + 1))
                        v = tiles_of(n1, turn, q)
                        dve.tensor_tensor(v, v, along(bias["l1_b"][:, :], GRP), ALU.add).then_inc(L.bn_in, 1)

                    pipeline(dve, GTURNS, [(1, variances), (0, means), (2, rows_out1), (4, add_bias)])
                elif L.n == 2:
                    dve.sem_inc(L.rows_out, 1)
                    dve.sem_inc(L.xw_dve, 2)
                    pipeline(dve, GTURNS, [(0, rows_out), (3, center), (4, scale), (3, variance), (5, xw_out)])
                else:
                    dve.sem_inc(L.rows_out, 1)
                    pipeline(dve, GTURNS, [(0, rows_out), (3, center), (4, scale), (3, variance)])

                if L.n == 1:
                    def part_of(array, c):
                        return array[:, c * PART:(c + 1) * PART]

                    dve.wait_ge(L.bn_sum, 1)
                    link(dve.tensor_reduce(bn_mean[:, :], ps_c[0:EP, 0:GRP * D].rearrange("p (t f) -> p f t", t=GRP),
                                           AX.X, ALU.add))
                    link(dve.tensor_scalar(bn_mean[:, :], bn_mean[:, :], 1.0 / N, None, ALU.mult))
                    for c in range(SLOTS):
                        v = part_of(n1, c)
                        dve.tensor_tensor(v, v, along(bn_mean[:, :], PART), ALU.subtract).then_inc(L.bn_cent, 1)
                    dve.wait_ge(L.bn_sum, 2)
                    link(dve.tensor_reduce(bn_scale[:, :], ps_c[0:EP, 0:SUB * D].rearrange("p (t f) -> p f t", t=SUB),
                                           AX.X, ALU.add))
                    dve.tensor_scalar(bn_scale[:, :], bn_scale[:, :], 1.0 / N, None, ALU.mult).then_inc(L.bn_var, 1)
                    dve.wait_ge(L.bn_std, 1)
                    link(dve.reciprocal(bn_scale[:, :], bn_scale[:, :]))
                    link(dve.tensor_tensor(bn_scale[:, :], bn_scale[:, :], bias["l1_gamma"][:, :], ALU.mult))
                    dve.wait_ge(L.bn_cent, SLOTS)
                    dve.wait_ge(table_ready, 16 * GROUPS)

                    for c in range(SLOTS + 3):
                        if c < SLOTS:
                            v = part_of(n1, c)
                            dve.tensor_tensor(v, v, along(bn_scale[:, :], PART), ALU.mult).then_inc(L.bn_scaled, 1)
                        if 0 <= c - 1 < SLOTS:
                            v, mean = part_of(n1, c - 1), part_of(ln_mean, c - 1)
                            dve.wait_ge(L.bn_affine, c)
                            link(dve.scalar_tensor_tensor(out=v, in0=v, scalar=0.0, in1=part_of(xres, c - 1), op0=ALU.max,
                                                          op1=ALU.add))
                            link(dve.tensor_reduce(mean, v, AX.X, ALU.add))
                            dve.scalar_tensor_tensor(out=v, in0=wide(mean, D), scalar=-1.0 / D, in1=v, op0=ALU.mult,
                                                     op1=ALU.add).then_inc(centered, GTURNS)
                        if 0 <= c - 3 < SLOTS:
                            v = part_of(ln_var, c - 3)
                            dve.wait_ge(std, GROUPS + (c - 2) * GTURNS)
                            link(dve.reciprocal(v, v))
                            dve.tensor_tensor(part_of(xres, c - 3), part_of(n1, c - 3), wide(v, D), ALU.mult) \
                                .then_inc(x_ready, GTURNS)
                        if 0 <= c - 2 < SLOTS:
                            dve.wait_ge(squared, GROUPS + (c - 1) * GTURNS)
                            dve.tensor_reduce(part_of(ln_var, c - 2), part_of(n2, c - 2), AX.X, ALU.add).then_inc(var, GTURNS)


def kernel(**inputs):
    import numpy as np
    import concourse.bacc as bacc
    from concourse.bass_utils import run_bass_kernel_spmd

    def turned(a):
        a = np.asarray(a)
        a = a.reshape(BLOCKS, P, -1).transpose(1, 0, 2)
        return np.ascontiguousarray(a).reshape(P, -1)

    def arr(name, *shape):
        a = np.asarray(inputs[name])
        return np.ascontiguousarray(a.reshape(shape) if shape else a)

    arrays = {
        "x_in": arr("x"),
        "src_e": turned(inputs["src"]),
        "etype_e": turned(inputs["edge_type_8"]),
        "weight_e": turned(inputs["edge_weight"]),
        "dst_n": arr("dst", EP, EW),
        "edge_attr": turned(inputs["edge_attr_64"]),
        "eps_in": arr("L0_gnn_eps", 1, 1),
        "we": arr("L0_gnn_We_w"),
        "we_b": arr("L0_gnn_We_b", 1, D),
        "w1": arr("L0_gnn_W1"),
        "b1": arr("L0_gnn_b1", H, 1),
        "w2": arr("L0_gnn_W2"),
        "b2": arr("L0_gnn_b2", 1, D),
        "l1_w": arr("L1_gnn_W"),
        "l1_b": arr("L1_gnn_b", 1, D),
        "l1_gamma": arr("L1_gnn_gamma", 1, D),
        "l1_beta": arr("L1_gnn_beta", 1, D),
        "wl_t": np.ascontiguousarray(np.asarray(inputs["L2_gnn_w_l"]).T),
        "wr_t": np.ascontiguousarray(np.asarray(inputs["L2_gnn_w_r"]).T),
        "l2_b": arr("L2_gnn_b", 1, D),
        "l3_w": arr("L3_gnn_W"),
    }
    nc = bacc.Bacc("TRN2", target_bir_lowering=False, num_devices=1)
    args = [nc.dram_tensor(n, a.shape, mybir.dt.from_np(a.dtype), kind="ExternalInput").ap() for n, a in arrays.items()]
    out = nc.dram_tensor("out", (N, D), F32, kind="ExternalOutput").ap()
    gnn_kernel(nc, *args, out)
    return run_bass_kernel_spmd(nc, [arrays], core_ids=[0]).results[0]["out"]
```
